# Optimizing a Trainium2 kernel written in Bass

```python
import numpy as np
import jax
import jax.numpy as jnp

def _softmax(x, axis=-1):
    return jax.nn.softmax(x, axis=axis)

def _gelu(x):
    return jax.nn.gelu(x, approximate=True)

def _silu(x):
    return jax.nn.silu(x)

def _sigmoid(x):
    return jax.nn.sigmoid(x)

def _layernorm(x, axis=-1, eps=1e-05):
    m = jnp.mean(x, axis=axis, keepdims=True)
    v = jnp.var(x, axis=axis, keepdims=True)
    return (x - m) / jnp.sqrt(v + eps)

def _scatter_add(tgt, idx, src, axis=0):
    return tgt.at[idx].add(src)

def _segment_sum(src, seg, n):
    return jax.ops.segment_sum(src, seg, n)
kernel_name = 'mk_perceiver_d1_seqx_r2_476550'

def setup_inputs(seed: int=0):
    np.random.seed(seed)
    _w = jnp.asarray

    def _rec_inputs():
        import jax
        import jax.numpy as jnp
        _rk = jax.random.key(seed)
        x = -0.0002928 + 1 * jax.random.normal(jax.random.fold_in(_rk, 1), (1, 512, 512), jnp.float32)
        _lenS = 512 - jax.random.randint(jax.random.fold_in(_rk, 7), (1,), 0, max(1, 512 // 4) + 1, jnp.int32)
        _lenS2 = 8192 - jax.random.randint(jax.random.fold_in(_rk, 8), (1,), 0, max(1, 8192 // 4) + 1, jnp.int32)
        _ctx_1024P = jax.random.normal(jax.random.fold_in(_rk, 11), (1, 16, 512), jnp.float32)
        _ctx_1024c = jax.random.dirichlet(jax.random.fold_in(_rk, 511), 0.3 * jnp.ones((16,), jnp.float32), (1, 8192))
        _ctx_1024t = jnp.einsum('bsk,bkd->bsd', _ctx_1024c, _ctx_1024P)
        _ctx_1024t = _ctx_1024t * jax.lax.rsqrt(jnp.mean(jnp.square(_ctx_1024t)) + 1e-12) * 0.953939
        ctx_1024 = -1.39393e-06 + 0.999914 * (_ctx_1024t + 0.3 * jax.random.normal(jax.random.fold_in(_rk, 611), (1, 8192, 512), jnp.float32))
        return (x, ctx_1024)
    x, ctx_1024 = _rec_inputs()

    def _L0_xattn_setup():
        import jax, jax.numpy as jnp
        import numpy as np
        EMBED_DIM = 512
        NUM_HEADS = 16
        HEAD_DIM = EMBED_DIM // NUM_HEADS
        key = jax.random.key(seed)
        ks = jax.random.split(key, 9)
        B, LQ, LKV_NEW, LC, E = (2, 1024, 1024, 1024, EMBED_DIM)
        s = 0.02
        return {'query': jax.random.normal(ks[0], (B, LQ, E), jnp.float32), 'key': jax.random.normal(ks[1], (B, LKV_NEW, E), jnp.float32), 'value': jax.random.normal(ks[2], (B, LKV_NEW, E), jnp.float32), 'cached_key': jax.random.normal(ks[3], (B, LC, E), jnp.float32), 'cached_value': jax.random.normal(ks[4], (B, LC, E), jnp.float32), 'in_proj_weight': jax.random.normal(ks[5], (3 * E, E), jnp.float32) * s, 'in_proj_bias': jax.random.normal(ks[6], (3 * E,), jnp.float32) * s, 'out_proj_weight': jax.random.normal(ks[7], (E, E), jnp.float32) * s, 'out_proj_bias': jax.random.normal(ks[8], (E,), jnp.float32) * s}
    _L0_xattn_all = _L0_xattn_setup()
    _L0_xattn_in = {k: v for k, v in _L0_xattn_all.items() if k in ('in_proj_weight', 'in_proj_bias', 'out_proj_weight', 'out_proj_bias')}
    del _L0_xattn_all

    def _L0_attn_setup():
        import jax, jax.numpy as jnp
        import numpy as np
        NUM_HEADS = 16
        key = jax.random.key(seed)
        k1, k2, k3 = jax.random.split(key, 3)
        S, B, E = (1024, 4, 512)
        std = float(np.sqrt(2.0 / (E + E)))
        query = jax.random.normal(k1, (S, B, E), dtype=jnp.float32)
        in_proj_weight = jax.random.normal(k2, (3 * E, E), dtype=jnp.float32) * std
        in_proj_bias = jnp.zeros((3 * E,), dtype=jnp.float32)
        out_proj_weight = jax.random.normal(k3, (E, E), dtype=jnp.float32) * std
        out_proj_bias = jnp.zeros((E,), dtype=jnp.float32)
        return {'query': query, 'in_proj_weight': in_proj_weight, 'in_proj_bias': in_proj_bias, 'out_proj_weight': out_proj_weight, 'out_proj_bias': out_proj_bias}
    _L0_attn_all = _L0_attn_setup()
    _L0_attn_in = {k: v for k, v in _L0_attn_all.items() if k in ('in_proj_weight', 'in_proj_bias', 'out_proj_weight', 'out_proj_bias')}
    del _L0_attn_all

    def _L0_ffn_setup():
        import jax, jax.numpy as jnp
        import numpy as np
        B, P, D, D_MLP, E, K = (2, 1024, 512, 2048, 8, 2)
        key = jax.random.key(seed)
        k_x, k_g, k_in, k_out = jax.random.split(key, 4)
        s_in = 1.0 / np.sqrt(D).astype(np.float32)
        s_out = 1.0 / np.sqrt(D_MLP).astype(np.float32)
        return {'x': jax.random.normal(k_x, (B, P, D), dtype=jnp.float32), 'W_gate': jax.random.normal(k_g, (D, E), dtype=jnp.float32) * s_in, 'W_in': jax.random.normal(k_in, (E, D, D_MLP), dtype=jnp.float32) * s_in, 'b_in': jnp.zeros((E, D_MLP), dtype=jnp.float32), 'W_out': jax.random.normal(k_out, (E, D_MLP, D), dtype=jnp.float32) * s_out, 'b_out': jnp.zeros((E, D), dtype=jnp.float32)}
    _L0_ffn_all = _L0_ffn_setup()
    _L0_ffn_in = {k: v for k, v in _L0_ffn_all.items() if k in ('W_gate', 'W_in', 'b_in', 'W_out', 'b_out')}
    del _L0_ffn_all
    return {'x': x, 'ctx_1024': ctx_1024, 'L0_xattn_in_proj_weight': _L0_xattn_in['in_proj_weight'], 'L0_xattn_in_proj_bias': _L0_xattn_in['in_proj_bias'], 'L0_xattn_out_proj_weight': _L0_xattn_in['out_proj_weight'], 'L0_xattn_out_proj_bias': _L0_xattn_in['out_proj_bias'], 'L0_attn_in_proj_weight': _L0_attn_in['in_proj_weight'], 'L0_attn_in_proj_bias': _L0_attn_in['in_proj_bias'], 'L0_attn_out_proj_weight': _L0_attn_in['out_proj_weight'], 'L0_attn_out_proj_bias': _L0_attn_in['out_proj_bias'], 'L0_ffn_W_gate': _L0_ffn_in['W_gate'], 'L0_ffn_W_in': _L0_ffn_in['W_in'], 'L0_ffn_b_in': _L0_ffn_in['b_in'], 'L0_ffn_W_out': _L0_ffn_in['W_out'], 'L0_ffn_b_out': _L0_ffn_in['b_out']}

def reference(x, ctx_1024, L0_xattn_in_proj_weight, L0_xattn_in_proj_bias, L0_xattn_out_proj_weight, L0_xattn_out_proj_bias, L0_attn_in_proj_weight, L0_attn_in_proj_bias, L0_attn_out_proj_weight, L0_attn_out_proj_bias, L0_ffn_W_gate, L0_ffn_W_in, L0_ffn_b_in, L0_ffn_W_out, L0_ffn_b_out):
    import jax
    import jax.numpy as jnp

    def _L0_xattn_ref(query, key, value, cached_key, cached_value, in_proj_weight, in_proj_bias, out_proj_weight, out_proj_bias):
        import jax, jax.numpy as jnp
        import numpy as np
        EMBED_DIM = 512
        NUM_HEADS = 16
        HEAD_DIM = EMBED_DIM // NUM_HEADS
        E, H, D = (EMBED_DIM, NUM_HEADS, HEAD_DIM)
        k_full = jnp.concatenate([cached_key, key], axis=1)
        v_full = jnp.concatenate([cached_value, value], axis=1)
        wq, wk, wv = (in_proj_weight[:E], in_proj_weight[E:2 * E], in_proj_weight[2 * E:])
        bq, bk, bv = (in_proj_bias[:E], in_proj_bias[E:2 * E], in_proj_bias[2 * E:])
        B, Lq, _ = query.shape
        Lkv = k_full.shape[1]
        q = (jnp.einsum('bqe,fe->bqf', query, wq) + bq).reshape(B, Lq, H, D)
        k = (jnp.einsum('bke,fe->bkf', k_full, wk) + bk).reshape(B, Lkv, H, D)
        v = (jnp.einsum('bke,fe->bkf', v_full, wv) + bv).reshape(B, Lkv, H, D)
        scale = 1.0 / np.sqrt(D).astype(np.float32)
        scores = jnp.einsum('bqhd,bkhd->bhqk', q, k) * scale
        attn = jax.nn.softmax(scores, axis=-1)
        ctx = jnp.einsum('bhqk,bkhd->bqhd', attn, v).reshape(B, Lq, E)
        out = jnp.einsum('bqe,fe->bqf', ctx, out_proj_weight) + out_proj_bias
        return out

    def _L0_attn_ref(query, in_proj_weight, in_proj_bias, out_proj_weight, out_proj_bias):
        import jax, jax.numpy as jnp
        import numpy as np
        NUM_HEADS = 16
        S, B, E = query.shape
        H = NUM_HEADS
        hd = E // H
        scale = hd ** (-0.5)
        lin = jnp.einsum('sbe,fe->sbf', query, in_proj_weight) + in_proj_bias
        lin = lin.reshape(S, B * H, 3, hd)
        q = lin[:, :, 0, :]
        k = lin[:, :, 1, :]
        v = lin[:, :, 2, :]
        scores = jnp.einsum('sbd,tbd->bst', q, k) * scale
        attn = jax.nn.softmax(scores.astype(jnp.float32), axis=-1).astype(scores.dtype)
        ctx = jnp.einsum('bst,tbd->sbd', attn, v).reshape(S, B, E)
        out = jnp.einsum('sbe,fe->sbf', ctx, out_proj_weight) + out_proj_bias
        return out

    def _L0_ffn_ref(x, W_gate, W_in, b_in, W_out, b_out):
        import jax, jax.numpy as jnp
        import numpy as np
        B, P, D, D_MLP, E, K = (2, 1024, 512, 2048, 8, 2)
        gate_logits = jnp.einsum('bpd,de->bpe', x, W_gate)
        top_w, top_idx = jax.lax.top_k(gate_logits, K)
        top_w = jax.nn.softmax(top_w, axis=-1)
        combine = jnp.einsum('bpke,bpk->bpe', jax.nn.one_hot(top_idx, E, dtype=x.dtype), top_w)
        out = jnp.zeros_like(x)
        for e in range(E):
            h = jax.nn.gelu(jnp.einsum('bpd,dm->bpm', x, W_in[e]) + b_in[e], approximate=False)
            y = jnp.einsum('bpm,md->bpd', h, W_out[e]) + b_out[e]
            out = out + combine[..., e, None] * y
        return out
    x = x + _L0_xattn_ref(_layernorm(x, axis=-1), ctx_1024, ctx_1024, ctx_1024, ctx_1024, L0_xattn_in_proj_weight, L0_xattn_in_proj_bias, L0_xattn_out_proj_weight, L0_xattn_out_proj_bias)
    x = x + _L0_attn_ref(_layernorm(x, axis=-1), L0_attn_in_proj_weight, L0_attn_in_proj_bias, L0_attn_out_proj_weight, L0_attn_out_proj_bias)
    x = x + _L0_ffn_ref(_layernorm(x, axis=-1), L0_ffn_W_gate, L0_ffn_W_in, L0_ffn_b_in, L0_ffn_W_out, L0_ffn_b_out)
    return x

_drawn_inputs = setup_inputs


def setup_inputs(seed=0):
    import zlib

    import numpy as np

    out = dict(_drawn_inputs(seed))
    spreads = {'L0_attn_in_proj_bias': (0.0, 0.1),
     'L0_attn_out_proj_bias': (0.0, 0.1),
     'L0_ffn_b_in': (0.0, 0.1),
     'L0_ffn_b_out': (0.0, 0.1)}
    factors = {}
    for name, (base, spread) in spreads.items():
        noise = np.random.default_rng([zlib.crc32(name.encode()), seed]).standard_normal(out[name].shape)
        drawn = base * np.exp(spread * noise) if base else spread * noise
        out[name] = jnp.asarray(drawn.astype(out[name].dtype))
    for name, factor in factors.items():
        out[name] = (out[name] * factor).astype(out[name].dtype)
    return out
```

```python
from contextlib import ExitStack

import concourse.bass as bass
from concourse import mybir

F32 = mybir.dt.float32
F32R = mybir.dt.float32r
U32 = mybir.dt.uint32
I32 = mybir.dt.int32
ACT = mybir.ActivationFunctionType
ALU = mybir.AluOpType
X = mybir.AxisListType.X

P = 128
NQ = 512
E = 512
NK = 8192
H = 16
D = E // H
ET = E // P
QT = NQ // P
HG = P // D
NG = H // HG
SCALE = float(D) ** -0.5
SAFE = 40.0
EPS = 1e-5
CH = 512
NCH = NK // CH
KT = CH // P
QROWS = 3 * D + 1
NX = 8
M = 2048
MC = 512
MT = MC // P
NMC = M // MC


def rolled(eng, steps, body):
    body(0, False)
    with eng.Fori(1, steps - 1) as i:
        body(i, False)
    body(steps - 1, True)


def wait_reuse(eng, sem, count):
    if not isinstance(count, int) or count > 0:
        eng.wait_ge(sem, count)


def norm_scalar(nc, act, var, root, var_ready, root_ready):
    act.wait_ge(var_ready, 1)
    nc.scalar.activation(root[:, :], var[:, :], ACT.Sqrt).then_inc(root_ready, 1)


def norm_vector(nc, dve, x, xn, stats, mv, var, root, rstd, chain, var_ready, root_ready, ready):
    for t in range(QT):
        nc.vector.bn_stats(stats[:, t, :], x[:, t, :]).then_inc(chain, 1)
    dve.wait_ge(chain, QT)
    for t in range(QT):
        nc.vector.bn_aggr(mv[:, t, :], stats[:, t, :]).then_inc(chain, 1)
    dve.wait_ge(chain, 2 * QT)
    nc.vector.tensor_scalar(var[:, :], mv[:, :, 1], EPS, None, ALU.add).then_inc(var_ready, 1)
    dve.wait_ge(root_ready, 1)
    nc.vector.reciprocal(rstd[:, 0, :], root[:, :]).then_inc(chain, 1)
    dve.wait_ge(chain, 2 * QT + 1)
    nc.vector.tensor_tensor(rstd[:, 1, :], rstd[:, 0, :], rstd[:, 0, :], ALU.mult).then_inc(chain, 1)
    dve.wait_ge(chain, 2 * QT + 2)
    dve.wait_ge(var_ready, 1)
    nc.vector.tensor_tensor(rstd[:, 2, :], rstd[:, 1, :], var[:, :], ALU.mult).then_inc(chain, 1)
    dve.wait_ge(chain, 2 * QT + 3)
    nc.vector.tensor_scalar(rstd[:, 3, :], rstd[:, 2, :], -0.5, 1.5, ALU.mult, ALU.add).then_inc(chain, 1)
    dve.wait_ge(chain, 2 * QT + 4)
    nc.vector.tensor_tensor(rstd[:, 4, :], rstd[:, 3, :], rstd[:, 0, :], ALU.mult).then_inc(chain, 1)
    dve.wait_ge(chain, 2 * QT + 5)
    for t in range(QT):
        nc.vector.tensor_scalar(xn[:, t, :], x[:, t, :], mv[:, t, 0:1], rstd[:, 4, t:t + 1],
                                ALU.subtract, ALU.mult).then_inc(ready, 1)


def norm_transpose(nc, pe, xn, ident, banks, ready, turned):
    for t in range(QT):
        pe.wait_ge(ready, t + 1)
        for d in range(ET):
            last = nc.tensor.transpose(banks[d][:, t * P:(t + 1) * P], xn[:, t, d * P:(d + 1) * P],
                                       ident[:, :])
    last.then_inc(turned, 1)


def make_identity(nc, pool, ident, zeroed, made):
    nc.gpsimd.memset(ident[:, :], 0.0).then_inc(zeroed, 1)
    pool.wait_ge(zeroed, 1)
    nc.gpsimd.affine_select(out=ident[:, :], in_=ident[:, :], compare_op=ALU.not_equal, fill=1.0,
                            base=0, pattern=[[-1, P]], channel_multiplier=1).then_inc(made, 1)


def project_queries(nc, ctx, x_dram, w_in, b_cols, x_sb, ident, q_stack, q_scratch, q_top, head_rows):
    sb = lambda n, s, d=F32: ctx.enter_context(nc.sbuf_tensor(n, s, d))
    sem = lambda n: ctx.enter_context(nc.semaphore(n))
    wq = sb("pq_wq", [P, ET, E])
    bq = sb("pq_bq", [P, NG])
    xn = sb("pq_xn", [P, QT, E])
    xt = sb("pq_xt", [P, ET, NQ])
    q_hi = sb("pq_q_hi", [P, NG, NQ], F32R)
    q_lo = sb("pq_q_lo", [P, NG, NQ], F32R)
    stats = sb("pq_stats", [P, QT, 6])
    mv = sb("pq_mv", [P, QT, 2])
    var = sb("pq_var", [P, QT])
    root = sb("pq_root", [P, QT])
    rstd = sb("pq_rstd", [P, 5, QT])
    var_ready, root_ready = map(sem, ("pq_var_ready", "pq_root_ready"))
    turn = [ctx.enter_context(nc.psum_tensor(f"pq_turn{d}", [P, NQ], F32)) for d in range(ET)]
    proj = [ctx.enter_context(nc.psum_tensor(f"pq_proj{g}", [P, NQ], F32)) for g in range(NG)]
    x_in, w_loaded, chain, normed, turned, xt_ready = map(sem, (
        "pq_x_in", "pq_w_loaded", "pq_chain", "pq_normed", "pq_turned", "pq_xt_ready"))
    projected, hi_ready, lo_ready, stacked, zeroed, ident_made = map(sem, (
        "pq_projected", "pq_hi_ready", "pq_lo_ready", "pq_stacked", "pq_zeroed", "pq_ident_made"))

    with nc.Block() as block:
        @block.sync
        def _(sp):
            sp.dma_start(x_sb[:, :, :], x_dram.rearrange("a (t p) e -> p (a t) e", p=P)).then_inc(x_in, 16)
            sp.dma_start(wq[:, :, :], w_in[:, 0:E].rearrange("(t p) f -> p t f", p=P)).then_inc(w_loaded, 16)
            sp.dma_start(bq[:, :], b_cols[:, 0:NG]).then_inc(w_loaded, 16)
            sp.wait_ge(lo_ready, NG)
            for j in range(HG):
                rows = slice(j * D, (j + 1) * D)
                for part, src in enumerate((q_hi, q_hi, q_lo)):
                    dst = q_stack[part * D:(part + 1) * D, :].bitcast(F32).rearrange("d (g j q) -> d g j q", j=HG, q=NQ)
                    sp.dma_start(dst[:, :, j, :], src[rows, :, :].bitcast(F32)).then_inc(stacked, 16)
            sp.wait_ge(stacked, 16 * 3 * HG)
            sp.dma_start(q_scratch, q_stack[0:3 * D, :].bitcast(F32)).then_inc(stacked, 16)
            sp.wait_ge(stacked, 16 * (3 * HG + 1))

        @block.gpsimd
        def _(pool):
            make_identity(nc, pool, ident, zeroed, ident_made)
            nc.gpsimd.memset(head_rows[:, :], 1.0).then_inc(zeroed, 1)
            pool.wait_ge(zeroed, 2)
            nc.gpsimd.affine_select(out=head_rows[:, :], in_=head_rows[:, :], compare_op=ALU.is_ge, fill=0.0,
                                    base=0, pattern=[[-D, HG]], channel_multiplier=1).then_inc(zeroed, 1)
            pool.wait_ge(zeroed, 3)
            nc.gpsimd.affine_select(out=head_rows[:, :], in_=head_rows[:, :], compare_op=ALU.is_ge, fill=0.0,
                                    base=D - 1, pattern=[[D, HG]], channel_multiplier=-1).then_inc(zeroed, 1)
            pool.wait_ge(zeroed, 4)
            nc.gpsimd.memset(q_stack[3 * D:QROWS, :].bitcast(F32), 0.0).then_inc(zeroed, 1)

        @block.vector
        def _(dve):
            dve.wait_ge(x_in, 16)
            norm_vector(nc, dve, x_sb, xn, stats, mv, var, root, rstd, chain, var_ready, root_ready, normed)
            for g in range(NG):
                dve.wait_ge(hi_ready, g + 1)
                nc.vector.scalar_tensor_tensor(q_lo[:, g, :], proj[g][:, :], bq[:, g:g + 1], q_hi[:, g, :].bitcast(F32),
                                               ALU.add, ALU.subtract).then_inc(lo_ready, 1)
            nc.vector.tensor_reduce(q_top[:, :], q_hi[:, :, :].bitcast(F32), X, ALU.max,
                                    apply_absolute_value=True).then_inc(chain, 1)

        @block.tensor
        def _(pe):
            pe.wait_ge(ident_made, 1)
            norm_transpose(nc, pe, xn, ident, turn, normed, turned)
            pe.wait_ge(w_loaded, 32)
            pe.wait_ge(xt_ready, ET)
            for g in range(NG):
                for d in range(ET):
                    last = nc.tensor.matmul(proj[g][:, :], wq[:, d, g * P:(g + 1) * P], xt[:, d, :],
                                            start=(d == 0), stop=(d == ET - 1))
                last.then_inc(projected, 1)

        @block.scalar
        def _(act):
            norm_scalar(nc, act, var, root, var_ready, root_ready)
            act.wait_ge(turned, 1)
            for d in range(ET):
                nc.scalar.activation(xt[:, d, :], turn[d][:, :], ACT.Copy).then_inc(xt_ready, 1)
            act.wait_ge(w_loaded, 32)
            for g in range(NG):
                act.wait_ge(projected, g + 1)
                nc.scalar.activation(q_hi[:, g, :], proj[g][:, :], ACT.Identity,
                                     bias=bq[:, g:g + 1]).then_inc(hi_ready, 1)


def stream_context(nc, ctx, c_dram, w_in, b_in, b_cols, k_hi_dram, k_lo_dram, v_dram, q_top, head_rows, bounded):
    sb = lambda n, s, d=F32: ctx.enter_context(nc.sbuf_tensor(n, s, d))
    sem = lambda n: ctx.enter_context(nc.semaphore(n))
    w = sb("sc_w", [P, ET, 2 * E])
    w_hi = sb("sc_w_hi", [P, ET, 2 * E], F32R)
    w_lo = sb("sc_w_lo", [P, ET, 2 * E], F32R)
    bk = sb("sc_bk", [P, NG])
    bv = sb("sc_bv", [P, E])
    c = [sb(f"sc_c{b}", [P, ET, CH]) for b in range(2)]
    c_hi = [sb(f"sc_c_hi{b}", [P, ET, CH], F32R) for b in range(2)]
    c_lo = [sb(f"sc_c_lo{b}", [P, ET, CH], F32R) for b in range(2)]
    k_hi = [sb(f"sc_k_hi{b}", [P, NG, CH], F32R) for b in range(2)]
    k_lo = [sb(f"sc_k_lo{b}", [P, NG, CH], F32R) for b in range(2)]
    v = [sb(f"sc_v{b}", [P, KT, E]) for b in range(2)]
    kp = [ctx.enter_context(nc.psum_tensor(f"sc_kp{g}", [P, CH], F32)) for g in range(NG)]
    vp = [ctx.enter_context(nc.psum_tensor(f"sc_vp{t}", [P, E], F32)) for t in range(KT)]
    k_top = [sb(f"sc_k_top{b}", [P, NG]) for b in range(2)]
    k_top_all = sb("sc_k_top_all", [P, NG])
    product = sb("sc_product", [P, NG])
    bound = sb("sc_bound", [1, 1])
    k_topped, k_top_kept, product_ready, bound_done, bound_ready, flagged = map(sem, (
        "sc_k_topped", "sc_k_top_kept", "sc_product_ready", "sc_bound_done", "sc_bound_ready", "sc_flagged"))
    w_loaded, w_hi_ready, w_lo_ready = map(sem, ("sc_w_loaded", "sc_w_hi_ready", "sc_w_lo_ready"))
    c_loaded = [sem(f"sc_c_loaded{b}") for b in range(2)]
    c_hi_ready, c_lo_ready = map(sem, ("sc_c_hi_ready", "sc_c_lo_ready"))
    k_done, v_done = map(sem, ("sc_k_done", "sc_v_done"))
    k_hi_ready, k_lo_ready, v_ready = map(sem, ("sc_k_hi_ready", "sc_k_lo_ready", "sc_v_ready"))
    stored = [sem(f"sc_stored{b}") for b in range(2)]
    PAIRS, STORES = NCH // 2, 3 * 16
    c_view = c_dram.rearrange("(t p) n -> p t n", p=P)
    k_hi_view = k_hi_dram.rearrange("(g p) n -> p g n", p=P)
    k_lo_view = k_lo_dram.rearrange("(g p) n -> p g n", p=P)

    with nc.Block() as block:
        @block.sync
        def _(sp):
            sp.dma_start(w[:, :, :], w_in[:, E:3 * E].rearrange("(t p) f -> p t f", p=P)).then_inc(w_loaded, 16)
            sp.dma_start(bk[:, :], b_cols[:, NG:2 * NG]).then_inc(w_loaded, 16)
            sp.dma_start(bv[:, :], b_in[2 * E:3 * E].partition_broadcast(P)).then_inc(w_loaded, 16)
            for b in range(2):
                sp.dma_start(c[b][:, :, :], c_view[:, :, b * CH:(b + 1) * CH]).then_inc(c_loaded[b], 16)

            def pair(i, last):
                for b in range(2):
                    n = 2 * i + b
                    if not last:
                        sp.wait_ge(c_lo_ready, n + 1)
                        sp.dma_start(c[b][:, :, :], c_view[:, :, bass.ds((n + 2) * CH, CH)]).then_inc(c_loaded[b], 16)
                    cols = bass.ds(n * CH, CH)
                    sp.wait_ge(k_lo_ready, NG * (n + 1))
                    sp.dma_start(k_hi_view[:, :, cols], k_hi[b][:, :, :].bitcast(F32)).then_inc(stored[b], 16)
                    sp.dma_start(k_lo_view[:, :, cols], k_lo[b][:, :, :].bitcast(F32)).then_inc(stored[b], 16)
                    sp.wait_ge(v_ready, KT * (n + 1))
                    sp.dma_start(v_dram[cols, :].rearrange("(t p) f -> p t f", p=P), v[b][:, :, :]).then_inc(stored[b], 16)

            rolled(sp, PAIRS, pair)
            for b in range(2):
                sp.wait_ge(stored[b], STORES * PAIRS)

        @block.vector
        def _(dve):
            for d in range(ET):
                dve.wait_ge(w_hi_ready, d + 1)
                nc.vector.tensor_tensor(w_lo[:, d, :], w[:, d, :], w_hi[:, d, :].bitcast(F32),
                                        ALU.subtract).then_inc(w_lo_ready, 1)
            dve.wait_ge(w_loaded, 48)

            def split(n, b):
                dve.wait_ge(c_hi_ready, n + 1)
                nc.vector.tensor_tensor(c_lo[b][:, :, :], c[b][:, :, :], c_hi[b][:, :, :].bitcast(F32),
                                        ALU.subtract).then_inc(c_lo_ready, 1)

            def pair(i, last):
                for b in range(2):
                    n = 2 * i + b
                    if not (last and b == 1):
                        split(n + 1, 1 - b)
                    for g in range(NG):
                        dve.wait_ge(k_hi_ready, NG * n + g + 1)
                        nc.vector.scalar_tensor_tensor(k_lo[b][:, g, :], kp[g][:, :], bk[:, g:g + 1],
                                                       k_hi[b][:, g, :].bitcast(F32), ALU.add,
                                                       ALU.subtract).then_inc(k_lo_ready, 1)
                    nc.vector.tensor_reduce(k_top[b][:, :], k_hi[b][:, :, :].bitcast(F32), X, ALU.max,
                                            apply_absolute_value=True).then_inc(k_topped, 1)
                    wait_reuse(dve, stored[b], STORES * i)
                    for t in range(KT):
                        dve.wait_ge(v_done, KT * n + t + 1)
                        nc.vector.tensor_tensor(v[b][:, t, :], vp[t][:, :], bv[:, :], ALU.add).then_inc(v_ready, 1)
                    dve.wait_ge(k_topped, n + 1)
                    dve.wait_ge(k_top_kept, n + 1)
                    nc.vector.tensor_tensor(k_top_all[:, :], k_top_all[:, :], k_top[b][:, :], ALU.max).then_inc(k_top_kept, 1)

            nc.vector.memset(k_top_all[:, :], 0.0).then_inc(k_top_kept, 1)
            split(0, 0)
            rolled(dve, PAIRS, pair)
            dve.wait_ge(k_top_kept, NCH + 1)
            nc.vector.tensor_tensor(product[:, :], q_top[:, :], k_top_all[:, :], ALU.mult).then_inc(product_ready, 1)
            dve.wait_ge(bound_done, 1)
            nc.vector.reduce_max(bound[:, :], kp[0][0:1, 0:H], X).then_inc(bound_ready, 1)
            dve.wait_ge(bound_ready, 1)
            nc.vector.tensor_scalar(bounded[:, :], bound[:, :], SAFE / SCALE, None, ALU.is_le).then_inc(flagged, 1)

        @block.tensor
        def _(pe):
            pe.wait_ge(w_lo_ready, ET)
            def pair(i, last):
                for b in range(2):
                    n = 2 * i + b
                    pe.wait_ge(c_lo_ready, n + 1)
                    wait_reuse(pe, k_lo_ready, NG * n)
                    for g in range(NG):
                        for a, (lhs, rhs) in enumerate(((w_hi, c_hi), (w_lo, c_hi), (w_hi, c_lo))):
                            for d in range(ET):
                                last = nc.tensor.matmul(kp[g][:, :], lhs[:, d, g * P:(g + 1) * P], rhs[b][:, d, :],
                                                        start=(a == 0 and d == 0), stop=(a == 2 and d == ET - 1))
                        last.then_inc(k_done, 1)
                    wait_reuse(pe, v_ready, KT * n)
                    for t in range(KT):
                        for a, (lhs, rhs) in enumerate(((c_hi, w_hi), (c_lo, w_hi), (c_hi, w_lo))):
                            for d in range(ET):
                                last = nc.tensor.matmul(vp[t][:, :], lhs[b][:, d, t * P:(t + 1) * P], rhs[:, d, E:2 * E],
                                                        start=(a == 0 and d == 0), stop=(a == 2 and d == ET - 1))
                        last.then_inc(v_done, 1)

            rolled(pe, PAIRS, pair)
            pe.wait_ge(product_ready, 1)
            for g in range(NG):
                last = nc.tensor.matmul(kp[0][0:1, g * HG:(g + 1) * HG], product[:, g:g + 1], head_rows[:, :],
                                        start=True, stop=True)
            last.then_inc(bound_done, 1)

        @block.scalar
        def _(act):
            act.wait_ge(w_loaded, 48)
            for d in range(ET):
                nc.scalar.activation(w_hi[:, d, :], w[:, d, :], ACT.Copy).then_inc(w_hi_ready, 1)

            def split(n, i, b):
                act.wait_ge(c_loaded[b], 16 * (i + 1))
                nc.scalar.activation(c_hi[b][:, :, :], c[b][:, :, :], ACT.Copy).then_inc(c_hi_ready, 1)

            def pair(i, last):
                for b in range(2):
                    n = 2 * i + b
                    if not (last and b == 1):
                        wait_reuse(act, v_done, KT * n)
                        split(n + 1, i + b, 1 - b)
                    wait_reuse(act, k_topped, n - 1)
                    wait_reuse(act, stored[b], STORES * i)
                    for g in range(NG):
                        act.wait_ge(k_done, NG * n + g + 1)
                        nc.scalar.activation(k_hi[b][:, g, :], kp[g][:, :], ACT.Identity,
                                             bias=bk[:, g:g + 1]).then_inc(k_hi_ready, 1)

            split(0, 0, 0)
            rolled(act, PAIRS, pair)


def find_maxima(nc, ctx, k_hi_dram, k_lo_dram, q_scratch, ident, q_stack, bounded):
    sb = lambda n, s, d=F32: ctx.enter_context(nc.sbuf_tensor(n, s, d))
    sem = lambda n: ctx.enter_context(nc.semaphore(n))
    KB = 2048
    NKB = NK // KB
    UNITS = NKB * QT
    q = [sb(f"fm_q{b}", [3 * D, NQ], F32R) for b in range(2)]
    k = [sb(f"fm_k{b}", [3 * D, NK], F32R) for b in range(2)]
    block_max = [sb(f"fm_block_max{b}", [P, QT, NKB]) for b in range(2)]
    head_max = [sb(f"fm_head_max{b}", [P, QT]) for b in range(2)]
    minus_max = sb("fm_minus_max", [P, H * QT])
    minus_row = sb("fm_minus_row", [H * QT, P], F32R)
    s = [ctx.enter_context(nc.psum_tensor(f"fm_s{r}", [P, KB], F32)) for r in range(2)]
    loaded = [sem(f"fm_loaded{b}") for b in range(2)]
    head_reduced = [sem(f"fm_head_reduced{b}") for b in range(2)]
    scored = [sem(f"fm_scored{r}") for r in range(2)]
    reduced = [sem(f"fm_reduced{r}") for r in range(2)]
    negated, turned, row_ready, placed = map(sem, (
        "fm_negated", "fm_turned", "fm_row_ready", "fm_placed"))
    LOADS = 4 * 16
    PER = UNITS // 2

    with nc.Block() as block:
        @block.sync
        def _(sp):
            flag = sp.value_load(bounded[:, :], min_val=0, max_val=1)
            with sp.If(flag < 1):
                def pair(i, last):
                    for b in range(2):
                        h = 2 * i + b
                        rows = bass.ds(h * D, D)
                        wait_reuse(sp, head_reduced[b], i)
                        sp.dma_start(q[b][:, :].bitcast(F32), q_scratch[:, bass.ds(h * NQ, NQ)]).then_inc(loaded[b], 16)
                        sp.dma_start(k[b][0:D, :].bitcast(F32), k_hi_dram[rows, :]).then_inc(loaded[b], 16)
                        sp.dma_start(k[b][D:2 * D, :].bitcast(F32), k_lo_dram[rows, :]).then_inc(loaded[b], 16)
                        sp.dma_start(k[b][2 * D:3 * D, :].bitcast(F32), k_hi_dram[rows, :]).then_inc(loaded[b], 16)
                rolled(sp, H // 2, pair)
                sp.wait_ge(row_ready, 1)
                sp.dma_start(q_stack[3 * D:QROWS, :].bitcast(F32), minus_row[:, :].bitcast(F32)).then_inc(placed, 16)
                sp.wait_ge(placed, 16)

        @block.tensor
        def _(pe):
            flag = pe.value_load(bounded[:, :], min_val=0, max_val=1)
            with pe.If(flag < 1):
                def pair(i, last):
                    for b in range(2):
                        h = 2 * i + b
                        pe.wait_ge(loaded[b], LOADS * (i + 1))
                        for u in range(UNITS):
                            kb, qt, r = u // QT, u % QT, u % 2
                            wait_reuse(pe, reduced[r], PER * h + u // 2)
                            for n in range(KB // 512):
                                cols = slice(kb * KB + n * 512, kb * KB + (n + 1) * 512)
                                last = nc.tensor.matmul(s[r][:, n * 512:(n + 1) * 512], q[b][:, qt * P:(qt + 1) * P],
                                                        k[b][:, cols], start=True, stop=True)
                            last.then_inc(scored[r], 1)
                rolled(pe, H // 2, pair)
                pe.wait_ge(negated, H)
                nc.tensor.transpose(s[0][0:H * QT, 0:P], minus_max[:, :], ident[:, :]).then_inc(turned, 1)

        @block.vector
        def _(dve):
            flag = dve.value_load(bounded[:, :], min_val=0, max_val=1)
            with dve.If(flag < 1):
                with dve.Fori(0, H // 2) as i:
                    for b in range(2):
                        h = 2 * i + b
                        for u in range(UNITS):
                            kb, qt, r = u // QT, u % QT, u % 2
                            dve.wait_ge(scored[r], PER * h + u // 2 + 1)
                            nc.vector.reduce_max(block_max[b][:, qt, kb:kb + 1], s[r][:, :], X).then_inc(reduced[r], 1)
                        for r in range(2):
                            dve.wait_ge(reduced[r], PER * (h + 1))
                        nc.vector.reduce_max(head_max[b][:, :], block_max[b][:, :, :], X).then_inc(head_reduced[b], 1)
                        dve.wait_ge(head_reduced[b], i + 1)
                        nc.vector.tensor_scalar(minus_max[:, bass.ds(h * QT, QT)], head_max[b][:, :], -1.0, None,
                                                ALU.mult).then_inc(negated, 1)

        @block.scalar
        def _(act):
            flag = act.value_load(bounded[:, :], min_val=0, max_val=1)
            with act.If(flag < 1):
                act.wait_ge(turned, 1)
                nc.scalar.activation(minus_row[:, :], s[0][0:H * QT, 0:P], ACT.Copy).then_inc(row_ready, 1)


def attend(nc, ctx, k_hi_dram, k_lo_dram, v_dram, q_stack, o_acc, p_sum, total_acc):
    sb = lambda n, s, d=F32: ctx.enter_context(nc.sbuf_tensor(n, s, d))
    sem = lambda n: ctx.enter_context(nc.semaphore(n))
    CB = 4
    ITERS = NG * NCH // CB
    PER_GROUP = NCH // CB
    UNITS = CB * KT * 2
    BY_PE = (6, 13, 19, 26, 31)
    SR, PR = 3, 8
    PPR = UNITS // PR
    LOADS = 4 * 16
    k = [sb(f"at_k{c}", [QROWS, HG, CH], F32R) for c in range(CB)]
    v = [sb(f"at_v{c}", [P, KT, P]) for c in range(CB)]
    p = [sb(f"at_p{r}", [P, 2 * NQ]) for r in range(PR)]
    s = [ctx.enter_context(nc.psum_tensor(f"at_s{r}", [P, 2 * NQ], F32)) for r in range(SR)]
    o = ctx.enter_context(nc.psum_tensor("at_o", [P, NQ], F32))
    totals = ctx.enter_context(nc.psum_tensor("at_totals", [P, NQ], F32))
    ones = sb("at_ones", [P, D])
    ones_set, zeroed = map(sem, ("at_ones_set", "at_zeroed"))
    loaded = [sem(f"at_loaded{c}") for c in range(CB)]
    s_ready = [sem(f"at_s_ready{r}") for r in range(SR)]
    p_ready = [sem(f"at_p_ready{r}") for r in range(PR)]
    p_used = [sem(f"at_p_used{r}") for r in range(PR)]
    p_summed = [sem(f"at_p_summed{r}") for r in range(PR)]
    o_added, totals_added = map(sem, ("at_o_added", "at_totals_added"))
    s_uses = [len(range(r, UNITS, SR)) for r in range(SR)]
    s_last = [max(range(r, UNITS, SR)) for r in range(SR)]

    def summed(it, u):
        mine = [w for w in range(u % PR, UNITS, PR) if w not in BY_PE]
        return len(mine) * it + (sum(w <= u for w in mine) if u >= 0 else -sum(w > u + UNITS for w in mine))

    with nc.Block() as block:
        @block.gpsimd
        def _(pool):
            nc.gpsimd.memset(ones[:, :], 1.0).then_inc(ones_set, 1)
            for c in range(CB):
                pool.wait_ge(ones_set, c + 1)
                nc.gpsimd.memset(k[c][3 * D:QROWS, :, :].bitcast(F32), 1.0).then_inc(ones_set, 1)
            pool.wait_ge(ones_set, CB + 1)
            nc.gpsimd.memset(p_sum[:, :], 0.0).then_inc(zeroed, 1)
            pool.wait_ge(zeroed, 1)
            nc.gpsimd.memset(o_acc[:, :, :], 0.0).then_inc(zeroed, 1)
            pool.wait_ge(zeroed, 2)
            nc.gpsimd.memset(total_acc[:, :, :], 0.0).then_inc(zeroed, 1)

        @block.sync
        def _(sp):
            def iteration(it, last):
                g, kb = it // PER_GROUP, it % PER_GROUP
                for c in range(CB):
                    keys = bass.ds((kb * CB + c) * CH, CH)
                    end = (c + 1) * KT * 2 - 1
                    wait_reuse(sp, p_used[end % PR], PPR * it - PPR + end // PR + 1)
                    hi = k_hi_dram[bass.ds(g * P, P), keys].rearrange("(j d) n -> d j n", d=D)
                    lo = k_lo_dram[bass.ds(g * P, P), keys].rearrange("(j d) n -> d j n", d=D)
                    for part, src in enumerate((hi, lo, hi)):
                        sp.dma_start(k[c][part * D:(part + 1) * D, :, :].bitcast(F32), src).then_inc(loaded[c], 16)
                    sp.dma_start(v[c][:, :, :], v_dram[keys, bass.ds(g * P, P)].rearrange("(t p) f -> p t f", p=P)).then_inc(loaded[c], 16)

            rolled(sp, ITERS, iteration)

        @block.tensor
        def _(pe):
            def scores(it, g, u):
                kt, pair, r = u // 2, u % 2, u % SR
                c, t = kt // KT, kt % KT
                if t == 0 and pair == 0:
                    pe.wait_ge(loaded[c], LOADS * (it + 1))
                if u >= SR:
                    pe.wait_ge(p_ready[(u - SR) % PR], PPR * it + (u - SR) // PR + 1)
                else:
                    wait_reuse(pe, p_ready[s_last[r] % PR], PPR * it - PPR + s_last[r] // PR + 1)
                for a in range(2):
                    j = 2 * pair + a
                    last = nc.tensor.matmul(s[r][:, a * NQ:(a + 1) * NQ], k[c][:, j, t * P:(t + 1) * P],
                                            q_stack[:, bass.ds(g * (HG * NQ) + j * NQ, NQ)], start=True, stop=True)
                last.then_inc(s_ready[r], 1)

            def outputs(it, u):
                kt, pair, r = u // 2, u % 2, u % PR
                c, t = kt // KT, kt % KT
                if u == 0:
                    wait_reuse(pe, o_added, it)
                if u == BY_PE[0]:
                    wait_reuse(pe, totals_added, it)
                pe.wait_ge(p_ready[r], PPR * it + u // PR + 1)
                for a in range(2):
                    j = 2 * pair + a
                    last = nc.tensor.matmul(o[j * D:(j + 1) * D, :], v[c][:, t, j * D:(j + 1) * D],
                                            p[r][:, a * NQ:(a + 1) * NQ], start=(u < 2), stop=(u >= UNITS - 2))
                if u in BY_PE:
                    same = [w for w in BY_PE if w % 2 == pair]
                    for a in range(2):
                        j = 2 * pair + a
                        last = nc.tensor.matmul(totals[j * D:(j + 1) * D, :], ones[:, :], p[r][:, a * NQ:(a + 1) * NQ],
                                                start=(u == same[0]), stop=(u == same[-1]))
                last.then_inc(p_used[r], 1)

            def iteration(it, last):
                for u in range(UNITS):
                    if u + 2 < UNITS:
                        scores(it, it // PER_GROUP, u + 2)
                    elif not last:
                        scores(it + 1, (it + 1) // PER_GROUP, u + 2 - UNITS)
                    outputs(it, u)

            pe.wait_ge(ones_set, CB + 1)
            scores(0, 0, 0)
            scores(0, 0, 1)
            rolled(pe, ITERS, iteration)

        @block.scalar
        def _(act):
            def iteration(it, last):
                for u in range(UNITS):
                    act.wait_ge(s_ready[u % SR], s_uses[u % SR] * it + u // SR + 1)
                    wait_reuse(act, p_used[u % PR], PPR * it + u // PR)
                    wait_reuse(act, p_summed[u % PR], summed(it, u - PR))
                    nc.scalar.activation(p[u % PR][:, :], s[u % SR][:, :], ACT.Exp, scale=SCALE).then_inc(p_ready[u % PR], 1)

            rolled(act, ITERS, iteration)

        @block.vector
        def _(dve):
            dve.wait_ge(zeroed, 3)
            def iteration(it, last):
                g = it // PER_GROUP
                for u in range(UNITS):
                    if u in BY_PE:
                        continue
                    r = u % PR
                    sums = p_sum[:, bass.ds(g * (HG * NQ) + (u % 2) * 2 * NQ, 2 * NQ)]
                    dve.wait_ge(p_ready[r], PPR * it + u // PR + 1)
                    before = max(w for w in range(-UNITS, u) if w % 2 == u % 2 and w % UNITS not in BY_PE)
                    wait_reuse(dve, p_summed[before % PR], summed(it, before))
                    nc.vector.tensor_tensor(sums, sums, p[r][:, :], ALU.add).then_inc(p_summed[r], 1)
                end = UNITS - 1
                dve.wait_ge(p_used[end % PR], PPR * it + end // PR + 1)
                for bank, acc, added in ((o, o_acc, o_added), (totals, total_acc, totals_added)):
                    wait_reuse(dve, added, it)
                    nc.vector.tensor_tensor(acc[:, bass.ds(g, 1), :], acc[:, bass.ds(g, 1), :],
                                            bank[:, :].rearrange("p (a q) -> p a q", a=1), ALU.add).then_inc(added, 1)

            rolled(dve, ITERS, iteration)


def cross_output(nc, ctx, w_out, b_out, o_acc, p_sum, total_acc, x_sb):
    sb = lambda n, s, d=F32: ctx.enter_context(nc.sbuf_tensor(n, s, d))
    sem = lambda n: ctx.enter_context(nc.semaphore(n))
    wo = sb("co_wo", [P, ET, E])
    bo = sb("co_bo", [P, E])
    ones = sb("co_ones", [P, D])
    rec = sb("co_rec", [P, NG, NQ])
    heads = sb("co_heads", [P, NG, NQ])
    total = [ctx.enter_context(nc.psum_tensor(f"co_total{g}", [P, NQ], F32)) for g in range(NG)]
    out = [ctx.enter_context(nc.psum_tensor(f"co_out{t}", [P, E], F32)) for t in range(QT)]
    loaded, ones_set, totalled, summed, inverted, normed, biased, projected, added = map(sem, (
        "co_loaded", "co_ones_set", "co_totalled", "co_summed", "co_inverted", "co_normed", "co_biased", "co_projected", "co_added"))

    with nc.Block() as block:
        @block.sync
        def _(sp):
            sp.dma_start(wo[:, :, :], w_out.rearrange("(t p) f -> p t f", p=P)).then_inc(loaded, 16)
            sp.dma_start(bo[:, :], b_out.partition_broadcast(P)).then_inc(loaded, 16)

        @block.gpsimd
        def _(pool):
            nc.gpsimd.memset(ones[:, :], 1.0).then_inc(ones_set, 1)

        @block.tensor
        def _(pe):
            pe.wait_ge(ones_set, 1)
            for g in range(NG):
                for j in range(HG):
                    h = g * HG + j
                    last = nc.tensor.matmul(total[g][j * D:(j + 1) * D, :], ones[:, :], p_sum[:, h * NQ:(h + 1) * NQ],
                                            start=True, stop=True)
                last.then_inc(totalled, 1)
            pe.wait_ge(loaded, 32)
            for g in range(NG):
                pe.wait_ge(normed, g + 1)
                for t in range(QT):
                    last = nc.tensor.matmul(out[t][:, :], heads[:, g, t * P:(t + 1) * P], wo[:, g, :],
                                            start=(g == 0), stop=(g == NG - 1))
            last.then_inc(projected, 1)

        @block.vector
        def _(dve):
            for g in range(NG):
                dve.wait_ge(totalled, g + 1)
                nc.vector.tensor_tensor(total_acc[:, g, :], total_acc[:, g, :], total[g][:, :], ALU.add).then_inc(summed, 1)
                dve.wait_ge(summed, g + 1)
                nc.vector.reciprocal(rec[:, g, :], total_acc[:, g, :]).then_inc(inverted, 1)
                dve.wait_ge(inverted, g + 1)
                nc.vector.tensor_tensor(heads[:, g, :], o_acc[:, g, :], rec[:, g, :], ALU.mult).then_inc(normed, 1)
            dve.wait_ge(loaded, 32)
            for t in range(QT):
                nc.vector.tensor_tensor(x_sb[:, t, :], x_sb[:, t, :], bo[:, :], ALU.add).then_inc(biased, 1)
            dve.wait_ge(projected, 1)
            for t in range(QT):
                dve.wait_ge(biased, t + 1)
                nc.vector.tensor_tensor(x_sb[:, t, :], x_sb[:, t, :], out[t][:, :], ALU.add).then_inc(added, 1)


def self_attention(nc, ctx, w_in, b_cols, w_out, b_out, ident, x_sb):
    sb = lambda n, s, d=F32: ctx.enter_context(nc.sbuf_tensor(n, s, d))
    sem = lambda n: ctx.enter_context(nc.semaphore(n))
    wv = sb("sa_wv", [P, ET, E])
    wo = sb("sa_wo", [P, ET, E])
    bv = sb("sa_bv", [P, ET])
    bo = sb("sa_bo", [P, E])
    xn = sb("sa_xn", [P, QT, E])
    xt = sb("sa_xt", [P, ET, NQ])
    vt = sb("sa_vt", [P, ET, NQ])
    stats = sb("sa_stats", [P, QT, 6])
    mv = sb("sa_mv", [P, QT, 2])
    var = sb("sa_var", [P, QT])
    root = sb("sa_root", [P, QT])
    rstd = sb("sa_rstd", [P, 5, QT])
    var_ready, root_ready = map(sem, ("sa_var_ready", "sa_root_ready"))
    turn = [ctx.enter_context(nc.psum_tensor(f"sa_turn{d}", [P, NQ], F32)) for d in range(ET)]
    proj = [ctx.enter_context(nc.psum_tensor(f"sa_proj{d}", [P, NQ], F32)) for d in range(ET)]
    loaded, chain, normed, turned, xt_ready, v_done, v_ready, biased, projected, added = map(sem, (
        "sa_loaded", "sa_chain", "sa_normed", "sa_turned", "sa_xt_ready", "sa_v_done", "sa_v_ready",
        "sa_biased", "sa_projected", "sa_added"))

    with nc.Block() as block:
        @block.sync
        def _(sp):
            sp.dma_start(wv[:, :, :], w_in[:, 2, :].rearrange("(t p) f -> p t f", p=P)).then_inc(loaded, 16)
            sp.dma_start(bv[:, :], b_cols[:, 2 * ET:3 * ET]).then_inc(loaded, 16)
            sp.dma_start(wo[:, :, :], w_out.rearrange("(t p) f -> p t f", p=P)).then_inc(loaded, 16)
            sp.dma_start(bo[:, :], b_out.partition_broadcast(P)).then_inc(loaded, 16)

        @block.tensor
        def _(pe):
            norm_transpose(nc, pe, xn, ident, turn, normed, turned)
            pe.wait_ge(loaded, 64)
            pe.wait_ge(xt_ready, ET)
            for f in range(ET):
                for d in range(ET):
                    last = nc.tensor.matmul(proj[f][:, :], wv[:, d, f * P:(f + 1) * P], xt[:, d, :],
                                            start=(d == 0), stop=(d == ET - 1))
                last.then_inc(v_done, 1)
            for f in range(ET):
                pe.wait_ge(v_ready, f + 1)
                for t in range(QT):
                    last = nc.tensor.matmul(turn[t][:, :], vt[:, f, t * P:(t + 1) * P], wo[:, f, :],
                                            start=(f == 0), stop=(f == ET - 1))
            last.then_inc(projected, 1)

        @block.scalar
        def _(act):
            norm_scalar(nc, act, var, root, var_ready, root_ready)
            act.wait_ge(turned, 1)
            for d in range(ET):
                nc.scalar.activation(xt[:, d, :], turn[d][:, :], ACT.Copy).then_inc(xt_ready, 1)
            act.wait_ge(loaded, 64)
            for f in range(ET):
                act.wait_ge(v_done, f + 1)
                nc.scalar.activation(vt[:, f, :], proj[f][:, :], ACT.Identity, bias=bv[:, f:f + 1]).then_inc(v_ready, 1)

        @block.vector
        def _(dve):
            norm_vector(nc, dve, x_sb, xn, stats, mv, var, root, rstd, chain, var_ready, root_ready, normed)
            dve.wait_ge(loaded, 64)
            for t in range(QT):
                dve.wait_ge(normed, t + 1)
                nc.vector.tensor_tensor(x_sb[:, t, :], x_sb[:, t, :], bo[:, :], ALU.add).then_inc(biased, 1)
            dve.wait_ge(projected, 1)
            for t in range(QT):
                dve.wait_ge(biased, t + 1)
                nc.vector.tensor_tensor(x_sb[:, t, :], x_sb[:, t, :], turn[t][:, :], ALU.add).then_inc(added, 1)


def feed_forward(nc, ctx, w_gate, w_in, b_in, w_out, b_out, ident, x_sb, out_dram):
    sb = lambda n, s, d=F32: ctx.enter_context(nc.sbuf_tensor(n, s, d))
    sem = lambda n: ctx.enter_context(nc.semaphore(n))
    xn = sb("ff_xn", [P, QT, E])
    xt = sb("ff_xt", [P, ET, NQ])
    xt_hi = sb("ff_xt_hi", [P, ET, NQ], F32R)
    xt_lo = sb("ff_xt_lo", [P, ET, NQ], F32R)
    stats = sb("ff_stats", [P, QT, 6])
    mv = sb("ff_mv", [P, QT, 2])
    var = sb("ff_var", [P, QT])
    root = sb("ff_root", [P, QT])
    rstd = sb("ff_rstd", [P, 5, QT])
    var_ready, root_ready = map(sem, ("ff_var_ready", "ff_root_ready"))
    wg = sb("ff_wg", [P, ET, NX])
    bo = sb("ff_bo", [NX, E])
    numbers = sb("ff_numbers", [P, NX])
    logits = sb("ff_logits", [P, QT, NX])
    sorted8 = sb("ff_sorted8", [P, QT, NX])
    places = sb("ff_places", [P, QT, NX], U32)
    places_f = sb("ff_places_f", [P, QT, NX])
    gap = sb("ff_gap", [P, QT])
    ratio = sb("ff_ratio", [P, QT])
    weight = sb("ff_weight", [P, 2, QT])
    first = sb("ff_first", [P, QT, NX])
    second = sb("ff_second", [P, QT, NX])
    combine = sb("ff_combine", [P, QT, NX])
    combine_t = sb("ff_combine_t", [NX, NQ])
    b_hidden = sb("ff_b_hidden", [P, NX, M // P])
    b_cur = sb("ff_b_cur", [P, M // P])
    wi = [sb(f"ff_wi{b}", [P, ET, MC]) for b in range(2)]
    wi_hi = [sb(f"ff_wi_hi{b}", [P, ET, MC], F32R) for b in range(2)]
    wi_lo = [sb(f"ff_wi_lo{b}", [P, ET, MC], F32R) for b in range(2)]
    wo = [sb(f"ff_wo{b}", [P, MT, E]) for b in range(2)]
    wo_hi = [sb(f"ff_wo_hi{b}", [P, MT, E], F32R) for b in range(2)]
    wo_lo = [sb(f"ff_wo_lo{b}", [P, MT, E], F32R) for b in range(2)]
    h = sb("ff_h", [P, MT, NQ])
    h_hi = [sb(f"ff_h_hi{b}", [P, MT, NQ], F32R) for b in range(2)]
    h_lo = [sb(f"ff_h_lo{b}", [P, MT, NQ], F32R) for b in range(2)]
    hp = [ctx.enter_context(nc.psum_tensor(f"ff_hp{t}", [P, NQ], F32)) for t in range(MT)]
    yp = [ctx.enter_context(nc.psum_tensor(f"ff_yp{t}", [P, E], F32)) for t in range(QT)]
    small, chain, normed, turned, xt_ready, xt_hi_ready, xt_lo_ready = map(sem, (
        "ff_small", "ff_chain", "ff_normed", "ff_turned", "ff_xt_ready", "ff_xt_hi_ready", "ff_xt_lo_ready"))
    numbered, gated, link, gap_ready, ratio_ready, combined, combine_turned, combine_t_ready, bias_done, bias_added = map(sem, (
        "ff_numbered", "ff_gated", "ff_link", "ff_gap_ready", "ff_ratio_ready", "ff_combined", "ff_combine_turned",
        "ff_combine_t_ready", "ff_bias_done", "ff_bias_added"))
    wi_loaded = [sem(f"ff_wi_loaded{b}") for b in range(2)]
    wo_loaded = [sem(f"ff_wo_loaded{b}") for b in range(2)]
    wi_hi_ready, wi_lo_ready, wo_hi_ready, wo_lo_ready = map(sem, (
        "ff_wi_hi_ready", "ff_wi_lo_ready", "ff_wo_hi_ready", "ff_wo_lo_ready"))
    h_done, h_ready, h_lo_ready, h_hi_ready, y_done, y_added, b_ready, stored = map(sem, (
        "ff_h_done", "ff_h_ready", "ff_h_lo_ready", "ff_h_hi_ready", "ff_y_done", "ff_y_added", "ff_b_ready", "ff_stored"))

    with nc.Block() as block:
        @block.sync
        def _(sp):
            sp.dma_start(wg[:, :, :], w_gate.rearrange("(t p) e -> p t e", p=P)).then_inc(small, 16)
            sp.dma_start(bo[:, :], b_out).then_inc(small, 16)
            sp.dma_start(b_hidden[:, :, :], b_in).then_inc(small, 16)

            def load_in(n, e, mc):
                sp.dma_start(wi[mc % 2][:, :, :], w_in[bass.ds(e * E, E), mc * MC:(mc + 1) * MC].rearrange("(t p) m -> p t m", p=P)).then_inc(wi_loaded[mc % 2], 16)

            def load_out(n, e, mc):
                sp.dma_start(wo[mc % 2][:, :, :], w_out[bass.ds(e * M + mc * MC, MC), :].rearrange("(t p) f -> p t f", p=P)).then_inc(wo_loaded[mc % 2], 16)

            for mc in range(2):
                load_in(mc, 0, mc)
                load_out(mc, 0, mc)

            def expert(e, last):
                for mc in range(NMC):
                    n = NMC * e + mc
                    e2, mc2 = (e, mc + 2) if mc + 2 < NMC else (e + 1, mc + 2 - NMC)
                    if last and mc + 2 >= NMC:
                        continue
                    sp.wait_ge(wi_lo_ready, n + 1)
                    load_in(n + 2, e2, mc2)
                    sp.wait_ge(wo_lo_ready, n + 1)
                    load_out(n + 2, e2, mc2)

            rolled(sp, NX, expert)
            sp.wait_ge(y_added, QT * NX)
            sp.dma_start(out_dram.rearrange("a (t p) e -> p (a t) e", p=P), x_sb[:, :, :]).then_inc(stored, 16)
            sp.wait_ge(stored, 16)

        @block.gpsimd
        def _(pool):
            nc.gpsimd.iota(numbers[:, :], pattern=[[1, NX]], base=0, channel_multiplier=0,
                           allow_small_or_imprecise_dtypes=True).then_inc(numbered, 1)

        @block.tensor
        def _(pe):
            norm_transpose(nc, pe, xn, ident, hp, normed, turned)
            pe.wait_ge(small, 48)
            pe.wait_ge(xt_ready, ET)
            for t in range(QT):
                for d in range(ET):
                    last = nc.tensor.matmul(yp[0][:, t * NX:(t + 1) * NX], xt[:, d, t * P:(t + 1) * P], wg[:, d, :],
                                            start=(d == 0), stop=(d == ET - 1))
            last.then_inc(gated, 1)
            pe.wait_ge(combined, 1)
            for t in range(QT):
                last = nc.tensor.transpose(yp[1][0:NX, t * P:(t + 1) * P], combine[:, t, :], ident[:, :])
            last.then_inc(combine_turned, 1)
            pe.wait_ge(combine_t_ready, 1)
            for t in range(QT):
                last = nc.tensor.matmul(yp[t][:, :], combine_t[:, t * P:(t + 1) * P], bo[:, :], start=True, stop=True)
            last.then_inc(bias_done, 1)
            pe.wait_ge(xt_lo_ready, ET)

            def hidden(e, mc):
                n, b = NMC * e + mc, mc % 2
                pe.wait_ge(wi_lo_ready, n + 1)
                wait_reuse(pe, h_ready, MT * n)
                for t in range(MT):
                    for a, (lhs, rhs) in enumerate(((wi_hi, xt_hi), (wi_lo, xt_hi), (wi_hi, xt_lo))):
                        for d in range(ET):
                            last = nc.tensor.matmul(hp[t][:, :], lhs[b][:, d, t * P:(t + 1) * P], rhs[:, d, :],
                                                    start=(a == 0 and d == 0), stop=(a == 2 and d == ET - 1))
                    last.then_inc(h_done, 1)

            def output(e, mc):
                n, b = NMC * e + mc, mc % 2
                pe.wait_ge(wo_lo_ready, n + 1)
                pe.wait_ge(h_lo_ready, MT * (n + 1))
                if mc == 0:
                    wait_reuse(pe, y_added, QT * e)
                for t in range(QT):
                    for m in range(MT):
                        for a, (lhs, rhs) in enumerate(((h_hi, wo_hi), (h_lo, wo_hi), (h_hi, wo_lo))):
                            last = nc.tensor.matmul(yp[t][:, :], lhs[b][:, m, t * P:(t + 1) * P], rhs[b][:, m, :],
                                                    start=(mc == 0 and m == 0 and a == 0),
                                                    stop=(mc == NMC - 1 and m == MT - 1 and a == 2))
                    last.then_inc(y_done, 1)

            pe.wait_ge(bias_added, QT)
            def expert(e, last):
                hidden(e, 0)
                for mc in range(1, NMC):
                    hidden(e, mc)
                    output(e, mc - 1)
                output(e, NMC - 1)

            rolled(pe, NX, expert)

        @block.scalar
        def _(act):
            norm_scalar(nc, act, var, root, var_ready, root_ready)
            act.wait_ge(turned, 1)
            for d in range(ET):
                nc.scalar.activation(xt[:, d, :], hp[d][:, :], ACT.Copy).then_inc(xt_ready, 1)
            for d in range(ET):
                act.wait_ge(xt_ready, d + 1)
                nc.scalar.activation(xt_hi[:, d, :], xt[:, d, :], ACT.Copy).then_inc(xt_hi_ready, 1)
            act.wait_ge(gap_ready, 1)
            nc.scalar.activation(ratio[:, :], gap[:, :], ACT.Exp).then_inc(ratio_ready, 1)
            act.wait_ge(combine_turned, 1)
            nc.scalar.activation(combine_t[:, :], yp[1][0:NX, :], ACT.Copy).then_inc(combine_t_ready, 1)

            def split_in(n, i, b):
                act.wait_ge(wi_loaded[b], 16 * (i + 1))
                nc.scalar.activation(wi_hi[b][:, :, :], wi[b][:, :, :], ACT.Copy).then_inc(wi_hi_ready, 1)

            def expert(e, last):
                for mc in range(NMC):
                    n, b = NMC * e + mc, mc % 2
                    if mc == 0:
                        act.wait_ge(b_ready, e + 1)
                    if not (last and mc == NMC - 1):
                        wait_reuse(act, h_done, MT * n)
                        split_in(n + 1, 2 * e + (mc + 1) // 2, 1 - b)
                    for t in range(MT):
                        act.wait_ge(h_done, MT * n + t + 1)
                        wait_reuse(act, h_lo_ready, MT * n)
                        nc.scalar.activation(h[:, t, :], hp[t][:, :], ACT.Gelu,
                                             bias=b_cur[:, mc * MT + t:mc * MT + t + 1]).then_inc(h_ready, 1)
                    act.wait_ge(wo_loaded[b], 16 * (2 * e + mc // 2 + 1))
                    if mc > 0:
                        wait_reuse(act, y_done, QT * (n - 1))
                    else:
                        wait_reuse(act, y_done, QT * NMC * e)
                    nc.scalar.activation(wo_hi[b][:, :, :], wo[b][:, :, :], ACT.Copy).then_inc(wo_hi_ready, 1)

            split_in(0, 0, 0)
            rolled(act, NX, expert)

        @block.vector
        def _(dve):
            norm_vector(nc, dve, x_sb, xn, stats, mv, var, root, rstd, chain, var_ready, root_ready, normed)
            for d in range(ET):
                dve.wait_ge(xt_hi_ready, d + 1)
                nc.vector.tensor_tensor(xt_lo[:, d, :], xt[:, d, :], xt_hi[:, d, :].bitcast(F32), ALU.subtract).then_inc(xt_lo_ready, 1)

            dve.wait_ge(gated, 1)
            nc.vector.tensor_copy(logits[:, :, :], yp[0][:, 0:QT * NX].rearrange("p (t e) -> p t e", e=NX)).then_inc(link, 1)
            dve.wait_ge(link, 1)
            for t in range(QT):
                nc.vector.max(sorted8[:, t, :], logits[:, t, :]).then_inc(link, 1)
            dve.wait_ge(link, 1 + QT)
            for t in range(QT):
                nc.vector.max_index(places[:, t, :], sorted8[:, t, :], logits[:, t, :]).then_inc(link, 1)
            nc.vector.tensor_tensor(gap[:, :], sorted8[:, :, 1], sorted8[:, :, 0], ALU.subtract).then_inc(gap_ready, 1)
            dve.wait_ge(link, 1 + 2 * QT)
            nc.vector.tensor_copy(places_f[:, :, :], places[:, :, :]).then_inc(link, 1)
            dve.wait_ge(ratio_ready, 1)
            nc.vector.tensor_scalar(weight[:, 1, :], ratio[:, :], 1.0, None, ALU.add).then_inc(link, 1)
            dve.wait_ge(link, 3 + 2 * QT)
            nc.vector.reciprocal(weight[:, 0, :], weight[:, 1, :]).then_inc(link, 1)
            dve.wait_ge(link, 4 + 2 * QT)
            nc.vector.tensor_tensor(weight[:, 1, :], weight[:, 0, :], ratio[:, :], ALU.mult).then_inc(link, 1)
            dve.wait_ge(numbered, 1)
            dve.wait_ge(link, 5 + 2 * QT)
            for t in range(QT):
                nc.vector.tensor_scalar(first[:, t, :], numbers[:, :], places_f[:, t, 0:1], weight[:, 0, t:t + 1],
                                        ALU.is_equal, ALU.mult).then_inc(link, 1)
                nc.vector.tensor_scalar(second[:, t, :], numbers[:, :], places_f[:, t, 1:2], weight[:, 1, t:t + 1],
                                        ALU.is_equal, ALU.mult).then_inc(link, 1)
            dve.wait_ge(link, 5 + 4 * QT)
            nc.vector.tensor_tensor(combine[:, :, :], first[:, :, :], second[:, :, :], ALU.add).then_inc(combined, 1)
            dve.wait_ge(bias_done, 1)
            for t in range(QT):
                nc.vector.tensor_tensor(x_sb[:, t, :], x_sb[:, t, :], yp[t][:, :], ALU.add).then_inc(bias_added, 1)
            dve.wait_ge(bias_added, QT)
            dve.wait_ge(combined, 1)
            dve.wait_ge(small, 48)

            def split_in(n, b):
                dve.wait_ge(wi_hi_ready, n + 1)
                nc.vector.tensor_tensor(wi_lo[b][:, :, :], wi[b][:, :, :], wi_hi[b][:, :, :].bitcast(F32), ALU.subtract).then_inc(wi_lo_ready, 1)

            def expert(e, last):
                wait_reuse(dve, h_ready, NMC * MT * e)
                nc.vector.tensor_scalar(b_cur[:, :], b_hidden[:, bass.ds(e, 1), :].rearrange("p a t -> p (a t)"), 1.0, None, ALU.mult).then_inc(b_ready, 1)
                for mc in range(NMC):
                    n, b = NMC * e + mc, mc % 2
                    if not (last and mc == NMC - 1):
                        split_in(n + 1, 1 - b)
                    wait_reuse(dve, y_done, QT * (n - 1) if mc > 0 else QT * NMC * e)
                    for t in range(MT):
                        dve.wait_ge(h_ready, MT * n + t + 1)
                        nc.vector.tensor_copy(h_hi[b][:, t, :], h[:, t, :]).then_inc(h_hi_ready, 1)
                        dve.wait_ge(h_hi_ready, MT * n + t + 1)
                        nc.vector.tensor_tensor(h_lo[b][:, t, :], h[:, t, :], h_hi[b][:, t, :].bitcast(F32), ALU.subtract).then_inc(h_lo_ready, 1)
                    dve.wait_ge(wo_hi_ready, n + 1)
                    nc.vector.tensor_tensor(wo_lo[b][:, :, :], wo[b][:, :, :], wo_hi[b][:, :, :].bitcast(F32), ALU.subtract).then_inc(wo_lo_ready, 1)
                for t in range(QT):
                    dve.wait_ge(y_done, QT * (NMC * e + NMC - 1) + t + 1)
                    wait_reuse(dve, y_added, QT * e)
                    nc.vector.scalar_tensor_tensor(x_sb[:, t, :], yp[t][:, :], combine[:, t, bass.ds(e, 1)], x_sb[:, t, :],
                                                   ALU.mult, ALU.add).then_inc(y_added, 1)

            split_in(0, 0)
            rolled(dve, NX, expert)


def perceiver_layer(nc, x, ctx_t, xw_in, xb_in, xb_cols, xw_out, xb_out, sw_in, sb_cols, sw_out, sb_out, w_gate,
                    w_in, b_in, w_out, b_out, out):
    q_scratch = nc.dram_tensor("q_scratch", [3 * D, H * NQ], F32, kind="Internal").ap()
    k_hi_dram = nc.dram_tensor("k_hi_scratch", [E, NK], F32, kind="Internal").ap()
    k_lo_dram = nc.dram_tensor("k_lo_scratch", [E, NK], F32, kind="Internal").ap()
    v_dram = nc.dram_tensor("v_scratch", [NK, E], F32, kind="Internal").ap()
    with ExitStack() as whole:
        x_sb = whole.enter_context(nc.sbuf_tensor("x_sb", [P, QT, E], F32))
        ident = whole.enter_context(nc.sbuf_tensor("ident", [P, P], F32))
        with ExitStack() as cross:
            q_stack = cross.enter_context(nc.sbuf_tensor("q_stack", [QROWS, H * NQ], F32R))
            q_top = cross.enter_context(nc.sbuf_tensor("q_top", [P, NG], F32))
            head_rows = cross.enter_context(nc.sbuf_tensor("head_rows", [P, HG], F32))
            bounded = cross.enter_context(nc.sbuf_tensor("bounded", [1, 1], I32))
            with ExitStack() as s:
                project_queries(nc, s, x, xw_in, xb_cols, x_sb, ident, q_stack, q_scratch, q_top, head_rows)
            with ExitStack() as s:
                stream_context(nc, s, ctx_t, xw_in, xb_in, xb_cols, k_hi_dram, k_lo_dram, v_dram, q_top,
                               head_rows, bounded)
            with ExitStack() as s:
                find_maxima(nc, s, k_hi_dram, k_lo_dram, q_scratch, ident, q_stack, bounded)
            o_acc = cross.enter_context(nc.sbuf_tensor("o_acc", [P, NG, NQ], F32))
            total_acc = cross.enter_context(nc.sbuf_tensor("total_acc", [P, NG, NQ], F32))
            p_sum = cross.enter_context(nc.sbuf_tensor("p_sum", [P, H * NQ], F32))
            with ExitStack() as s:
                attend(nc, s, k_hi_dram, k_lo_dram, v_dram, q_stack, o_acc, p_sum, total_acc)
            with ExitStack() as s:
                cross_output(nc, s, xw_out, xb_out, o_acc, p_sum, total_acc, x_sb)
        with ExitStack() as s:
            self_attention(nc, s, sw_in, sb_cols, sw_out, sb_out, ident, x_sb)
        with ExitStack() as s:
            feed_forward(nc, s, w_gate, w_in, b_in, w_out, b_out, ident, x_sb, out)


def kernel(**inputs):
    import numpy as np
    import concourse.bacc as bacc
    from concourse.bass_utils import run_bass_kernel_spmd

    a = {k: np.asarray(v) for k, v in inputs.items()}
    arrays = {
        "x": a["x"],
        "ctx_t": a["ctx_1024"][0].T,
        "xw_in": a["L0_xattn_in_proj_weight"].T,
        "xb_in": a["L0_xattn_in_proj_bias"],
        "xb_cols": a["L0_xattn_in_proj_bias"].reshape(3 * ET, P).T,
        "xw_out": a["L0_xattn_out_proj_weight"].T,
        "xb_out": a["L0_xattn_out_proj_bias"],
        "sw_in": a["L0_attn_in_proj_weight"].reshape(H, 3, D, E).transpose(3, 1, 0, 2).reshape(E, 3, E),
        "sb_cols": a["L0_attn_in_proj_bias"].reshape(H, 3, D).transpose(1, 0, 2).reshape(3 * ET, P).T,
        "sw_out": a["L0_attn_out_proj_weight"].T,
        "sb_out": a["L0_attn_out_proj_bias"],
        "w_gate": a["L0_ffn_W_gate"],
        "w_in": a["L0_ffn_W_in"].reshape(NX * E, M),
        "b_in": a["L0_ffn_b_in"].reshape(NX, M // P, P).transpose(2, 0, 1),
        "w_out": a["L0_ffn_W_out"].reshape(NX * M, E),
        "b_out": a["L0_ffn_b_out"],
    }
    arrays = {k: np.ascontiguousarray(v) for k, v in arrays.items()}
    nc = bacc.Bacc("TRN2", target_bir_lowering=False, num_devices=1)
    args = [nc.dram_tensor(k, v.shape, mybir.dt.from_np(v.dtype), kind="ExternalInput").ap() for k, v in arrays.items()]
    out = nc.dram_tensor("out", (1, NQ, E), F32, kind="ExternalOutput").ap()
    perceiver_layer(nc, *args, out)
    got = run_bass_kernel_spmd(nc, [arrays], core_ids=[0])
    return got.results[0]["out"]
```

```python
from contextlib import ExitStack

import concourse.bass as bass
from concourse import mybir

F32 = mybir.dt.float32
F32R = mybir.dt.float32r
U32 = mybir.dt.uint32
I32 = mybir.dt.int32
ACT = mybir.ActivationFunctionType
ALU = mybir.AluOpType
X = mybir.AxisListType.X

P = 128
NQ = 512
E = 512
NK = 8192
H = 16
D = E // H
ET = E // P
QT = NQ // P
HG = P // D
NG = H // HG
SCALE = float(D) ** -0.5
SAFE = 40.0
EPS = 1e-5
CH = 512
NCH = NK // CH
KT = CH // P
QROWS = 3 * D + 1
NX = 8
M = 2048
MC = 512
MT = MC // P
NMC = M // MC
SLOTS = 256


class Routing:
    pass


def rolled(eng, steps, body):
    body(0, False)
    with eng.Fori(1, steps - 1) as i:
        body(i, False)
    body(steps - 1, True)


def wait_reuse(eng, sem, count):
    if not isinstance(count, int) or count > 0:
        eng.wait_ge(sem, count)


def norm_scalar(nc, act, var, root, var_ready, root_ready):
    act.wait_ge(var_ready, 1)
    nc.scalar.activation(root[:, :], var[:, :], ACT.Sqrt).then_inc(root_ready, 1)


def norm_vector(nc, dve, x, xn, stats, mv, var, root, rstd, chain, var_ready, root_ready, ready):
    for t in range(QT):
        nc.vector.bn_stats(stats[:, t, :], x[:, t, :]).then_inc(chain, 1)
    dve.wait_ge(chain, QT)
    for t in range(QT):
        nc.vector.bn_aggr(mv[:, t, :], stats[:, t, :]).then_inc(chain, 1)
    dve.wait_ge(chain, 2 * QT)
    nc.vector.tensor_scalar(var[:, :], mv[:, :, 1], EPS, None, ALU.add).then_inc(var_ready, 1)
    dve.wait_ge(root_ready, 1)
    nc.vector.reciprocal(rstd[:, 0, :], root[:, :]).then_inc(chain, 1)
    dve.wait_ge(chain, 2 * QT + 1)
    nc.vector.tensor_tensor(rstd[:, 1, :], rstd[:, 0, :], rstd[:, 0, :], ALU.mult).then_inc(chain, 1)
    dve.wait_ge(chain, 2 * QT + 2)
    dve.wait_ge(var_ready, 1)
    nc.vector.tensor_tensor(rstd[:, 2, :], rstd[:, 1, :], var[:, :], ALU.mult).then_inc(chain, 1)
    dve.wait_ge(chain, 2 * QT + 3)
    nc.vector.tensor_scalar(rstd[:, 3, :], rstd[:, 2, :], -0.5, 1.5, ALU.mult, ALU.add).then_inc(chain, 1)
    dve.wait_ge(chain, 2 * QT + 4)
    nc.vector.tensor_tensor(rstd[:, 4, :], rstd[:, 3, :], rstd[:, 0, :], ALU.mult).then_inc(chain, 1)
    dve.wait_ge(chain, 2 * QT + 5)
    for t in range(QT):
        nc.vector.tensor_scalar(xn[:, t, :], x[:, t, :], mv[:, t, 0:1], rstd[:, 4, t:t + 1],
                                ALU.subtract, ALU.mult).then_inc(ready, 1)


def norm_transpose(nc, pe, xn, ident, banks, ready, turned):
    for t in range(QT):
        pe.wait_ge(ready, t + 1)
        for d in range(ET):
            last = nc.tensor.transpose(banks[d][:, t * P:(t + 1) * P], xn[:, t, d * P:(d + 1) * P],
                                       ident[:, :])
    last.then_inc(turned, 1)


def make_identity(nc, pool, ident, zeroed, made):
    nc.gpsimd.memset(ident[:, :], 0.0).then_inc(zeroed, 1)
    pool.wait_ge(zeroed, 1)
    nc.gpsimd.affine_select(out=ident[:, :], in_=ident[:, :], compare_op=ALU.not_equal, fill=1.0,
                            base=0, pattern=[[-1, P]], channel_multiplier=1).then_inc(made, 1)


def project_queries(nc, ctx, x_dram, w_in, b_cols, x_sb, ident, q_stack, q_scratch, q_top, head_rows):
    sb = lambda n, s, d=F32: ctx.enter_context(nc.sbuf_tensor(n, s, d))
    sem = lambda n: ctx.enter_context(nc.semaphore(n))
    wq = sb("pq_wq", [P, ET, E])
    bq = sb("pq_bq", [P, NG])
    xn = sb("pq_xn", [P, QT, E])
    xt = sb("pq_xt", [P, ET, NQ])
    q_hi = sb("pq_q_hi", [P, NG, NQ], F32R)
    q_lo = sb("pq_q_lo", [P, NG, NQ], F32R)
    stats = sb("pq_stats", [P, QT, 6])
    mv = sb("pq_mv", [P, QT, 2])
    var = sb("pq_var", [P, QT])
    root = sb("pq_root", [P, QT])
    rstd = sb("pq_rstd", [P, 5, QT])
    var_ready, root_ready = map(sem, ("pq_var_ready", "pq_root_ready"))
    turn = [ctx.enter_context(nc.psum_tensor(f"pq_turn{d}", [P, NQ], F32)) for d in range(ET)]
    proj = [ctx.enter_context(nc.psum_tensor(f"pq_proj{g}", [P, NQ], F32)) for g in range(NG)]
    x_in, w_loaded, chain, normed, turned, xt_ready = map(sem, (
        "pq_x_in", "pq_w_loaded", "pq_chain", "pq_normed", "pq_turned", "pq_xt_ready"))
    projected, hi_ready, lo_ready, stacked, zeroed, ident_made = map(sem, (
        "pq_projected", "pq_hi_ready", "pq_lo_ready", "pq_stacked", "pq_zeroed", "pq_ident_made"))

    with nc.Block() as block:
        @block.sync
        def _(sp):
            sp.dma_start(x_sb[:, :, :], x_dram.rearrange("a (t p) e -> p (a t) e", p=P)).then_inc(x_in, 16)
            sp.dma_start(wq[:, :, :], w_in[:, 0:E].rearrange("(t p) f -> p t f", p=P)).then_inc(w_loaded, 16)
            sp.dma_start(bq[:, :], b_cols[:, 0:NG]).then_inc(w_loaded, 16)
            sp.wait_ge(lo_ready, NG)
            for j in range(HG):
                rows = slice(j * D, (j + 1) * D)
                for part, src in enumerate((q_hi, q_hi, q_lo)):
                    dst = q_stack[part * D:(part + 1) * D, :].bitcast(F32).rearrange("d (g j q) -> d g j q", j=HG, q=NQ)
                    sp.dma_start(dst[:, :, j, :], src[rows, :, :].bitcast(F32)).then_inc(stacked, 16)
            sp.wait_ge(stacked, 16 * 3 * HG)
            sp.dma_start(q_scratch, q_stack[0:3 * D, :].bitcast(F32)).then_inc(stacked, 16)
            sp.wait_ge(stacked, 16 * (3 * HG + 1))

        @block.gpsimd
        def _(pool):
            make_identity(nc, pool, ident, zeroed, ident_made)
            nc.gpsimd.memset(head_rows[:, :], 1.0).then_inc(zeroed, 1)
            pool.wait_ge(zeroed, 2)
            nc.gpsimd.affine_select(out=head_rows[:, :], in_=head_rows[:, :], compare_op=ALU.is_ge, fill=0.0,
                                    base=0, pattern=[[-D, HG]], channel_multiplier=1).then_inc(zeroed, 1)
            pool.wait_ge(zeroed, 3)
            nc.gpsimd.affine_select(out=head_rows[:, :], in_=head_rows[:, :], compare_op=ALU.is_ge, fill=0.0,
                                    base=D - 1, pattern=[[D, HG]], channel_multiplier=-1).then_inc(zeroed, 1)
            pool.wait_ge(zeroed, 4)
            nc.gpsimd.memset(q_stack[3 * D:QROWS, :].bitcast(F32), 0.0).then_inc(zeroed, 1)

        @block.vector
        def _(dve):
            dve.wait_ge(x_in, 16)
            norm_vector(nc, dve, x_sb, xn, stats, mv, var, root, rstd, chain, var_ready, root_ready, normed)
            for g in range(NG):
                dve.wait_ge(hi_ready, g + 1)
                nc.vector.scalar_tensor_tensor(q_lo[:, g, :], proj[g][:, :], bq[:, g:g + 1], q_hi[:, g, :].bitcast(F32),
                                               ALU.add, ALU.subtract).then_inc(lo_ready, 1)
            nc.vector.tensor_reduce(q_top[:, :], q_hi[:, :, :].bitcast(F32), X, ALU.max,
                                    apply_absolute_value=True).then_inc(chain, 1)

        @block.tensor
        def _(pe):
            pe.wait_ge(ident_made, 1)
            norm_transpose(nc, pe, xn, ident, turn, normed, turned)
            pe.wait_ge(w_loaded, 32)
            pe.wait_ge(xt_ready, ET)
            for g in range(NG):
                for d in range(ET):
                    last = nc.tensor.matmul(proj[g][:, :], wq[:, d, g * P:(g + 1) * P], xt[:, d, :],
                                            start=(d == 0), stop=(d == ET - 1))
                last.then_inc(projected, 1)

        @block.scalar
        def _(act):
            norm_scalar(nc, act, var, root, var_ready, root_ready)
            act.wait_ge(turned, 1)
            for d in range(ET):
                nc.scalar.activation(xt[:, d, :], turn[d][:, :], ACT.Copy).then_inc(xt_ready, 1)
            act.wait_ge(w_loaded, 32)
            for g in range(NG):
                act.wait_ge(projected, g + 1)
                nc.scalar.activation(q_hi[:, g, :], proj[g][:, :], ACT.Identity,
                                     bias=bq[:, g:g + 1]).then_inc(hi_ready, 1)


def stream_context(nc, ctx, c_dram, w_in, b_in, b_cols, k_hi_dram, k_lo_dram, v_dram, q_top, head_rows, bounded):
    sb = lambda n, s, d=F32: ctx.enter_context(nc.sbuf_tensor(n, s, d))
    sem = lambda n: ctx.enter_context(nc.semaphore(n))
    w = sb("sc_w", [P, ET, 2 * E])
    w_hi = sb("sc_w_hi", [P, ET, 2 * E], F32R)
    w_lo = sb("sc_w_lo", [P, ET, 2 * E], F32R)
    bk = sb("sc_bk", [P, NG])
    bv = sb("sc_bv", [P, E])
    c = [sb(f"sc_c{b}", [P, ET, CH]) for b in range(2)]
    c_hi = [sb(f"sc_c_hi{b}", [P, ET, CH], F32R) for b in range(2)]
    c_lo = [sb(f"sc_c_lo{b}", [P, ET, CH], F32R) for b in range(2)]
    k_hi = [sb(f"sc_k_hi{b}", [P, NG, CH], F32R) for b in range(2)]
    k_lo = [sb(f"sc_k_lo{b}", [P, NG, CH], F32R) for b in range(2)]
    v = [sb(f"sc_v{b}", [P, KT, E]) for b in range(2)]
    kp = [ctx.enter_context(nc.psum_tensor(f"sc_kp{g}", [P, CH], F32)) for g in range(NG)]
    vp = [ctx.enter_context(nc.psum_tensor(f"sc_vp{t}", [P, E], F32)) for t in range(KT)]
    k_top = [sb(f"sc_k_top{b}", [P, NG]) for b in range(2)]
    k_top_all = sb("sc_k_top_all", [P, NG])
    product = sb("sc_product", [P, NG])
    bound = sb("sc_bound", [1, 1])
    k_topped, k_top_kept, product_ready, bound_done, bound_ready, flagged = map(sem, (
        "sc_k_topped", "sc_k_top_kept", "sc_product_ready", "sc_bound_done", "sc_bound_ready", "sc_flagged"))
    w_loaded, w_hi_ready, w_lo_ready = map(sem, ("sc_w_loaded", "sc_w_hi_ready", "sc_w_lo_ready"))
    c_loaded = [sem(f"sc_c_loaded{b}") for b in range(2)]
    c_hi_ready, c_lo_ready = map(sem, ("sc_c_hi_ready", "sc_c_lo_ready"))
    k_done, v_done = map(sem, ("sc_k_done", "sc_v_done"))
    k_hi_ready, k_lo_ready, v_ready = map(sem, ("sc_k_hi_ready", "sc_k_lo_ready", "sc_v_ready"))
    stored = [sem(f"sc_stored{b}") for b in range(2)]
    PAIRS, STORES = NCH // 2, 3 * 16
    c_view = c_dram.rearrange("(t p) n -> p t n", p=P)
    k_hi_view = k_hi_dram.rearrange("(g p) n -> p g n", p=P)
    k_lo_view = k_lo_dram.rearrange("(g p) n -> p g n", p=P)

    with nc.Block() as block:
        @block.sync
        def _(sp):
            sp.dma_start(w[:, :, :], w_in[:, E:3 * E].rearrange("(t p) f -> p t f", p=P)).then_inc(w_loaded, 16)
            sp.dma_start(bk[:, :], b_cols[:, NG:2 * NG]).then_inc(w_loaded, 16)
            sp.dma_start(bv[:, :], b_in[2 * E:3 * E].partition_broadcast(P)).then_inc(w_loaded, 16)
            for b in range(2):
                sp.dma_start(c[b][:, :, :], c_view[:, :, b * CH:(b + 1) * CH]).then_inc(c_loaded[b], 16)

            def pair(i, last):
                for b in range(2):
                    n = 2 * i + b
                    if not last:
                        sp.wait_ge(c_lo_ready, n + 1)
                        sp.dma_start(c[b][:, :, :], c_view[:, :, bass.ds((n + 2) * CH, CH)]).then_inc(c_loaded[b], 16)
                    cols = bass.ds(n * CH, CH)
                    sp.wait_ge(k_lo_ready, NG * (n + 1))
                    sp.dma_start(k_hi_view[:, :, cols], k_hi[b][:, :, :].bitcast(F32)).then_inc(stored[b], 16)
                    sp.dma_start(k_lo_view[:, :, cols], k_lo[b][:, :, :].bitcast(F32)).then_inc(stored[b], 16)
                    sp.wait_ge(v_ready, KT * (n + 1))
                    sp.dma_start(v_dram[cols, :].rearrange("(t p) f -> p t f", p=P), v[b][:, :, :]).then_inc(stored[b], 16)

            rolled(sp, PAIRS, pair)
            for b in range(2):
                sp.wait_ge(stored[b], STORES * PAIRS)

        @block.vector
        def _(dve):
            for d in range(ET):
                dve.wait_ge(w_hi_ready, d + 1)
                nc.vector.tensor_tensor(w_lo[:, d, :], w[:, d, :], w_hi[:, d, :].bitcast(F32),
                                        ALU.subtract).then_inc(w_lo_ready, 1)
            dve.wait_ge(w_loaded, 48)

            def split(n, b):
                dve.wait_ge(c_hi_ready, n + 1)
                nc.vector.tensor_tensor(c_lo[b][:, :, :], c[b][:, :, :], c_hi[b][:, :, :].bitcast(F32),
                                        ALU.subtract).then_inc(c_lo_ready, 1)

            def pair(i, last):
                for b in range(2):
                    n = 2 * i + b
                    if not (last and b == 1):
                        split(n + 1, 1 - b)
                    for g in range(NG):
                        dve.wait_ge(k_hi_ready, NG * n + g + 1)
                        nc.vector.scalar_tensor_tensor(k_lo[b][:, g, :], kp[g][:, :], bk[:, g:g + 1],
                                                       k_hi[b][:, g, :].bitcast(F32), ALU.add,
                                                       ALU.subtract).then_inc(k_lo_ready, 1)
                    nc.vector.tensor_reduce(k_top[b][:, :], k_hi[b][:, :, :].bitcast(F32), X, ALU.max,
                                            apply_absolute_value=True).then_inc(k_topped, 1)
                    wait_reuse(dve, stored[b], STORES * i)
                    for t in range(KT):
                        dve.wait_ge(v_done, KT * n + t + 1)
                        nc.vector.tensor_tensor(v[b][:, t, :], vp[t][:, :], bv[:, :], ALU.add).then_inc(v_ready, 1)
                    dve.wait_ge(k_topped, n + 1)
                    dve.wait_ge(k_top_kept, n + 1)
                    nc.vector.tensor_tensor(k_top_all[:, :], k_top_all[:, :], k_top[b][:, :], ALU.max).then_inc(k_top_kept, 1)

            nc.vector.memset(k_top_all[:, :], 0.0).then_inc(k_top_kept, 1)
            split(0, 0)
            rolled(dve, PAIRS, pair)
            dve.wait_ge(k_top_kept, NCH + 1)
            nc.vector.tensor_tensor(product[:, :], q_top[:, :], k_top_all[:, :], ALU.mult).then_inc(product_ready, 1)
            dve.wait_ge(bound_done, 1)
            nc.vector.reduce_max(bound[:, :], kp[0][0:1, 0:H], X).then_inc(bound_ready, 1)
            dve.wait_ge(bound_ready, 1)
            nc.vector.tensor_scalar(bounded[:, :], bound[:, :], SAFE / SCALE, None, ALU.is_le).then_inc(flagged, 1)

        @block.tensor
        def _(pe):
            pe.wait_ge(w_lo_ready, ET)
            def pair(i, last):
                for b in range(2):
                    n = 2 * i + b
                    pe.wait_ge(c_lo_ready, n + 1)
                    wait_reuse(pe, k_lo_ready, NG * n)
                    for g in range(NG):
                        for a, (lhs, rhs) in enumerate(((w_hi, c_hi), (w_lo, c_hi), (w_hi, c_lo))):
                            for d in range(ET):
                                last = nc.tensor.matmul(kp[g][:, :], lhs[:, d, g * P:(g + 1) * P], rhs[b][:, d, :],
                                                        start=(a == 0 and d == 0), stop=(a == 2 and d == ET - 1))
                        last.then_inc(k_done, 1)
                    wait_reuse(pe, v_ready, KT * n)
                    for t in range(KT):
                        for a, (lhs, rhs) in enumerate(((c_hi, w_hi), (c_lo, w_hi), (c_hi, w_lo))):
                            for d in range(ET):
                                last = nc.tensor.matmul(vp[t][:, :], lhs[b][:, d, t * P:(t + 1) * P], rhs[:, d, E:2 * E],
                                                        start=(a == 0 and d == 0), stop=(a == 2 and d == ET - 1))
                        last.then_inc(v_done, 1)

            rolled(pe, PAIRS, pair)
            pe.wait_ge(product_ready, 1)
            for g in range(NG):
                last = nc.tensor.matmul(kp[0][0:1, g * HG:(g + 1) * HG], product[:, g:g + 1], head_rows[:, :],
                                        start=True, stop=True)
            last.then_inc(bound_done, 1)

        @block.scalar
        def _(act):
            act.wait_ge(w_loaded, 48)
            for d in range(ET):
                nc.scalar.activation(w_hi[:, d, :], w[:, d, :], ACT.Copy).then_inc(w_hi_ready, 1)

            def split(n, i, b):
                act.wait_ge(c_loaded[b], 16 * (i + 1))
                nc.scalar.activation(c_hi[b][:, :, :], c[b][:, :, :], ACT.Copy).then_inc(c_hi_ready, 1)

            def pair(i, last):
                for b in range(2):
                    n = 2 * i + b
                    if not (last and b == 1):
                        wait_reuse(act, v_done, KT * n)
                        split(n + 1, i + b, 1 - b)
                    wait_reuse(act, k_topped, n - 1)
                    wait_reuse(act, stored[b], STORES * i)
                    for g in range(NG):
                        act.wait_ge(k_done, NG * n + g + 1)
                        nc.scalar.activation(k_hi[b][:, g, :], kp[g][:, :], ACT.Identity,
                                             bias=bk[:, g:g + 1]).then_inc(k_hi_ready, 1)

            split(0, 0, 0)
            rolled(act, PAIRS, pair)


def find_maxima(nc, ctx, k_hi_dram, k_lo_dram, q_scratch, ident, q_stack, bounded):
    sb = lambda n, s, d=F32: ctx.enter_context(nc.sbuf_tensor(n, s, d))
    sem = lambda n: ctx.enter_context(nc.semaphore(n))
    KB = 2048
    NKB = NK // KB
    UNITS = NKB * QT
    q = [sb(f"fm_q{b}", [3 * D, NQ], F32R) for b in range(2)]
    k = [sb(f"fm_k{b}", [3 * D, NK], F32R) for b in range(2)]
    block_max = [sb(f"fm_block_max{b}", [P, QT, NKB]) for b in range(2)]
    head_max = [sb(f"fm_head_max{b}", [P, QT]) for b in range(2)]
    minus_max = sb("fm_minus_max", [P, H * QT])
    minus_row = sb("fm_minus_row", [H * QT, P], F32R)
    s = [ctx.enter_context(nc.psum_tensor(f"fm_s{r}", [P, KB], F32)) for r in range(2)]
    loaded = [sem(f"fm_loaded{b}") for b in range(2)]
    head_reduced = [sem(f"fm_head_reduced{b}") for b in range(2)]
    scored = [sem(f"fm_scored{r}") for r in range(2)]
    reduced = [sem(f"fm_reduced{r}") for r in range(2)]
    negated, turned, row_ready, placed = map(sem, (
        "fm_negated", "fm_turned", "fm_row_ready", "fm_placed"))
    LOADS = 4 * 16
    PER = UNITS // 2

    with nc.Block() as block:
        @block.sync
        def _(sp):
            flag = sp.value_load(bounded[:, :], min_val=0, max_val=1)
            with sp.If(flag < 1):
                def pair(i, last):
                    for b in range(2):
                        h = 2 * i + b
                        rows = bass.ds(h * D, D)
                        wait_reuse(sp, head_reduced[b], i)
                        sp.dma_start(q[b][:, :].bitcast(F32), q_scratch[:, bass.ds(h * NQ, NQ)]).then_inc(loaded[b], 16)
                        sp.dma_start(k[b][0:D, :].bitcast(F32), k_hi_dram[rows, :]).then_inc(loaded[b], 16)
                        sp.dma_start(k[b][D:2 * D, :].bitcast(F32), k_lo_dram[rows, :]).then_inc(loaded[b], 16)
                        sp.dma_start(k[b][2 * D:3 * D, :].bitcast(F32), k_hi_dram[rows, :]).then_inc(loaded[b], 16)
                rolled(sp, H // 2, pair)
                sp.wait_ge(row_ready, 1)
                sp.dma_start(q_stack[3 * D:QROWS, :].bitcast(F32), minus_row[:, :].bitcast(F32)).then_inc(placed, 16)
                sp.wait_ge(placed, 16)

        @block.tensor
        def _(pe):
            flag = pe.value_load(bounded[:, :], min_val=0, max_val=1)
            with pe.If(flag < 1):
                def pair(i, last):
                    for b in range(2):
                        h = 2 * i + b
                        pe.wait_ge(loaded[b], LOADS * (i + 1))
                        for u in range(UNITS):
                            kb, qt, r = u // QT, u % QT, u % 2
                            wait_reuse(pe, reduced[r], PER * h + u // 2)
                            for n in range(KB // 512):
                                cols = slice(kb * KB + n * 512, kb * KB + (n + 1) * 512)
                                last = nc.tensor.matmul(s[r][:, n * 512:(n + 1) * 512], q[b][:, qt * P:(qt + 1) * P],
                                                        k[b][:, cols], start=True, stop=True)
                            last.then_inc(scored[r], 1)
                rolled(pe, H // 2, pair)
                pe.wait_ge(negated, H)
                nc.tensor.transpose(s[0][0:H * QT, 0:P], minus_max[:, :], ident[:, :]).then_inc(turned, 1)

        @block.vector
        def _(dve):
            flag = dve.value_load(bounded[:, :], min_val=0, max_val=1)
            with dve.If(flag < 1):
                with dve.Fori(0, H // 2) as i:
                    for b in range(2):
                        h = 2 * i + b
                        for u in range(UNITS):
                            kb, qt, r = u // QT, u % QT, u % 2
                            dve.wait_ge(scored[r], PER * h + u // 2 + 1)
                            nc.vector.reduce_max(block_max[b][:, qt, kb:kb + 1], s[r][:, :], X).then_inc(reduced[r], 1)
                        for r in range(2):
                            dve.wait_ge(reduced[r], PER * (h + 1))
                        nc.vector.reduce_max(head_max[b][:, :], block_max[b][:, :, :], X).then_inc(head_reduced[b], 1)
                        dve.wait_ge(head_reduced[b], i + 1)
                        nc.vector.tensor_scalar(minus_max[:, bass.ds(h * QT, QT)], head_max[b][:, :], -1.0, None,
                                                ALU.mult).then_inc(negated, 1)

        @block.scalar
        def _(act):
            flag = act.value_load(bounded[:, :], min_val=0, max_val=1)
            with act.If(flag < 1):
                act.wait_ge(turned, 1)
                nc.scalar.activation(minus_row[:, :], s[0][0:H * QT, 0:P], ACT.Copy).then_inc(row_ready, 1)


def attend(nc, ctx, k_hi_dram, k_lo_dram, v_dram, q_stack, o_acc, p_sum, total_acc):
    sb = lambda n, s, d=F32: ctx.enter_context(nc.sbuf_tensor(n, s, d))
    sem = lambda n: ctx.enter_context(nc.semaphore(n))
    CB = 4
    TILES = CB * KT
    ITERS = NG * NCH // CB
    PER_GROUP = NCH // CB
    BY_PE = (4, 9, 15)
    SR, PR = 3, 4
    AHEAD = 3
    TPR = TILES // PR
    LOADS = 4 * 16
    k = [sb(f"at_k{c}", [QROWS, HG, CH], F32R) for c in range(CB)]
    v = [sb(f"at_v{c}", [P, KT, P]) for c in range(CB)]
    p = [sb(f"at_p{r}", [P, HG * NQ]) for r in range(PR)]
    s = [ctx.enter_context(nc.psum_tensor(f"at_s{r}", [P, 2 * NQ], F32)) for r in range(SR)]
    o = ctx.enter_context(nc.psum_tensor("at_o", [P, NQ], F32))
    totals = ctx.enter_context(nc.psum_tensor("at_totals", [P, NQ], F32))
    ones = sb("at_ones", [P, D])
    ones_set, zeroed = map(sem, ("at_ones_set", "at_zeroed"))
    loaded = [sem(f"at_loaded{c}") for c in range(CB)]
    s_ready = [sem(f"at_s_ready{r}") for r in range(SR)]
    p_ready = [sem(f"at_p_ready{r}") for r in range(PR)]
    p_used = [sem(f"at_p_used{r}") for r in range(PR)]
    p_summed = [sem(f"at_p_summed{r}") for r in range(PR)]
    o_added, totals_added = map(sem, ("at_o_added", "at_totals_added"))
    s_uses = [len(range(r, 2 * TILES, SR)) for r in range(SR)]
    s_last = [max(range(r, 2 * TILES, SR)) for r in range(SR)]

    def exped(it, u):
        return 2 * TPR * it + 2 * (u // 2 // PR) + u % 2 + 1

    def used(it, t):
        return TPR * it + t // PR + 1

    def summed(it, t):
        mine = [w for w in range(t % PR, TILES, PR) if w not in BY_PE]
        return len(mine) * it + (sum(w <= t for w in mine) if t >= 0 else -sum(w > t + TILES for w in mine))

    with nc.Block() as block:
        @block.gpsimd
        def _(pool):
            nc.gpsimd.memset(ones[:, :], 1.0).then_inc(ones_set, 1)
            for c in range(CB):
                pool.wait_ge(ones_set, c + 1)
                nc.gpsimd.memset(k[c][3 * D:QROWS, :, :].bitcast(F32), 1.0).then_inc(ones_set, 1)
            pool.wait_ge(ones_set, CB + 1)
            nc.gpsimd.memset(p_sum[:, :], 0.0).then_inc(zeroed, 1)
            pool.wait_ge(zeroed, 1)
            nc.gpsimd.memset(o_acc[:, :, :], 0.0).then_inc(zeroed, 1)
            pool.wait_ge(zeroed, 2)
            nc.gpsimd.memset(total_acc[:, :, :], 0.0).then_inc(zeroed, 1)

        @block.sync
        def _(sp):
            def iteration(it, last):
                g, kb = it // PER_GROUP, it % PER_GROUP
                for c in range(CB):
                    keys = bass.ds((kb * CB + c) * CH, CH)
                    end = (c + 1) * KT - 1
                    wait_reuse(sp, p_used[end % PR], used(it, end) - TPR)
                    hi = k_hi_dram[bass.ds(g * P, P), keys].rearrange("(j d) n -> d j n", d=D)
                    lo = k_lo_dram[bass.ds(g * P, P), keys].rearrange("(j d) n -> d j n", d=D)
                    for part, src in enumerate((hi, lo, hi)):
                        sp.dma_start(k[c][part * D:(part + 1) * D, :, :].bitcast(F32), src).then_inc(loaded[c], 16)
                    sp.dma_start(v[c][:, :, :], v_dram[keys, bass.ds(g * P, P)].rearrange("(t p) f -> p t f", p=P)).then_inc(loaded[c], 16)

            rolled(sp, ITERS, iteration)

        @block.tensor
        def _(pe):
            def scores(it, u):
                c, t, pair, r = u // 2 // KT, u // 2 % KT, u % 2, u % SR
                if t == 0 and pair == 0:
                    pe.wait_ge(loaded[c], LOADS * (it + 1))
                if u >= SR:
                    pe.wait_ge(p_ready[(u - SR) // 2 % PR], exped(it, u - SR))
                else:
                    wait_reuse(pe, p_ready[s_last[r] // 2 % PR], exped(it, s_last[r]) - 2 * TPR)
                for a in range(2):
                    j = 2 * pair + a
                    last = nc.tensor.matmul(s[r][:, a * NQ:(a + 1) * NQ], k[c][:, j, t * P:(t + 1) * P],
                                            q_stack[:, bass.ds(it // PER_GROUP * (HG * NQ) + j * NQ, NQ)],
                                            start=True, stop=True)
                last.then_inc(s_ready[r], 1)

            def outputs(it, t):
                c, r = t // KT, t % PR
                if t == 0:
                    wait_reuse(pe, o_added, it)
                if t == BY_PE[0]:
                    wait_reuse(pe, totals_added, it)
                pe.wait_ge(p_ready[r], exped(it, 2 * t + 1))
                for j in range(HG):
                    last = nc.tensor.matmul(o[j * D:(j + 1) * D, :], v[c][:, t % KT, j * D:(j + 1) * D],
                                            p[r][:, j * NQ:(j + 1) * NQ], start=(t == 0), stop=(t == TILES - 1))
                if t in BY_PE:
                    for j in range(HG):
                        last = nc.tensor.matmul(totals[j * D:(j + 1) * D, :], ones[:, :], p[r][:, j * NQ:(j + 1) * NQ],
                                                start=(t == BY_PE[0]), stop=(t == BY_PE[-1]))
                last.then_inc(p_used[r], 1)

            def iteration(it, last):
                for t in range(TILES):
                    for u in (2 * t + AHEAD, 2 * t + AHEAD + 1):
                        if u < 2 * TILES:
                            scores(it, u)
                        elif not last:
                            scores(it + 1, u - 2 * TILES)
                    outputs(it, t)

            pe.wait_ge(ones_set, CB + 1)
            for u in range(AHEAD):
                scores(0, u)
            rolled(pe, ITERS, iteration)

        @block.scalar
        def _(act):
            def iteration(it, last):
                for u in range(2 * TILES):
                    t, pair = u // 2, u % 2
                    if pair == 0:
                        wait_reuse(act, p_used[t % PR], used(it, t) - 1)
                        wait_reuse(act, p_summed[t % PR], summed(it, t - PR))
                    act.wait_ge(s_ready[u % SR], s_uses[u % SR] * it + u // SR + 1)
                    nc.scalar.activation(p[t % PR][:, pair * 2 * NQ:(pair + 1) * 2 * NQ], s[u % SR][:, :], ACT.Exp,
                                         scale=SCALE).then_inc(p_ready[t % PR], 1)

            rolled(act, ITERS, iteration)

        @block.vector
        def _(dve):
            dve.wait_ge(zeroed, 3)

            def iteration(it, last):
                g = it // PER_GROUP
                sums = p_sum[:, bass.ds(g * (HG * NQ), HG * NQ)]
                for t in range(TILES):
                    if t in BY_PE:
                        continue
                    before = max(w for w in range(-TILES, t) if w % TILES not in BY_PE)
                    wait_reuse(dve, p_summed[before % PR], summed(it, before))
                    dve.wait_ge(p_ready[t % PR], exped(it, 2 * t + 1))
                    nc.vector.tensor_tensor(sums, sums, p[t % PR][:, :], ALU.add).then_inc(p_summed[t % PR], 1)
                dve.wait_ge(p_used[(TILES - 1) % PR], used(it, TILES - 1))
                for bank, acc, added in ((o, o_acc, o_added), (totals, total_acc, totals_added)):
                    wait_reuse(dve, added, it)
                    nc.vector.tensor_tensor(acc[:, bass.ds(g, 1), :], acc[:, bass.ds(g, 1), :],
                                            bank[:, :].rearrange("p (a q) -> p a q", a=1), ALU.add).then_inc(added, 1)

            rolled(dve, ITERS, iteration)


def cross_output(nc, ctx, w_out, b_out, o_acc, p_sum, total_acc, x_sb):
    sb = lambda n, s, d=F32: ctx.enter_context(nc.sbuf_tensor(n, s, d))
    sem = lambda n: ctx.enter_context(nc.semaphore(n))
    wo = sb("co_wo", [P, ET, E])
    bo = sb("co_bo", [P, E])
    ones = sb("co_ones", [P, D])
    rec = sb("co_rec", [P, NG, NQ])
    heads = sb("co_heads", [P, NG, NQ])
    total = [ctx.enter_context(nc.psum_tensor(f"co_total{g}", [P, NQ], F32)) for g in range(NG)]
    out = [ctx.enter_context(nc.psum_tensor(f"co_out{t}", [P, E], F32)) for t in range(QT)]
    loaded, ones_set, totalled, summed, inverted, normed, biased, projected, added = map(sem, (
        "co_loaded", "co_ones_set", "co_totalled", "co_summed", "co_inverted", "co_normed", "co_biased", "co_projected", "co_added"))

    with nc.Block() as block:
        @block.sync
        def _(sp):
            sp.dma_start(wo[:, :, :], w_out.rearrange("(t p) f -> p t f", p=P)).then_inc(loaded, 16)
            sp.dma_start(bo[:, :], b_out.partition_broadcast(P)).then_inc(loaded, 16)

        @block.gpsimd
        def _(pool):
            nc.gpsimd.memset(ones[:, :], 1.0).then_inc(ones_set, 1)

        @block.tensor
        def _(pe):
            pe.wait_ge(ones_set, 1)
            for g in range(NG):
                for j in range(HG):
                    h = g * HG + j
                    last = nc.tensor.matmul(total[g][j * D:(j + 1) * D, :], ones[:, :], p_sum[:, h * NQ:(h + 1) * NQ],
                                            start=True, stop=True)
                last.then_inc(totalled, 1)
            pe.wait_ge(loaded, 32)
            for g in range(NG):
                pe.wait_ge(normed, g + 1)
                for t in range(QT):
                    last = nc.tensor.matmul(out[t][:, :], heads[:, g, t * P:(t + 1) * P], wo[:, g, :],
                                            start=(g == 0), stop=(g == NG - 1))
            last.then_inc(projected, 1)

        @block.vector
        def _(dve):
            for g in range(NG):
                dve.wait_ge(totalled, g + 1)
                nc.vector.tensor_tensor(total_acc[:, g, :], total_acc[:, g, :], total[g][:, :], ALU.add).then_inc(summed, 1)
                dve.wait_ge(summed, g + 1)
                nc.vector.reciprocal(rec[:, g, :], total_acc[:, g, :]).then_inc(inverted, 1)
                dve.wait_ge(inverted, g + 1)
                nc.vector.tensor_tensor(heads[:, g, :], o_acc[:, g, :], rec[:, g, :], ALU.mult).then_inc(normed, 1)
            dve.wait_ge(loaded, 32)
            for t in range(QT):
                nc.vector.tensor_tensor(x_sb[:, t, :], x_sb[:, t, :], bo[:, :], ALU.add).then_inc(biased, 1)
            dve.wait_ge(projected, 1)
            for t in range(QT):
                dve.wait_ge(biased, t + 1)
                nc.vector.tensor_tensor(x_sb[:, t, :], x_sb[:, t, :], out[t][:, :], ALU.add).then_inc(added, 1)


def self_attention(nc, ctx, w_in, b_cols, w_out, b_out, ident, x_sb):
    sb = lambda n, s, d=F32: ctx.enter_context(nc.sbuf_tensor(n, s, d))
    sem = lambda n: ctx.enter_context(nc.semaphore(n))
    wv = sb("sa_wv", [P, ET, E])
    wo = sb("sa_wo", [P, ET, E])
    bv = sb("sa_bv", [P, ET])
    bo = sb("sa_bo", [P, E])
    xn = sb("sa_xn", [P, QT, E])
    xt = sb("sa_xt", [P, ET, NQ])
    vt = sb("sa_vt", [P, ET, NQ])
    stats = sb("sa_stats", [P, QT, 6])
    mv = sb("sa_mv", [P, QT, 2])
    var = sb("sa_var", [P, QT])
    root = sb("sa_root", [P, QT])
    rstd = sb("sa_rstd", [P, 5, QT])
    var_ready, root_ready = map(sem, ("sa_var_ready", "sa_root_ready"))
    turn = [ctx.enter_context(nc.psum_tensor(f"sa_turn{d}", [P, NQ], F32)) for d in range(ET)]
    proj = [ctx.enter_context(nc.psum_tensor(f"sa_proj{d}", [P, NQ], F32)) for d in range(ET)]
    loaded, chain, normed, turned, xt_ready, v_done, v_ready, biased, projected, added = map(sem, (
        "sa_loaded", "sa_chain", "sa_normed", "sa_turned", "sa_xt_ready", "sa_v_done", "sa_v_ready",
        "sa_biased", "sa_projected", "sa_added"))

    with nc.Block() as block:
        @block.sync
        def _(sp):
            sp.dma_start(wv[:, :, :], w_in[:, 2, :].rearrange("(t p) f -> p t f", p=P)).then_inc(loaded, 16)
            sp.dma_start(bv[:, :], b_cols[:, 2 * ET:3 * ET]).then_inc(loaded, 16)
            sp.dma_start(wo[:, :, :], w_out.rearrange("(t p) f -> p t f", p=P)).then_inc(loaded, 16)
            sp.dma_start(bo[:, :], b_out.partition_broadcast(P)).then_inc(loaded, 16)

        @block.tensor
        def _(pe):
            norm_transpose(nc, pe, xn, ident, turn, normed, turned)
            pe.wait_ge(loaded, 64)
            pe.wait_ge(xt_ready, ET)
            for f in range(ET):
                for d in range(ET):
                    last = nc.tensor.matmul(proj[f][:, :], wv[:, d, f * P:(f + 1) * P], xt[:, d, :],
                                            start=(d == 0), stop=(d == ET - 1))
                last.then_inc(v_done, 1)
            for f in range(ET):
                pe.wait_ge(v_ready, f + 1)
                for t in range(QT):
                    last = nc.tensor.matmul(turn[t][:, :], vt[:, f, t * P:(t + 1) * P], wo[:, f, :],
                                            start=(f == 0), stop=(f == ET - 1))
            last.then_inc(projected, 1)

        @block.scalar
        def _(act):
            norm_scalar(nc, act, var, root, var_ready, root_ready)
            act.wait_ge(turned, 1)
            for d in range(ET):
                nc.scalar.activation(xt[:, d, :], turn[d][:, :], ACT.Copy).then_inc(xt_ready, 1)
            act.wait_ge(loaded, 64)
            for f in range(ET):
                act.wait_ge(v_done, f + 1)
                nc.scalar.activation(vt[:, f, :], proj[f][:, :], ACT.Identity, bias=bv[:, f:f + 1]).then_inc(v_ready, 1)

        @block.vector
        def _(dve):
            norm_vector(nc, dve, x_sb, xn, stats, mv, var, root, rstd, chain, var_ready, root_ready, normed)
            dve.wait_ge(loaded, 64)
            for t in range(QT):
                dve.wait_ge(normed, t + 1)
                nc.vector.tensor_tensor(x_sb[:, t, :], x_sb[:, t, :], bo[:, :], ALU.add).then_inc(biased, 1)
            dve.wait_ge(projected, 1)
            for t in range(QT):
                dve.wait_ge(biased, t + 1)
                nc.vector.tensor_tensor(x_sb[:, t, :], x_sb[:, t, :], turn[t][:, :], ALU.add).then_inc(added, 1)


def route(nc, ctx, w_gate, b_out, ident, x_sb, r):
    sb = lambda n, s, d=F32: ctx.enter_context(nc.sbuf_tensor(n, s, d))
    sem = lambda n: ctx.enter_context(nc.semaphore(n))
    xn = sb("ro_xn", [P, QT, E])
    xt = sb("ro_xt", [P, ET, NQ])
    stats = sb("ro_stats", [P, QT, 6])
    mv = sb("ro_mv", [P, QT, 2])
    var = sb("ro_var", [P, QT])
    root = sb("ro_root", [P, QT])
    rstd = sb("ro_rstd", [P, 5, QT])
    wg = sb("ro_wg", [P, ET, NX])
    bo = sb("ro_bo", [NX, E])
    before = sb("ro_before", [P, P])
    every = sb("ro_every", [P, P])
    logits = sb("ro_logits", [P, QT, NX])
    sorted8 = sb("ro_sorted8", [P, QT, NX])
    places = sb("ro_places", [P, QT, NX], U32)
    places_f = sb("ro_places_f", [P, QT, NX])
    gap = sb("ro_gap", [P, QT])
    ratio = sb("ro_ratio", [P, QT])
    weight = sb("ro_weight", [P, 2, QT])
    first = sb("ro_first", [P, QT, NX])
    second = sb("ro_second", [P, QT, NX])
    combine_t = sb("ro_combine_t", [NX, NQ])
    longest = sb("ro_longest", [1, 1])
    turn = [ctx.enter_context(nc.psum_tensor(f"ro_turn{t}", [P, NQ], F32)) for t in range(ET)]
    gate = ctx.enter_context(nc.psum_tensor("ro_gate", [P, QT * NX], F32))
    ranks = ctx.enter_context(nc.psum_tensor("ro_ranks", [P, (QT + 1) * NX], F32))
    turned_weights = ctx.enter_context(nc.psum_tensor("ro_turned_weights", [NX, NQ], F32))
    var_ready, root_ready, small, chain, normed, turned, xt_ready = map(sem, (
        "ro_var_ready", "ro_root_ready", "ro_small", "ro_chain", "ro_normed", "ro_turned", "ro_xt_ready"))
    made, gated, link, gap_ready, ratio_ready, masked, combined = map(sem, (
        "ro_made", "ro_gated", "ro_link", "ro_gap_ready", "ro_ratio_ready", "ro_masked", "ro_combined"))
    weights_turned, combine_t_ready, bias_done, ranked, hi_ready, done = map(sem, (
        "ro_weights_turned", "ro_combine_t_ready", "ro_bias_done", "ro_ranked", "ro_hi_ready", "ro_done"))

    with nc.Block() as block:
        @block.sync
        def _(sp):
            sp.dma_start(wg[:, :, :], w_gate.rearrange("(t p) e -> p t e", p=P)).then_inc(small, 16)
            sp.dma_start(bo[:, :], b_out).then_inc(small, 16)

        @block.gpsimd
        def _(pool):
            nc.gpsimd.iota(r.numbers[:, :], pattern=[[1, NQ]], base=0, channel_multiplier=0,
                           allow_small_or_imprecise_dtypes=True).then_inc(made, 1)
            pool.wait_ge(made, 1)
            nc.gpsimd.memset(every[:, :], 1.0).then_inc(made, 1)
            pool.wait_ge(made, 2)
            nc.gpsimd.affine_select(out=before[:, :], in_=every[:, :], compare_op=ALU.is_gt, fill=0.0,
                                    base=0, pattern=[[1, P]], channel_multiplier=-1).then_inc(made, 1)

        @block.tensor
        def _(pe):
            norm_transpose(nc, pe, xn, ident, turn, normed, turned)
            pe.wait_ge(small, 32)
            pe.wait_ge(xt_ready, ET)
            for t in range(QT):
                for d in range(ET):
                    last = nc.tensor.matmul(gate[:, t * NX:(t + 1) * NX], xt[:, d, t * P:(t + 1) * P], wg[:, d, :],
                                            start=(d == 0), stop=(d == ET - 1))
            last.then_inc(gated, 1)
            pe.wait_ge(made, 3)
            pe.wait_ge(masked, 1)
            for t in range(QT + 1):
                for u in range(min(t + 1, QT)):
                    last = nc.tensor.matmul(ranks[:, t * NX:(t + 1) * NX], (before if u == t else every)[:, :],
                                            r.mask[:, u, :], start=(u == 0), stop=(u == min(t, QT - 1)))
            last.then_inc(ranked, 1)
            pe.wait_ge(combined, 1)
            for t in range(QT):
                last = nc.tensor.transpose(turned_weights[:, t * P:(t + 1) * P], r.combine[:, t, :], ident[:, :])
            last.then_inc(weights_turned, 1)
            pe.wait_ge(combine_t_ready, 1)
            for t in range(QT):
                last = nc.tensor.matmul(turn[t][:, :], combine_t[:, t * P:(t + 1) * P], bo[:, :], start=True, stop=True)
            last.then_inc(bias_done, 1)

        @block.scalar
        def _(act):
            norm_scalar(nc, act, var, root, var_ready, root_ready)
            act.wait_ge(turned, 1)
            for d in range(ET):
                nc.scalar.activation(xt[:, d, :], turn[d][:, :], ACT.Copy).then_inc(xt_ready, 1)
            nc.scalar.activation(r.x_hi[:, :, :], xn[:, :, :], ACT.Copy).then_inc(hi_ready, 1)
            act.wait_ge(gap_ready, 1)
            nc.scalar.activation(ratio[:, :], gap[:, :], ACT.Exp).then_inc(ratio_ready, 1)
            act.wait_ge(weights_turned, 1)
            nc.scalar.activation(combine_t[:, :], turned_weights[:, :], ACT.Copy).then_inc(combine_t_ready, 1)

        @block.vector
        def _(dve):
            norm_vector(nc, dve, x_sb, xn, stats, mv, var, root, rstd, chain, var_ready, root_ready, normed)
            dve.wait_ge(gated, 1)
            nc.vector.tensor_copy(logits[:, :, :], gate[:, :].rearrange("p (t e) -> p t e", e=NX)).then_inc(link, 1)
            dve.wait_ge(link, 1)
            for t in range(QT):
                nc.vector.max(sorted8[:, t, :], logits[:, t, :]).then_inc(link, 1)
            dve.wait_ge(link, 1 + QT)
            nc.vector.tensor_tensor(gap[:, :], sorted8[:, :, 1], sorted8[:, :, 0], ALU.subtract).then_inc(gap_ready, 1)
            for t in range(QT):
                nc.vector.max_index(places[:, t, :], sorted8[:, t, :], logits[:, t, :]).then_inc(link, 1)
            dve.wait_ge(link, 1 + 2 * QT)
            nc.vector.tensor_copy(places_f[:, :, :], places[:, :, :]).then_inc(link, 1)
            dve.wait_ge(made, 1)
            dve.wait_ge(link, 2 + 2 * QT)
            for t in range(QT):
                for place, chosen in enumerate((first, second)):
                    nc.vector.tensor_scalar(chosen[:, t, :], r.numbers[:, 0:NX], places_f[:, t, place:place + 1], None,
                                            ALU.is_equal).then_inc(link, 1)
            dve.wait_ge(link, 2 + 4 * QT)
            nc.vector.tensor_tensor(r.mask[:, :, :], first[:, :, :], second[:, :, :], ALU.add).then_inc(masked, 1)
            dve.wait_ge(ratio_ready, 1)
            nc.vector.tensor_scalar(weight[:, 1, :], ratio[:, :], 1.0, None, ALU.add).then_inc(link, 1)
            dve.wait_ge(link, 3 + 4 * QT)
            nc.vector.reciprocal(weight[:, 0, :], weight[:, 1, :]).then_inc(link, 1)
            dve.wait_ge(link, 4 + 4 * QT)
            nc.vector.tensor_tensor(weight[:, 1, :], weight[:, 0, :], ratio[:, :], ALU.mult).then_inc(link, 1)
            dve.wait_ge(link, 5 + 4 * QT)
            for t in range(QT):
                nc.vector.tensor_scalar(second[:, t, :], second[:, t, :], weight[:, 1, t:t + 1], None, ALU.mult).then_inc(link, 1)
            dve.wait_ge(masked, 1)
            dve.wait_ge(link, 5 + 5 * QT)
            for t in range(QT):
                nc.vector.scalar_tensor_tensor(r.combine[:, t, :], first[:, t, :], weight[:, 0, t:t + 1], second[:, t, :],
                                               ALU.mult, ALU.add).then_inc(link, 1)
            dve.wait_ge(link, 5 + 6 * QT)
            nc.vector.tensor_copy(gap[:, :], ratio[:, :]).then_inc(combined, 1)
            dve.wait_ge(hi_ready, 1)
            nc.vector.tensor_tensor(r.x_lo[:, :, :], xn[:, :, :], r.x_hi[:, :, :].bitcast(F32), ALU.subtract).then_inc(done, 1)
            dve.wait_ge(ranked, 1)
            nc.vector.tensor_copy(r.rank[:, :, :], ranks[:, 0:QT * NX].rearrange("p (t e) -> p t e", e=NX)).then_inc(done, 1)
            nc.vector.reduce_max(longest[:, :], ranks[0:1, QT * NX:(QT + 1) * NX], X).then_inc(link, 1)
            dve.wait_ge(link, 6 + 6 * QT)
            nc.vector.tensor_scalar(r.long[:, :], longest[:, :], float(SLOTS), None, ALU.is_gt).then_inc(done, 1)
            dve.wait_ge(bias_done, 1)
            for t in range(QT):
                nc.vector.tensor_tensor(x_sb[:, t, :], x_sb[:, t, :], turn[t][:, :], ALU.add).then_inc(done, 1)


def run_experts(nc, ctx, half, w_in, b_in, w_out, ident, x_sb, r):
    u = f"ex{half}_"
    sb = lambda n, s, d=F32: ctx.enter_context(nc.sbuf_tensor(u + n, s, d))
    sem = lambda n: ctx.enter_context(nc.semaphore(u + n))
    ST = SLOTS // P
    b_hidden = sb("b_hidden", [P, NX, M // P])
    b_cur = sb("b_cur", [P, M // P])
    wi = [sb(f"wi{b}", [P, ET, MC]) for b in range(2)]
    wi_hi = [sb(f"wi_hi{b}", [P, ET, MC], F32R) for b in range(2)]
    wi_lo = [sb(f"wi_lo{b}", [P, ET, MC], F32R) for b in range(2)]
    wo = [sb(f"wo{b}", [P, MT, E]) for b in range(2)]
    wo_hi = [sb(f"wo_hi{b}", [P, MT, E], F32R) for b in range(2)]
    wo_lo = [sb(f"wo_lo{b}", [P, MT, E], F32R) for b in range(2)]
    h = sb("h", [P, MT, SLOTS])
    h_hi = [sb(f"h_hi{b}", [P, MT, SLOTS], F32R) for b in range(2)]
    h_lo = [sb(f"h_lo{b}", [P, MT, SLOTS], F32R) for b in range(2)]
    sel = sb("sel", [P, QT, SLOTS], F32R)
    sel_t = sb("sel_t", [P, ST, NQ], F32R)
    xg_hi = sb("xg_hi", [P, ET, SLOTS], F32R)
    xg_lo = sb("xg_lo", [P, ET, SLOTS], F32R)
    y_hi = sb("y_hi", [P, ST, E], F32R)
    y_lo = sb("y_lo", [P, ST, E], F32R)
    hp = [ctx.enter_context(nc.psum_tensor(f"{u}hp{b}", [P, MT, SLOTS], F32)) for b in range(2)]
    yp = ctx.enter_context(nc.psum_tensor(u + "yp", [P, ST, E], F32))
    move = ctx.enter_context(nc.psum_tensor(u + "move", [P, 2, NQ], F32))
    move_g = move[:, :, :].rearrange("p a (b n) -> p (a b) n", n=SLOTS)
    biases, b_ready = map(sem, ("biases", "b_ready"))
    wi_loaded = [sem(f"wi_loaded{b}") for b in range(2)]
    wo_loaded = [sem(f"wo_loaded{b}") for b in range(2)]
    wi_hi_ready, wi_lo_ready, wo_hi_ready, wo_lo_ready = map(sem, ("wi_hi_ready", "wi_lo_ready", "wo_hi_ready", "wo_lo_ready"))
    h_done, h_ready, h_hi_ready, h_lo_ready, y_done, y_hi_ready, y_lo_ready = map(sem, (
        "h_done", "h_ready", "h_hi_ready", "h_lo_ready", "y_done", "y_hi_ready", "y_lo_ready"))
    sel_ready, sel_turned, sel_t_ready, gathered, xg_ready, scattered, x_stands = map(sem, (
        "sel_ready", "sel_turned", "sel_t_ready", "gathered", "xg_ready", "scattered", "x_stands"))

    def guarded(eng, program):
        if half == 0:
            program()
        else:
            flag = eng.value_load(r.long[:, :], min_val=0, max_val=1)
            with eng.If(flag > 0):
                program()

    with nc.Block() as block:
        @block.sync
        def _(sp):
            def load_in(e, mc):
                sp.dma_start(wi[mc % 2][:, :, :], w_in[bass.ds(e * E, E), mc * MC:(mc + 1) * MC]
                             .rearrange("(t p) m -> p t m", p=P)).then_inc(wi_loaded[mc % 2], 16)

            def load_out(e, mc):
                sp.dma_start(wo[mc % 2][:, :, :], w_out[bass.ds(e * M + mc * MC, MC), :]
                             .rearrange("(t p) f -> p t f", p=P)).then_inc(wo_loaded[mc % 2], 16)

            def expert(e, last):
                for mc in range(NMC):
                    n = NMC * e + mc
                    ahead = (e, mc + 2) if mc + 2 < NMC else (e + 1, mc + 2 - NMC)
                    if last and mc + 2 >= NMC:
                        continue
                    sp.wait_ge(wi_lo_ready, n + 1)
                    load_in(*ahead)
                    sp.wait_ge(wo_lo_ready, n + 1)
                    load_out(*ahead)

            def program():
                sp.dma_start(b_hidden[:, :, :], b_in).then_inc(biases, 16)
                for mc in range(2):
                    load_in(0, mc)
                    load_out(0, mc)
                rolled(sp, NX, expert)

            guarded(sp, program)

        @block.tensor
        def _(pe):
            def hidden(e, mc):
                n, b = NMC * e + mc, mc % 2
                pe.wait_ge(wi_lo_ready, n + 1)
                if mc == 0:
                    pe.wait_ge(xg_ready, 2 * (e + 1))
                wait_reuse(pe, h_ready, MT * (n - 1))
                for t in range(MT):
                    for a, (lhs, rhs) in enumerate(((wi_hi, xg_hi), (wi_lo, xg_hi), (wi_hi, xg_lo))):
                        for d in range(ET):
                            last = nc.tensor.matmul(hp[b][:, t, :], lhs[b][:, d, t * P:(t + 1) * P], rhs[:, d, :],
                                                    start=(a == 0 and d == 0), stop=(a == 2 and d == ET - 1))
                    if t % 2 == 1:
                        last.then_inc(h_done, 1)

            def output(e, mc):
                n, b = NMC * e + mc, mc % 2
                pe.wait_ge(wo_lo_ready, n + 1)
                pe.wait_ge(h_lo_ready, MT * (n + 1))
                if mc == 0:
                    wait_reuse(pe, y_lo_ready, e)
                for t in range(ST):
                    for m in range(MT):
                        for a, (lhs, rhs) in enumerate(((h_hi, wo_hi), (h_lo, wo_hi), (h_hi, wo_lo))):
                            last = nc.tensor.matmul(yp[:, t, :], lhs[b][:, m, t * P:(t + 1) * P], rhs[b][:, m, :],
                                                    start=(mc == 0 and m == 0 and a == 0),
                                                    stop=(mc == NMC - 1 and m == MT - 1 and a == 2))
                last.then_inc(y_done, 1)

            def gather(e, part):
                if part == 0:
                    pe.wait_ge(sel_ready, QT * (e + 1))
                    wait_reuse(pe, sel_t_ready, e)
                else:
                    pe.wait_ge(xg_ready, 2 * e + 1)
                for d in range(ET):
                    for t in range(QT):
                        last = nc.tensor.matmul(move_g[:, d, :], (r.x_hi, r.x_lo)[part][:, t, d * P:(d + 1) * P],
                                                sel[:, t, :], start=(t == 0), stop=(t == QT - 1))
                last.then_inc(gathered, 1)

            def turn_sel(e):
                pe.wait_ge(x_stands, QT * (e + 1))
                for s in range(ST):
                    for t in range(QT):
                        last = nc.tensor.transpose(move[:, s, t * P:(t + 1) * P], sel[:, t, s * P:(s + 1) * P].bitcast(F32),
                                                   ident[:, :])
                last.then_inc(sel_turned, 1)

            def scatter(e, tiles):
                if tiles[0] == 0:
                    pe.wait_ge(y_lo_ready, e + 1)
                    pe.wait_ge(sel_t_ready, e + 1)
                else:
                    pe.wait_ge(x_stands, QT * (e + 1) + tiles[0])
                for t in tiles:
                    for a, y in enumerate((y_hi, y_lo)):
                        for s in range(ST):
                            last = nc.tensor.matmul(move[:, t % 2, :], sel_t[:, s, t * P:(t + 1) * P], y[:, s, :],
                                                    start=(a == 0 and s == 0), stop=(a == 1 and s == ST - 1))
                last.then_inc(scattered, 1)

            def expert(e, last):
                first = isinstance(e, int) and e == 0
                hidden(e, 0)
                if not first:
                    scatter(e - 1, (0, 1))
                hidden(e, 1)
                if not first:
                    scatter(e - 1, (2, 3))
                output(e, 0)
                turn_sel(e)
                hidden(e, 2)
                output(e, 1)
                hidden(e, 3)
                if not last:
                    gather(e + 1, 0)
                output(e, 2)
                if not last:
                    gather(e + 1, 1)
                output(e, 3)

            def program():
                gather(0, 0)
                gather(0, 1)
                rolled(pe, NX, expert)
                scatter(NX - 1, (0, 1))
                scatter(NX - 1, (2, 3))

            guarded(pe, program)

        @block.scalar
        def _(act):
            def split_in(i, b):
                act.wait_ge(wi_loaded[b], 16 * (i + 1))
                nc.scalar.activation(wi_hi[b][:, :, :], wi[b][:, :, :], ACT.Copy).then_inc(wi_hi_ready, 1)

            def keep_gathered(e):
                for part, to in enumerate((xg_hi, xg_lo)):
                    act.wait_ge(gathered, 2 * e + part + 1)
                    nc.scalar.activation(to[:, :, :], move_g, ACT.Copy).then_inc(xg_ready, 1)

            def expert(e, last):
                for mc in range(NMC):
                    n, b = NMC * e + mc, mc % 2
                    if mc == 0:
                        act.wait_ge(b_ready, e + 1)
                    if not (last and mc == NMC - 1):
                        wait_reuse(act, h_done, 2 * n)
                        split_in(2 * e + (mc + 1) // 2, 1 - b)
                    wait_reuse(act, h_lo_ready, MT * n)
                    for t in range(MT):
                        act.wait_ge(h_done, 2 * n + t // 2 + 1)
                        nc.scalar.activation(h[:, t, :], hp[b][:, t, :], ACT.Gelu,
                                             bias=b_cur[:, mc * MT + t:mc * MT + t + 1]).then_inc(h_ready, 1)
                    act.wait_ge(wo_loaded[b], 16 * (2 * e + mc // 2 + 1))
                    wait_reuse(act, y_done, n - 1)
                    nc.scalar.activation(wo_hi[b][:, :, :], wo[b][:, :, :], ACT.Copy).then_inc(wo_hi_ready, 1)
                    if mc == 1:
                        act.wait_ge(sel_turned, e + 1)
                        nc.scalar.activation(sel_t[:, :, :], move[:, :, :], ACT.Copy).then_inc(sel_t_ready, 1)
                if not last:
                    keep_gathered(e + 1)
                act.wait_ge(y_done, NMC * (e + 1))
                nc.scalar.activation(y_hi[:, :, :], yp[:, :, :], ACT.Copy).then_inc(y_hi_ready, 1)

            def program():
                keep_gathered(0)
                split_in(0, 0)
                rolled(act, NX, expert)

            guarded(act, program)

        @block.vector
        def _(dve):
            def split_in(n, b):
                dve.wait_ge(wi_hi_ready, n + 1)
                nc.vector.tensor_tensor(wi_lo[b][:, :, :], wi[b][:, :, :], wi_hi[b][:, :, :].bitcast(F32),
                                        ALU.subtract).then_inc(wi_lo_ready, 1)

            def select(e):
                for t in range(QT):
                    nc.vector.tensor_scalar(sel[:, t, :], r.numbers[:, half * SLOTS:(half + 1) * SLOTS],
                                            r.rank[:, t, bass.ds(e, 1)], r.mask[:, t, bass.ds(e, 1)],
                                            ALU.is_equal, ALU.mult).then_inc(sel_ready, 1)

            def add(e, tiles):
                dve.wait_ge(x_stands, QT * (e + 1))
                dve.wait_ge(scattered, 2 * e + tiles[0] // 2 + 1)
                for t in tiles:
                    nc.vector.scalar_tensor_tensor(x_sb[:, t, :], move[:, t % 2, :], r.combine[:, t, bass.ds(e, 1)],
                                                   x_sb[:, t, :], ALU.mult, ALU.add).then_inc(x_stands, 1)

            def expert(e, last):
                first = isinstance(e, int) and e == 0
                wait_reuse(dve, h_ready, NMC * MT * e)
                nc.vector.tensor_scalar(b_cur[:, :], b_hidden[:, bass.ds(e, 1), :].rearrange("p a t -> p (a t)"), 1.0,
                                        None, ALU.mult).then_inc(b_ready, 1)
                for mc in range(NMC):
                    n, b = NMC * e + mc, mc % 2
                    if not (last and mc == NMC - 1):
                        split_in(n + 1, 1 - b)
                    wait_reuse(dve, y_done, n - 1)
                    for t in range(0, MT, 2):
                        two = slice(t, t + 2)
                        dve.wait_ge(h_ready, MT * n + t + 2)
                        nc.vector.tensor_copy(h_hi[b][:, two, :], h[:, two, :]).then_inc(h_hi_ready, 1)
                        dve.wait_ge(h_hi_ready, 2 * n + t // 2 + 1)
                        nc.vector.tensor_tensor(h_lo[b][:, two, :], h[:, two, :], h_hi[b][:, two, :].bitcast(F32),
                                                ALU.subtract).then_inc(h_lo_ready, 2)
                    dve.wait_ge(wo_hi_ready, n + 1)
                    nc.vector.tensor_tensor(wo_lo[b][:, :, :], wo[b][:, :, :], wo_hi[b][:, :, :].bitcast(F32),
                                            ALU.subtract).then_inc(wo_lo_ready, 1)
                    if mc < 2 and not first:
                        add(e - 1, (2 * mc, 2 * mc + 1))
                    if mc == 2 and not last:
                        dve.wait_ge(sel_turned, e + 1)
                        select(e + 1)
                dve.wait_ge(y_hi_ready, e + 1)
                nc.vector.tensor_tensor(y_lo[:, :, :], yp[:, :, :], y_hi[:, :, :].bitcast(F32),
                                        ALU.subtract).then_inc(y_lo_ready, 1)

            def program():
                dve.sem_inc(x_stands, QT)
                select(0)
                dve.wait_ge(biases, 16)
                split_in(0, 0)
                rolled(dve, NX, expert)
                add(NX - 1, (0, 1))
                add(NX - 1, (2, 3))

            guarded(dve, program)


def feed_forward(nc, ctx, w_gate, w_in, b_in, w_out, b_out, ident, x_sb, out_dram):
    sb = lambda n, s, d=F32: ctx.enter_context(nc.sbuf_tensor(n, s, d))
    r = Routing()
    r.x_hi = sb("ff_x_hi", [P, QT, E], F32R)
    r.x_lo = sb("ff_x_lo", [P, QT, E], F32R)
    r.numbers = sb("ff_numbers", [P, NQ])
    r.mask = sb("ff_mask", [P, QT, NX])
    r.rank = sb("ff_rank", [P, QT, NX])
    r.combine = sb("ff_combine", [P, QT, NX])
    r.long = sb("ff_long", [1, 1], I32)
    stored = ctx.enter_context(nc.semaphore("ff_stored"))
    with ExitStack() as s:
        route(nc, s, w_gate, b_out, ident, x_sb, r)
    for half in range(NQ // SLOTS):
        with ExitStack() as s:
            run_experts(nc, s, half, w_in, b_in, w_out, ident, x_sb, r)
    with nc.Block() as block:
        @block.sync
        def _(sp):
            sp.dma_start(out_dram.rearrange("a (t p) e -> p (a t) e", p=P), x_sb[:, :, :]).then_inc(stored, 16)
            sp.wait_ge(stored, 16)


def perceiver_layer(nc, x, ctx_t, xw_in, xb_in, xb_cols, xw_out, xb_out, sw_in, sb_cols, sw_out, sb_out, w_gate,
                    w_in, b_in, w_out, b_out, out):
    q_scratch = nc.dram_tensor("q_scratch", [3 * D, H * NQ], F32, kind="Internal").ap()
    k_hi_dram = nc.dram_tensor("k_hi_scratch", [E, NK], F32, kind="Internal").ap()
    k_lo_dram = nc.dram_tensor("k_lo_scratch", [E, NK], F32, kind="Internal").ap()
    v_dram = nc.dram_tensor("v_scratch", [NK, E], F32, kind="Internal").ap()
    with ExitStack() as whole:
        x_sb = whole.enter_context(nc.sbuf_tensor("x_sb", [P, QT, E], F32))
        ident = whole.enter_context(nc.sbuf_tensor("ident", [P, P], F32))
        with ExitStack() as cross:
            q_stack = cross.enter_context(nc.sbuf_tensor("q_stack", [QROWS, H * NQ], F32R))
            q_top = cross.enter_context(nc.sbuf_tensor("q_top", [P, NG], F32))
            head_rows = cross.enter_context(nc.sbuf_tensor("head_rows", [P, HG], F32))
            bounded = cross.enter_context(nc.sbuf_tensor("bounded", [1, 1], I32))
            with ExitStack() as s:
                project_queries(nc, s, x, xw_in, xb_cols, x_sb, ident, q_stack, q_scratch, q_top, head_rows)
            with ExitStack() as s:
                stream_context(nc, s, ctx_t, xw_in, xb_in, xb_cols, k_hi_dram, k_lo_dram, v_dram, q_top,
                               head_rows, bounded)
            with ExitStack() as s:
                find_maxima(nc, s, k_hi_dram, k_lo_dram, q_scratch, ident, q_stack, bounded)
            o_acc = cross.enter_context(nc.sbuf_tensor("o_acc", [P, NG, NQ], F32))
            total_acc = cross.enter_context(nc.sbuf_tensor("total_acc", [P, NG, NQ], F32))
            p_sum = cross.enter_context(nc.sbuf_tensor("p_sum", [P, H * NQ], F32))
            with ExitStack() as s:
                attend(nc, s, k_hi_dram, k_lo_dram, v_dram, q_stack, o_acc, p_sum, total_acc)
            with ExitStack() as s:
                cross_output(nc, s, xw_out, xb_out, o_acc, p_sum, total_acc, x_sb)
        with ExitStack() as s:
            self_attention(nc, s, sw_in, sb_cols, sw_out, sb_out, ident, x_sb)
        with ExitStack() as s:
            feed_forward(nc, s, w_gate, w_in, b_in, w_out, b_out, ident, x_sb, out)


def kernel(**inputs):
    import numpy as np
    import concourse.bacc as bacc
    from concourse.bass_utils import run_bass_kernel_spmd

    a = {k: np.asarray(v) for k, v in inputs.items()}
    arrays = {
        "x": a["x"],
        "ctx_t": a["ctx_1024"][0].T,
        "xw_in": a["L0_xattn_in_proj_weight"].T,
        "xb_in": a["L0_xattn_in_proj_bias"],
        "xb_cols": a["L0_xattn_in_proj_bias"].reshape(3 * ET, P).T,
        "xw_out": a["L0_xattn_out_proj_weight"].T,
        "xb_out": a["L0_xattn_out_proj_bias"],
        "sw_in": a["L0_attn_in_proj_weight"].reshape(H, 3, D, E).transpose(3, 1, 0, 2).reshape(E, 3, E),
        "sb_cols": a["L0_attn_in_proj_bias"].reshape(H, 3, D).transpose(1, 0, 2).reshape(3 * ET, P).T,
        "sw_out": a["L0_attn_out_proj_weight"].T,
        "sb_out": a["L0_attn_out_proj_bias"],
        "w_gate": a["L0_ffn_W_gate"],
        "w_in": a["L0_ffn_W_in"].reshape(NX * E, M),
        "b_in": a["L0_ffn_b_in"].reshape(NX, M // P, P).transpose(2, 0, 1),
        "w_out": a["L0_ffn_W_out"].reshape(NX * M, E),
        "b_out": a["L0_ffn_b_out"],
    }
    arrays = {k: np.ascontiguousarray(v) for k, v in arrays.items()}
    nc = bacc.Bacc("TRN2", target_bir_lowering=False, num_devices=1)
    args = [nc.dram_tensor(k, v.shape, mybir.dt.from_np(v.dtype), kind="ExternalInput").ap() for k, v in arrays.items()]
    out = nc.dram_tensor("out", (1, NQ, E), F32, kind="ExternalOutput").ap()
    perceiver_layer(nc, *args, out)
    got = run_bass_kernel_spmd(nc, [arrays], core_ids=[0])
    return got.results[0]["out"]
```

```python
from contextlib import ExitStack

import concourse.bass as bass
from concourse import mybir

F32 = mybir.dt.float32
F32R = mybir.dt.float32r
U32 = mybir.dt.uint32
I32 = mybir.dt.int32
ACT = mybir.ActivationFunctionType
ALU = mybir.AluOpType
X = mybir.AxisListType.X

P = 128
NQ = 512
E = 512
NK = 8192
H = 16
D = E // H
ET = E // P
QT = NQ // P
HG = P // D
NG = H // HG
SCALE = float(D) ** -0.5
SAFE = 30.0
EPS = 1e-5
CH = 512
NCH = NK // CH
KT = CH // P
QROWS = 3 * D + 1
NX = 8
M = 2048
MC = 512
MT = MC // P
NMC = M // MC
SLOTS = 192
PAIRED = SLOTS - P
COLS = 2 * P
ROUNDS = -(-NQ // SLOTS)


class Ahead:
    pass


class Routing:
    pass


def rolled(eng, steps, body):
    body(0, False)
    with eng.Fori(1, steps - 1) as i:
        body(i, False)
    body(steps - 1, True)


def wait_reuse(eng, sem, count):
    if not isinstance(count, int) or count > 0:
        eng.wait_ge(sem, count)


def norm_scalar(nc, act, var, root, var_ready, root_ready):
    act.wait_ge(var_ready, 1)
    nc.scalar.activation(root[:, :], var[:, :], ACT.Sqrt).then_inc(root_ready, 1)


def norm_vector(nc, dve, x, xn, stats, mv, var, root, rstd, chain, var_ready, root_ready, ready, loaded=None):
    for t in range(QT):
        if loaded:
            dve.wait_ge(loaded[t], 16)
        nc.vector.bn_stats(stats[:, t, :], x[:, t, :]).then_inc(chain, 1)
    dve.wait_ge(chain, QT)
    for t in range(QT):
        nc.vector.bn_aggr(mv[:, t, :], stats[:, t, :]).then_inc(chain, 1)
    dve.wait_ge(chain, 2 * QT)
    nc.vector.tensor_scalar(var[:, :], mv[:, :, 1], EPS, None, ALU.add).then_inc(var_ready, 1)
    dve.wait_ge(root_ready, 1)
    nc.vector.reciprocal(rstd[:, 0, :], root[:, :]).then_inc(chain, 1)
    dve.wait_ge(chain, 2 * QT + 1)
    nc.vector.tensor_tensor(rstd[:, 1, :], rstd[:, 0, :], rstd[:, 0, :], ALU.mult).then_inc(chain, 1)
    dve.wait_ge(chain, 2 * QT + 2)
    dve.wait_ge(var_ready, 1)
    nc.vector.tensor_tensor(rstd[:, 2, :], rstd[:, 1, :], var[:, :], ALU.mult).then_inc(chain, 1)
    dve.wait_ge(chain, 2 * QT + 3)
    nc.vector.tensor_scalar(rstd[:, 3, :], rstd[:, 2, :], -0.5, 1.5, ALU.mult, ALU.add).then_inc(chain, 1)
    dve.wait_ge(chain, 2 * QT + 4)
    nc.vector.tensor_tensor(rstd[:, 4, :], rstd[:, 3, :], rstd[:, 0, :], ALU.mult).then_inc(chain, 1)
    dve.wait_ge(chain, 2 * QT + 5)
    for t in range(QT):
        nc.vector.tensor_scalar(xn[:, t, :], x[:, t, :], mv[:, t, 0:1], rstd[:, 4, t:t + 1],
                                ALU.subtract, ALU.mult).then_inc(ready, 1)


def norm_transpose(nc, pe, xn, ident, banks, ready, turned):
    for t in range(QT):
        pe.wait_ge(ready, t + 1)
        for d in range(ET):
            last = nc.tensor.transpose(banks[d][:, t * P:(t + 1) * P], xn[:, t, d * P:(d + 1) * P],
                                       ident[:, :])
    last.then_inc(turned, 1)


def make_identity(nc, pool, ident, zeroed, made):
    nc.gpsimd.memset(ident[:, :], 0.0).then_inc(zeroed, 1)
    pool.wait_ge(zeroed, 1)
    nc.gpsimd.affine_select(out=ident[:, :], in_=ident[:, :], compare_op=ALU.not_equal, fill=1.0,
                            base=0, pattern=[[-1, P]], channel_multiplier=1).then_inc(made, 1)


def split_chunk_high(nc, act, a, n, i, b):
    act.wait_ge(a.c_loaded[b], 16 * (i + 1))
    nc.scalar.activation(a.c_hi[b][:, :, :], a.c[b][:, :, :], ACT.Copy).then_inc(a.c_hi_ready, 1)


def split_chunk_low(nc, dve, a, n, b):
    dve.wait_ge(a.c_hi_ready, n + 1)
    nc.vector.tensor_tensor(a.c_lo[b][:, :, :], a.c[b][:, :, :], a.c_hi[b][:, :, :].bitcast(F32),
                            ALU.subtract).then_inc(a.c_lo_ready, 1)


def project_queries(nc, ctx, x_dram, c_dram, w_in, b_in, b_cols, x_sb, ident, q_stack, head_rows, a):
    sb = lambda n, s, d=F32: ctx.enter_context(nc.sbuf_tensor(n, s, d))
    sem = lambda n: ctx.enter_context(nc.semaphore(n))
    wq = sb("pq_wq", [P, ET, E])
    bq = sb("pq_bq", [P, NG])
    xn = sb("pq_xn", [P, QT, E])
    wq_hi, wq_lo = (sb(f"pq_wq_{n}", [P, ET, E], F32R) for n in ("hi", "lo"))
    xt_hi, xt_lo = (sb(f"pq_xt_{n}", [P, ET, NQ], F32R) for n in ("hi", "lo"))
    w = sb("pq_w", [P, ET, 2 * E])
    q_hi, q_lo = a.q_hi, a.q_lo
    stats = sb("pq_stats", [P, QT, 6])
    mv = sb("pq_mv", [P, QT, 2])
    var = sb("pq_var", [P, QT])
    root = sb("pq_root", [P, QT])
    rstd = sb("pq_rstd", [P, 5, QT])
    var_ready, root_ready = map(sem, ("pq_var_ready", "pq_root_ready"))
    turn = [ctx.enter_context(nc.psum_tensor(f"pq_turn{d}", [P, NQ], F32)) for d in range(ET)]
    proj = [ctx.enter_context(nc.psum_tensor(f"pq_proj{g}", [P, NQ], F32)) for g in range(NG)]
    w_loaded, chain, normed, turned, xt_ready = map(sem, (
        "pq_w_loaded", "pq_chain", "pq_normed", "pq_turned", "pq_xt_ready"))
    projected, hi_ready, lo_ready, zeroed, ident_made, kv_loaded, w_hi_ready, w_lo_ready = map(sem, (
        "pq_projected", "pq_hi_ready", "pq_lo_ready", "pq_zeroed", "pq_ident_made", "pq_kv_loaded",
        "pq_w_hi_ready", "pq_w_lo_ready"))

    x_loaded = [sem(f"pq_x_loaded{t}") for t in range(QT)]
    wq_hi_ready, wq_lo_ready, xt_lo_ready = map(sem, ("pq_wq_hi_ready", "pq_wq_lo_ready", "pq_xt_lo_ready"))

    with nc.Block() as block:
        @block.sync
        def _(sp):
            for t in range(QT):
                sp.dma_start(x_sb[:, t, :], x_dram.rearrange("a (t p) e -> p (a t) e", p=P)[:, t, :]).then_inc(x_loaded[t], 16)
            sp.dma_start(wq[:, :, :], w_in[:, 0:E].rearrange("(t p) f -> p t f", p=P)).then_inc(w_loaded, 16)
            sp.dma_start(bq[:, :], b_cols[:, 0:NG]).then_inc(w_loaded, 16)
            sp.dma_start(w[:, :, :], w_in[:, E:3 * E].rearrange("(t p) f -> p t f", p=P)).then_inc(kv_loaded, 16)
            sp.dma_start(a.bk[:, :], b_cols[:, NG:2 * NG]).then_inc(a.biases, 16)
            sp.dma_start(a.bv[:, :], b_in[2 * E:3 * E].partition_broadcast(P)).then_inc(a.biases, 16)
            for b in range(2):
                sp.dma_start(a.c[b][:, :, :], c_dram.rearrange("(t p) n -> p t n", p=P)[:, :, b * CH:(b + 1) * CH]
                             ).then_inc(a.c_loaded[b], 16)

        @block.gpsimd
        def _(pool):
            make_identity(nc, pool, ident, zeroed, ident_made)
            nc.gpsimd.memset(head_rows[:, :], 1.0).then_inc(zeroed, 1)
            pool.wait_ge(zeroed, 2)
            nc.gpsimd.affine_select(out=head_rows[:, :], in_=head_rows[:, :], compare_op=ALU.is_ge, fill=0.0,
                                    base=0, pattern=[[-D, HG]], channel_multiplier=1).then_inc(zeroed, 1)
            pool.wait_ge(zeroed, 3)
            nc.gpsimd.affine_select(out=head_rows[:, :], in_=head_rows[:, :], compare_op=ALU.is_ge, fill=0.0,
                                    base=D - 1, pattern=[[D, HG]], channel_multiplier=-1).then_inc(zeroed, 1)
            pool.wait_ge(zeroed, 4)
            nc.gpsimd.memset(q_stack[3 * D:QROWS, :].bitcast(F32), 0.0).then_inc(zeroed, 1)

        @block.vector
        def _(dve):
            norm_vector(nc, dve, x_sb, xn, stats, mv, var, root, rstd, chain, var_ready, root_ready, normed, x_loaded)
            dve.wait_ge(wq_hi_ready, 1)
            nc.vector.tensor_tensor(wq_lo[:, :, :], wq[:, :, :], wq_hi[:, :, :].bitcast(F32),
                                    ALU.subtract).then_inc(wq_lo_ready, 1)
            for d in range(ET):
                dve.wait_ge(xt_ready, d + 1)
                nc.vector.tensor_tensor(xt_lo[:, d, :], turn[d][:, :], xt_hi[:, d, :].bitcast(F32),
                                        ALU.subtract).then_inc(xt_lo_ready, 1)
            for d in range(ET):
                dve.wait_ge(w_hi_ready, d + 1)
                nc.vector.tensor_tensor(a.w_lo[:, d, :], w[:, d, :], a.w_hi[:, d, :].bitcast(F32),
                                        ALU.subtract).then_inc(w_lo_ready, 1)
            for g in range(NG):
                if g == 1:
                    split_chunk_low(nc, dve, a, 0, 0)
                dve.wait_ge(hi_ready, g + 1)
                nc.vector.scalar_tensor_tensor(q_lo[:, g, :], proj[g][:, :], bq[:, g:g + 1], q_hi[:, g, :].bitcast(F32),
                                               ALU.add, ALU.subtract).then_inc(lo_ready, 1)

        @block.tensor
        def _(pe):
            pe.wait_ge(ident_made, 1)
            norm_transpose(nc, pe, xn, ident, turn, normed, turned)
            pe.wait_ge(xt_ready, ET)
            for g in range(NG):
                for a, (lhs, rhs) in enumerate(((wq_hi, xt_hi), (wq_lo, xt_hi), (wq_hi, xt_lo))):
                    if g == 0 and a == 1:
                        pe.wait_ge(wq_lo_ready, 1)
                    if g == 0 and a == 2:
                        pe.wait_ge(xt_lo_ready, ET)
                    for d in range(ET):
                        last = nc.tensor.matmul(proj[g][:, :], lhs[:, d, g * P:(g + 1) * P], rhs[:, d, :],
                                                start=(a == 0 and d == 0), stop=(a == 2 and d == ET - 1))
                last.then_inc(projected, 1)

        @block.scalar
        def _(act):
            norm_scalar(nc, act, var, root, var_ready, root_ready)
            act.wait_ge(w_loaded, 32)
            nc.scalar.activation(wq_hi[:, :, :], wq[:, :, :], ACT.Copy).then_inc(wq_hi_ready, 1)
            act.wait_ge(turned, 1)
            for d in range(ET):
                nc.scalar.activation(xt_hi[:, d, :], turn[d][:, :], ACT.Copy).then_inc(xt_ready, 1)
            act.wait_ge(kv_loaded, 16)
            for d in range(ET):
                nc.scalar.activation(a.w_hi[:, d, :], w[:, d, :], ACT.Copy).then_inc(w_hi_ready, 1)
            for g in range(NG):
                if g == 1:
                    split_chunk_high(nc, act, a, 0, 0, 0)
                act.wait_ge(projected, g + 1)
                nc.scalar.activation(q_hi[:, g, :], proj[g][:, :], ACT.Identity,
                                     bias=bq[:, g:g + 1]).then_inc(hi_ready, 1)


def stream_context(nc, ctx, c_dram, k_hi_dram, k_lo_dram, v_dram, q_stack, head_rows, bounded, a):
    sb = lambda n, s, d=F32: ctx.enter_context(nc.sbuf_tensor(n, s, d))
    sem = lambda n: ctx.enter_context(nc.semaphore(n))
    w_hi, w_lo, bk, bv, c, c_loaded = a.w_hi, a.w_lo, a.bk, a.bv, a.c, a.c_loaded
    a.c_hi.append(sb("sc_c_hi1", [P, ET, CH], F32R))
    a.c_lo.append(sb("sc_c_lo1", [P, ET, CH], F32R))
    c_hi, c_lo, c_lo_ready, q_hi, q_lo = a.c_hi, a.c_lo, a.c_lo_ready, a.q_hi, a.q_lo
    q_top = sb("sc_q_top", [P, NG])
    k_hi = [sb(f"sc_k_hi{b}", [P, NG, CH], F32R) for b in range(2)]
    k_lo = [sb(f"sc_k_lo{b}", [P, NG, CH], F32R) for b in range(2)]
    v = [sb(f"sc_v{b}", [P, KT, E]) for b in range(2)]
    kp = [ctx.enter_context(nc.psum_tensor(f"sc_kp{g}", [P, CH], F32)) for g in range(NG)]
    vp = [ctx.enter_context(nc.psum_tensor(f"sc_vp{t}", [P, E], F32)) for t in range(KT)]
    k_top = [sb(f"sc_k_top{b}", [P, NG]) for b in range(2)]
    k_top_all = sb("sc_k_top_all", [P, NG])
    product = sb("sc_product", [P, NG])
    bound = sb("sc_bound", [1, 1])
    q_topped, k_topped, k_top_kept, product_ready, bound_done, bound_ready, flagged = map(sem, (
        "sc_q_topped", "sc_k_topped", "sc_k_top_kept", "sc_product_ready", "sc_bound_done", "sc_bound_ready", "sc_flagged"))
    k_done, v_done = map(sem, ("sc_k_done", "sc_v_done"))
    k_hi_ready, k_lo_ready, v_ready = map(sem, ("sc_k_hi_ready", "sc_k_lo_ready", "sc_v_ready"))
    stored = [sem(f"sc_stored{b}") for b in range(2)]
    PAIRS, STORES = NCH // 2, 3 * 16
    c_view = c_dram.rearrange("(t p) n -> p t n", p=P)
    k_hi_view = k_hi_dram.rearrange("(g p) n -> p g n", p=P)
    k_lo_view = k_lo_dram.rearrange("(g p) n -> p g n", p=P)

    with nc.Block() as block:
        @block.sync
        def _(sp):
            def pair(i, last):
                for b in range(2):
                    n = 2 * i + b
                    if last and b == 0:
                        sp.wait_ge(stored[0], STORES)
                        load_keys(sp, a, 0, 0, 0, k_hi_dram, k_lo_dram, v_dram)
                    if not last:
                        sp.wait_ge(c_lo_ready, n + 1)
                        sp.dma_start(c[b][:, :, :], c_view[:, :, bass.ds((n + 2) * CH, CH)]).then_inc(c_loaded[b], 16)
                    cols = bass.ds(n * CH, CH)
                    sp.wait_ge(k_lo_ready, NG * (n + 1))
                    sp.dma_start(k_hi_view[:, :, cols], k_hi[b][:, :, :].bitcast(F32)).then_inc(stored[b], 16)
                    sp.dma_start(k_lo_view[:, :, cols], k_lo[b][:, :, :].bitcast(F32)).then_inc(stored[b], 16)
                    parts = [slice(t, t + 1) for t in range(KT)] if last and b == 1 else [slice(0, KT)]
                    for part in parts:
                        sp.wait_ge(v_ready, KT * n + part.stop)
                        to = v_dram[bass.ds(n * CH + part.start * P, (part.stop - part.start) * P), :]
                        sp.dma_start(to.rearrange("(t p) f -> p t f", p=P), v[b][:, part, :]).then_inc(stored[b], 16)

            for j in range(HG):
                rows = slice(j * D, (j + 1) * D)
                for part, src in enumerate((q_hi, q_hi, q_lo)):
                    dst = q_stack[part * D:(part + 1) * D, :].bitcast(F32).rearrange("d (g j q) -> d g j q", j=HG, q=NQ)
                    sp.dma_start(dst[:, :, j, :], src[rows, :, :].bitcast(F32)).then_inc(a.stacked, 16)
            rolled(sp, PAIRS, pair)
            sp.wait_ge(a.stacked, 16 * 3 * HG)
            sp.wait_ge(stored[0], STORES * PAIRS)
            sp.wait_ge(stored[1], STORES * PAIRS + 16 * (KT - 1))

        @block.gpsimd
        def _(pool):
            nc.gpsimd.memset(a.k[0][3 * D:QROWS, :, :].bitcast(F32), 1.0).then_inc(a.ones_set, 1)

        @block.vector
        def _(dve):
            dve.wait_ge(a.biases, 32)

            def pair(i, last):
                for b in range(2):
                    n = 2 * i + b
                    if not (last and b == 1):
                        split_chunk_low(nc, dve, a, n + 1, 1 - b)
                    for g in range(NG):
                        dve.wait_ge(k_hi_ready, NG * n + g + 1)
                        nc.vector.scalar_tensor_tensor(k_lo[b][:, g, :], kp[g][:, :], bk[:, g:g + 1],
                                                       k_hi[b][:, g, :].bitcast(F32), ALU.add,
                                                       ALU.subtract).then_inc(k_lo_ready, 1)
                    nc.vector.tensor_reduce(k_top[b][:, :], k_hi[b][:, :, :].bitcast(F32), X, ALU.max,
                                            apply_absolute_value=True).then_inc(k_topped, 1)
                    wait_reuse(dve, stored[b], STORES * i)
                    for t in range(KT):
                        dve.wait_ge(v_done, KT * n + t + 1)
                        nc.vector.tensor_tensor(v[b][:, t, :], vp[t][:, :], bv[:, :], ALU.add).then_inc(v_ready, 1)
                    dve.wait_ge(k_topped, n + 1)
                    dve.wait_ge(k_top_kept, n + 1)
                    nc.vector.tensor_tensor(k_top_all[:, :], k_top_all[:, :], k_top[b][:, :], ALU.max).then_inc(k_top_kept, 1)

            nc.vector.memset(k_top_all[:, :], 0.0).then_inc(k_top_kept, 1)
            nc.vector.tensor_reduce(q_top[:, :], q_hi[:, :, :].bitcast(F32), X, ALU.max,
                                    apply_absolute_value=True).then_inc(q_topped, 1)
            rolled(dve, PAIRS, pair)
            dve.wait_ge(k_top_kept, NCH + 1)
            dve.wait_ge(q_topped, 1)
            nc.vector.tensor_tensor(product[:, :], q_top[:, :], k_top_all[:, :], ALU.mult).then_inc(product_ready, 1)
            dve.wait_ge(bound_done, 1)
            nc.vector.reduce_max(bound[:, :], kp[0][0:1, 0:H], X).then_inc(bound_ready, 1)
            dve.wait_ge(bound_ready, 1)
            nc.vector.tensor_scalar(bounded[:, :], bound[:, :], SAFE / SCALE, None, ALU.is_le).then_inc(flagged, 1)

        @block.tensor
        def _(pe):
            def pair(i, last):
                for b in range(2):
                    n = 2 * i + b
                    pe.wait_ge(c_lo_ready, n + 1)
                    wait_reuse(pe, k_lo_ready, NG * n)
                    for g in range(NG):
                        for a, (lhs, rhs) in enumerate(((w_hi, c_hi), (w_lo, c_hi), (w_hi, c_lo))):
                            for d in range(ET):
                                last = nc.tensor.matmul(kp[g][:, :], lhs[:, d, g * P:(g + 1) * P], rhs[b][:, d, :],
                                                        start=(a == 0 and d == 0), stop=(a == 2 and d == ET - 1))
                        last.then_inc(k_done, 1)
                    wait_reuse(pe, v_ready, KT * n)
                    for t in range(KT):
                        for a, (lhs, rhs) in enumerate(((c_hi, w_hi), (c_lo, w_hi), (c_hi, w_lo))):
                            for d in range(ET):
                                last = nc.tensor.matmul(vp[t][:, :], lhs[b][:, d, t * P:(t + 1) * P], rhs[:, d, E:2 * E],
                                                        start=(a == 0 and d == 0), stop=(a == 2 and d == ET - 1))
                        last.then_inc(v_done, 1)

            rolled(pe, PAIRS, pair)
            pe.wait_ge(product_ready, 1)
            for g in range(NG):
                last = nc.tensor.matmul(kp[0][0:1, g * HG:(g + 1) * HG], product[:, g:g + 1], head_rows[:, :],
                                        start=True, stop=True)
            last.then_inc(bound_done, 1)

        @block.scalar
        def _(act):
            act.wait_ge(a.biases, 32)

            def pair(i, last):
                for b in range(2):
                    n = 2 * i + b
                    if not (last and b == 1):
                        wait_reuse(act, v_done, KT * n)
                        split_chunk_high(nc, act, a, n + 1, i + b, 1 - b)
                    wait_reuse(act, k_topped, n - 1)
                    wait_reuse(act, stored[b], STORES * i)
                    for g in range(NG):
                        act.wait_ge(k_done, NG * n + g + 1)
                        nc.scalar.activation(k_hi[b][:, g, :], kp[g][:, :], ACT.Identity,
                                             bias=bk[:, g:g + 1]).then_inc(k_hi_ready, 1)

            rolled(act, PAIRS, pair)


def find_maxima(nc, ctx, k_hi_dram, k_lo_dram, ident, q_stack, bounded):
    sb = lambda n, s, d=F32: ctx.enter_context(nc.sbuf_tensor(n, s, d))
    sem = lambda n: ctx.enter_context(nc.semaphore(n))
    KB = 2048
    NKB = NK // KB
    UNITS = NKB * QT
    q = [sb(f"fm_q{b}", [3 * D, NQ], F32R) for b in range(2)]
    k = [sb(f"fm_k{b}", [3 * D, NK], F32R) for b in range(2)]
    block_max = [sb(f"fm_block_max{b}", [P, QT, NKB]) for b in range(2)]
    head_max = [sb(f"fm_head_max{b}", [P, QT]) for b in range(2)]
    minus_max = sb("fm_minus_max", [P, H * QT])
    minus_row = sb("fm_minus_row", [H * QT, P], F32R)
    s = [ctx.enter_context(nc.psum_tensor(f"fm_s{r}", [P, KB], F32)) for r in range(2)]
    loaded = [sem(f"fm_loaded{b}") for b in range(2)]
    head_reduced = [sem(f"fm_head_reduced{b}") for b in range(2)]
    scored = [sem(f"fm_scored{r}") for r in range(2)]
    reduced = [sem(f"fm_reduced{r}") for r in range(2)]
    negated, turned, row_ready, placed = map(sem, (
        "fm_negated", "fm_turned", "fm_row_ready", "fm_placed"))
    LOADS = 4 * 16
    PER = UNITS // 2

    with nc.Block() as block:
        @block.sync
        def _(sp):
            flag = sp.value_load(bounded[:, :], min_val=0, max_val=1)
            with sp.If(flag < 1):
                def pair(i, last):
                    for b in range(2):
                        h = 2 * i + b
                        rows = bass.ds(h * D, D)
                        wait_reuse(sp, head_reduced[b], i)
                        sp.dma_start(q[b][:, :].bitcast(F32),
                                     q_stack[0:3 * D, bass.ds(h * NQ, NQ)].bitcast(F32)).then_inc(loaded[b], 16)
                        sp.dma_start(k[b][0:D, :].bitcast(F32), k_hi_dram[rows, :]).then_inc(loaded[b], 16)
                        sp.dma_start(k[b][D:2 * D, :].bitcast(F32), k_lo_dram[rows, :]).then_inc(loaded[b], 16)
                        sp.dma_start(k[b][2 * D:3 * D, :].bitcast(F32), k_hi_dram[rows, :]).then_inc(loaded[b], 16)
                rolled(sp, H // 2, pair)
                sp.wait_ge(row_ready, 1)
                sp.dma_start(q_stack[3 * D:QROWS, :].bitcast(F32), minus_row[:, :].bitcast(F32)).then_inc(placed, 16)
                sp.wait_ge(placed, 16)

        @block.tensor
        def _(pe):
            flag = pe.value_load(bounded[:, :], min_val=0, max_val=1)
            with pe.If(flag < 1):
                def pair(i, last):
                    for b in range(2):
                        h = 2 * i + b
                        pe.wait_ge(loaded[b], LOADS * (i + 1))
                        for u in range(UNITS):
                            kb, qt, r = u // QT, u % QT, u % 2
                            wait_reuse(pe, reduced[r], PER * h + u // 2)
                            for n in range(KB // 512):
                                cols = slice(kb * KB + n * 512, kb * KB + (n + 1) * 512)
                                last = nc.tensor.matmul(s[r][:, n * 512:(n + 1) * 512], q[b][:, qt * P:(qt + 1) * P],
                                                        k[b][:, cols], start=True, stop=True)
                            last.then_inc(scored[r], 1)
                rolled(pe, H // 2, pair)
                pe.wait_ge(negated, H)
                nc.tensor.transpose(s[0][0:H * QT, 0:P], minus_max[:, :], ident[:, :]).then_inc(turned, 1)

        @block.vector
        def _(dve):
            flag = dve.value_load(bounded[:, :], min_val=0, max_val=1)
            with dve.If(flag < 1):
                with dve.Fori(0, H // 2) as i:
                    for b in range(2):
                        h = 2 * i + b
                        for u in range(UNITS):
                            kb, qt, r = u // QT, u % QT, u % 2
                            dve.wait_ge(scored[r], PER * h + u // 2 + 1)
                            nc.vector.reduce_max(block_max[b][:, qt, kb:kb + 1], s[r][:, :], X).then_inc(reduced[r], 1)
                        for r in range(2):
                            dve.wait_ge(reduced[r], PER * (h + 1))
                        nc.vector.reduce_max(head_max[b][:, :], block_max[b][:, :, :], X).then_inc(head_reduced[b], 1)
                        dve.wait_ge(head_reduced[b], i + 1)
                        nc.vector.tensor_scalar(minus_max[:, bass.ds(h * QT, QT)], head_max[b][:, :], -1.0, None,
                                                ALU.mult).then_inc(negated, 1)

        @block.scalar
        def _(act):
            flag = act.value_load(bounded[:, :], min_val=0, max_val=1)
            with act.If(flag < 1):
                act.wait_ge(turned, 1)
                nc.scalar.activation(minus_row[:, :], s[0][0:H * QT, 0:P], ACT.Copy).then_inc(row_ready, 1)


def load_keys(sp, a, c, g, chunk, k_hi_dram, k_lo_dram, v_dram):
    keys, feats = bass.ds(chunk * CH, CH), bass.ds(g * P, P)
    hi = k_hi_dram[feats, keys].rearrange("(j d) n -> d j n", d=D)
    lo = k_lo_dram[feats, keys].rearrange("(j d) n -> d j n", d=D)
    for part, src in enumerate((hi, lo, hi)):
        sp.dma_start(a.k[c][part * D:(part + 1) * D, :, :].bitcast(F32), src).then_inc(a.loaded[c], 16)
    sp.dma_start(a.v[c][:, :, :], v_dram[keys, feats].rearrange("(t p) f -> p t f", p=P)).then_inc(a.loaded[c], 16)


def attend(nc, ctx, k_hi_dram, k_lo_dram, v_dram, q_stack, o_acc, p_sum, total_acc, a, late, late_dram):
    sb = lambda n, s, d=F32: ctx.enter_context(nc.sbuf_tensor(n, s, d))
    sem = lambda n: ctx.enter_context(nc.semaphore(n))
    CB = 4
    TILES = CB * KT
    ITERS = NG * NCH // CB
    PER_GROUP = NCH // CB
    BY_PE = (4, 9, 15)
    SR, PR = 3, 4
    AHEAD = 3
    TPR = TILES // PR
    LOADS = 4 * 16
    a.k += [sb(f"at_k{c}", [QROWS, HG, CH], F32R) for c in range(1, CB)]
    a.v += [sb(f"at_v{c}", [P, KT, P]) for c in range(1, CB)]
    a.loaded += [sem(f"at_loaded{c}") for c in range(1, CB)]
    k, v, loaded, ones_set = a.k, a.v, a.loaded, a.ones_set
    p = [sb(f"at_p{r}", [P, HG * NQ]) for r in range(PR)]
    s = [ctx.enter_context(nc.psum_tensor(f"at_s{r}", [P, 2 * NQ], F32)) for r in range(SR)]
    o = ctx.enter_context(nc.psum_tensor("at_o", [P, NQ], F32))
    totals = ctx.enter_context(nc.psum_tensor("at_totals", [P, NQ], F32))
    ones = sb("at_ones", [P, D])
    zeroed, first_zeroed = map(sem, ("at_zeroed", "at_first_zeroed"))
    s_ready = [sem(f"at_s_ready{r}") for r in range(SR)]
    p_ready = [sem(f"at_p_ready{r}") for r in range(PR)]
    p_used = [sem(f"at_p_used{r}") for r in range(PR)]
    p_summed = [sem(f"at_p_summed{r}") for r in range(PR)]
    o_done, o_added, totals_added = map(sem, ("at_o_done", "at_o_added", "at_totals_added"))
    s_uses = [len(range(r, 2 * TILES, SR)) for r in range(SR)]
    s_last = [max(range(r, 2 * TILES, SR)) for r in range(SR)]

    def exped(it, u):
        return 2 * TPR * it + 2 * (u // 2 // PR) + u % 2 + 1

    def used(it, t):
        return TPR * it + t // PR + 1

    def summed(it, t):
        mine = [w for w in range(t % PR, TILES, PR) if w not in BY_PE]
        return len(mine) * it + (sum(w <= t for w in mine) if t >= 0 else -sum(w > t + TILES for w in mine))

    with nc.Block() as block:
        @block.gpsimd
        def _(pool):
            for c in range(1, CB):
                pool.wait_ge(ones_set, c)
                nc.gpsimd.memset(k[c][3 * D:QROWS, :, :].bitcast(F32), 1.0).then_inc(ones_set, 1)
            pool.wait_ge(ones_set, CB)
            nc.gpsimd.memset(ones[:, :], 1.0).then_inc(ones_set, 1)
            pool.wait_ge(ones_set, CB + 1)
            nc.gpsimd.memset(p_sum[:, HG * NQ:], 0.0).then_inc(zeroed, 1)
            pool.wait_ge(zeroed, 1)
            nc.gpsimd.memset(o_acc[:, :, :], 0.0).then_inc(zeroed, 1)
            pool.wait_ge(zeroed, 2)
            nc.gpsimd.memset(total_acc[:, :, :], 0.0).then_inc(zeroed, 1)

        @block.sync
        def _(sp):
            def iteration(it, last):
                for c in range(CB):
                    end = (c + 1) * KT - 1
                    wait_reuse(sp, p_used[end % PR], used(it, end) - TPR)
                    if c > 0 or not (isinstance(it, int) and it == 0):
                        load_keys(sp, a, c, it // PER_GROUP, it % PER_GROUP * CB + c, k_hi_dram, k_lo_dram, v_dram)
                if isinstance(it, int) and it == 0:
                    for to, src in zip(late, late_dram):
                        sp.dma_start(to, src).then_inc(a.late_loaded, 16)

            rolled(sp, ITERS, iteration)
            sp.wait_ge(a.late_loaded, 16 * len(late))

        @block.tensor
        def _(pe):
            def scores(it, u):
                c, t, pair, r = u // 2 // KT, u // 2 % KT, u % 2, u % SR
                if t == 0 and pair == 0:
                    pe.wait_ge(loaded[c], LOADS * (it + 1))
                    if isinstance(it, int) and it == 0:
                        pe.wait_ge(ones_set, c + 1)
                if u >= SR:
                    pe.wait_ge(p_ready[(u - SR) // 2 % PR], exped(it, u - SR))
                else:
                    wait_reuse(pe, p_ready[s_last[r] // 2 % PR], exped(it, s_last[r]) - 2 * TPR)
                for a in range(2):
                    j = 2 * pair + a
                    last = nc.tensor.matmul(s[r][:, a * NQ:(a + 1) * NQ], k[c][:, j, t * P:(t + 1) * P],
                                            q_stack[:, bass.ds(it // PER_GROUP * (HG * NQ) + j * NQ, NQ)],
                                            start=True, stop=True)
                last.then_inc(s_ready[r], 1)

            def outputs(it, t):
                c, r = t // KT, t % PR
                if t == 0:
                    wait_reuse(pe, o_added, it)
                if t == BY_PE[0]:
                    wait_reuse(pe, totals_added, it)
                pe.wait_ge(p_ready[r], exped(it, 2 * t + 1))
                for j in range(HG):
                    last = nc.tensor.matmul(o[j * D:(j + 1) * D, :], v[c][:, t % KT, j * D:(j + 1) * D],
                                            p[r][:, j * NQ:(j + 1) * NQ], start=(t == 0), stop=(t == TILES - 1))
                if t == TILES - 1:
                    last.then_inc(o_done, 1)
                if t in BY_PE:
                    if isinstance(it, int) and it == 0:
                        pe.wait_ge(ones_set, CB + 1)
                    for j in range(HG):
                        last = nc.tensor.matmul(totals[j * D:(j + 1) * D, :], ones[:, :], p[r][:, j * NQ:(j + 1) * NQ],
                                                start=(t == BY_PE[0]), stop=(t == BY_PE[-1]))
                last.then_inc(p_used[r], 1)

            def iteration(it, last):
                for t in range(TILES):
                    for u in (2 * t + AHEAD, 2 * t + AHEAD + 1):
                        if u < 2 * TILES:
                            scores(it, u)
                        elif not last:
                            scores(it + 1, u - 2 * TILES)
                    outputs(it, t)

            for u in range(AHEAD):
                scores(0, u)
            rolled(pe, ITERS, iteration)

        @block.scalar
        def _(act):
            def iteration(it, last):
                for u in range(2 * TILES):
                    t, pair = u // 2, u % 2
                    if pair == 0:
                        wait_reuse(act, p_used[t % PR], used(it, t) - 1)
                        wait_reuse(act, p_summed[t % PR], summed(it, t - PR))
                    act.wait_ge(s_ready[u % SR], s_uses[u % SR] * it + u // SR + 1)
                    nc.scalar.activation(p[t % PR][:, pair * 2 * NQ:(pair + 1) * 2 * NQ], s[u % SR][:, :], ACT.Exp,
                                         scale=SCALE).then_inc(p_ready[t % PR], 1)

            rolled(act, ITERS, iteration)

        @block.vector
        def _(dve):
            nc.vector.memset(p_sum[:, 0:HG * NQ], 0.0).then_inc(first_zeroed, 1)
            dve.wait_ge(first_zeroed, 1)

            def iteration(it, last):
                g = it // PER_GROUP
                sums = p_sum[:, bass.ds(g * (HG * NQ), HG * NQ)]
                for t in range(TILES):
                    if t in BY_PE:
                        continue
                    before = max(w for w in range(-TILES, t) if w % TILES not in BY_PE)
                    wait_reuse(dve, p_summed[before % PR], summed(it, before))
                    dve.wait_ge(p_ready[t % PR], exped(it, 2 * t + 1))
                    nc.vector.tensor_tensor(sums, sums, p[t % PR][:, :], ALU.add).then_inc(p_summed[t % PR], 1)
                if isinstance(it, int) and it == 0:
                    dve.wait_ge(zeroed, 3)
                for bank, acc, added in ((o, o_acc, o_added), (totals, total_acc, totals_added)):
                    if bank is o:
                        dve.wait_ge(o_done, it + 1)
                    else:
                        dve.wait_ge(p_used[BY_PE[-1] % PR], used(it, BY_PE[-1]))
                    wait_reuse(dve, added, it)
                    nc.vector.tensor_tensor(acc[:, bass.ds(g, 1), :], acc[:, bass.ds(g, 1), :],
                                            bank[:, :].rearrange("p (a q) -> p a q", a=1), ALU.add).then_inc(added, 1)

            rolled(dve, ITERS, iteration)


def cross_output(nc, ctx, wo, bo, o_acc, p_sum, total_acc, x_sb):
    sb = lambda n, s, d=F32: ctx.enter_context(nc.sbuf_tensor(n, s, d))
    sem = lambda n: ctx.enter_context(nc.semaphore(n))
    ones = sb("co_ones", [P, D])
    log = sb("co_log", [P, NG, NQ])
    table_loader = sb("co_table_loader", [P, 1])
    guess = sb("co_guess", [P, NG, NQ])
    error = sb("co_error", [P, NG, NQ])
    minus_rec = sb("co_minus_rec", [P, NG, NQ])
    heads = sb("co_heads", [P, NG, NQ])
    total = [ctx.enter_context(nc.psum_tensor(f"co_total{g}", [P, NQ], F32)) for g in range(NG)]
    out = [ctx.enter_context(nc.psum_tensor(f"co_out{t}", [P, E], F32)) for t in range(QT)]
    ones_set, totalled, summed, logged, guessed, checked, inverted, normed, biased, projected, added, loaded_table = map(sem, (
        "co_ones_set", "co_totalled", "co_summed", "co_logged", "co_guessed", "co_checked", "co_inverted", "co_normed",
        "co_biased", "co_projected", "co_added", "co_loaded_table"))

    with nc.Block() as block:
        @block.gpsimd
        def _(pool):
            nc.gpsimd.memset(ones[:, :], 1.0).then_inc(ones_set, 1)

        @block.tensor
        def _(pe):
            pe.wait_ge(ones_set, 1)
            for g in range(NG):
                for j in range(HG):
                    h = g * HG + j
                    last = nc.tensor.matmul(total[g][j * D:(j + 1) * D, :], ones[:, :], p_sum[:, h * NQ:(h + 1) * NQ],
                                            start=True, stop=True)
                last.then_inc(totalled, 1)
            for g in range(NG):
                pe.wait_ge(normed, g + 1)
                for t in range(QT):
                    last = nc.tensor.matmul(out[t][:, :], heads[:, g, t * P:(t + 1) * P], wo[:, g, :],
                                            start=(g == 0), stop=(g == NG - 1))
                    if g == NG - 1:
                        last.then_inc(projected, 1)

        @block.scalar
        def _(act):
            act.wait_ge(ones_set, 1)
            nc.scalar.activation(table_loader[:, :], ones[:, 0:1], ACT.Ln).then_inc(loaded_table, 1)
            for g in range(NG):
                act.wait_ge(summed, g + 1)
                nc.scalar.activation(log[:, g, :], total_acc[:, g, :], ACT.Ln).then_inc(logged, 1)
            for g in range(NG):
                act.wait_ge(logged, g + 1)
                nc.scalar.activation(guess[:, g, :], log[:, g, :], ACT.Exp, scale=-1.0).then_inc(guessed, 1)

        @block.vector
        def _(dve):
            for g in range(NG):
                dve.wait_ge(totalled, g + 1)
                nc.vector.tensor_tensor(total_acc[:, g, :], total_acc[:, g, :], total[g][:, :], ALU.add).then_inc(summed, 1)
            for g in range(NG):
                dve.wait_ge(guessed, g + 1)
                nc.vector.tensor_tensor(error[:, g, :], total_acc[:, g, :], guess[:, g, :], ALU.mult).then_inc(checked, 1)
                dve.wait_ge(checked, g + 1)
                nc.vector.scalar_tensor_tensor(minus_rec[:, g, :], error[:, g, :], 2.0, guess[:, g, :], ALU.subtract,
                                               ALU.mult).then_inc(inverted, 1)
                dve.wait_ge(inverted, g + 1)
                nc.vector.scalar_tensor_tensor(heads[:, g, :], o_acc[:, g, :], -1.0, minus_rec[:, g, :], ALU.mult,
                                               ALU.mult).then_inc(normed, 1)
            for t in range(QT):
                nc.vector.tensor_tensor(x_sb[:, t, :], x_sb[:, t, :], bo[:, :], ALU.add).then_inc(biased, 1)
            for t in range(QT):
                dve.wait_ge(projected, t + 1)
                dve.wait_ge(biased, t + 1)
                nc.vector.tensor_tensor(x_sb[:, t, :], x_sb[:, t, :], out[t][:, :], ALU.add).then_inc(added, 1)


def self_attention(nc, ctx, wv, bv, wo, bo, ident, x_sb, prefetch):
    sb = lambda n, s, d=F32: ctx.enter_context(nc.sbuf_tensor(n, s, d))
    sem = lambda n: ctx.enter_context(nc.semaphore(n))
    xn = sb("sa_xn", [P, QT, E])
    wv_hi, wv_lo, wo_hi, wo_lo = (sb(f"sa_{n}", [P, ET, E], F32R) for n in ("wv_hi", "wv_lo", "wo_hi", "wo_lo"))
    xt_hi, xt_lo, vt_hi, vt_lo = (sb(f"sa_{n}", [P, ET, NQ], F32R) for n in ("xt_hi", "xt_lo", "vt_hi", "vt_lo"))
    stats = sb("sa_stats", [P, QT, 6])
    mv = sb("sa_mv", [P, QT, 2])
    var = sb("sa_var", [P, QT])
    root = sb("sa_root", [P, QT])
    rstd = sb("sa_rstd", [P, 5, QT])
    var_ready, root_ready = map(sem, ("sa_var_ready", "sa_root_ready"))
    turn = [ctx.enter_context(nc.psum_tensor(f"sa_turn{d}", [P, NQ], F32)) for d in range(ET)]
    proj = [ctx.enter_context(nc.psum_tensor(f"sa_proj{d}", [P, NQ], F32)) for d in range(ET)]
    chain, normed, turned, xt_ready, v_done, v_ready, biased, projected, added = map(sem, (
        "sa_chain", "sa_normed", "sa_turned", "sa_xt_ready", "sa_v_done", "sa_v_ready",
        "sa_biased", "sa_projected", "sa_added"))

    w_hi_ready, wv_lo_ready, wo_lo_ready, xt_lo_ready, vt_hi_ready = map(sem, (
        "sa_w_hi_ready", "sa_wv_lo_ready", "sa_wo_lo_ready", "sa_xt_lo_ready", "sa_vt_hi_ready"))

    with nc.Block() as block:
        @block.sync
        def _(sp):
            prefetch(sp)

        @block.tensor
        def _(pe):
            norm_transpose(nc, pe, xn, ident, turn, normed, turned)
            pe.wait_ge(xt_ready, ET)
            for f in range(ET):
                for a, (lhs, rhs) in enumerate(((wv_hi, xt_hi), (wv_lo, xt_hi), (wv_hi, xt_lo))):
                    if f == 0 and a == 1:
                        pe.wait_ge(wv_lo_ready, 1)
                    if f == 0 and a == 2:
                        pe.wait_ge(xt_lo_ready, ET)
                    for d in range(ET):
                        last = nc.tensor.matmul(proj[f][:, :], lhs[:, d, f * P:(f + 1) * P], rhs[:, d, :],
                                                start=(a == 0 and d == 0), stop=(a == 2 and d == ET - 1))
                last.then_inc(v_done, 1)
            pe.wait_ge(wo_lo_ready, 1)
            for f in range(ET):
                pe.wait_ge(v_ready, f + 1)
                for t in range(QT):
                    for a, (lhs, rhs) in enumerate(((vt_hi, wo_hi), (vt_lo, wo_hi), (vt_hi, wo_lo))):
                        last = nc.tensor.matmul(turn[t][:, :], lhs[:, f, t * P:(t + 1) * P], rhs[:, f, :],
                                                start=(f == 0 and a == 0), stop=(f == ET - 1 and a == 2))
                    if f == ET - 1:
                        last.then_inc(projected, 1)

        @block.scalar
        def _(act):
            nc.scalar.activation(wv_hi[:, :, :], wv[:, :, :], ACT.Copy).then_inc(w_hi_ready, 1)
            norm_scalar(nc, act, var, root, var_ready, root_ready)
            nc.scalar.activation(wo_hi[:, :, :], wo[:, :, :], ACT.Copy).then_inc(w_hi_ready, 1)
            act.wait_ge(turned, 1)
            for d in range(ET):
                nc.scalar.activation(xt_hi[:, d, :], turn[d][:, :], ACT.Copy).then_inc(xt_ready, 1)
            for f in range(ET):
                act.wait_ge(v_done, f + 1)
                nc.scalar.activation(vt_hi[:, f, :], proj[f][:, :], ACT.Identity, bias=bv[:, f:f + 1]).then_inc(vt_hi_ready, 1)

        @block.vector
        def _(dve):
            norm_vector(nc, dve, x_sb, xn, stats, mv, var, root, rstd, chain, var_ready, root_ready, normed)
            dve.wait_ge(w_hi_ready, 1)
            nc.vector.tensor_tensor(wv_lo[:, :, :], wv[:, :, :], wv_hi[:, :, :].bitcast(F32),
                                    ALU.subtract).then_inc(wv_lo_ready, 1)
            for d in range(ET):
                dve.wait_ge(xt_ready, d + 1)
                nc.vector.tensor_tensor(xt_lo[:, d, :], turn[d][:, :], xt_hi[:, d, :].bitcast(F32),
                                        ALU.subtract).then_inc(xt_lo_ready, 1)
            dve.wait_ge(w_hi_ready, 2)
            nc.vector.tensor_tensor(wo_lo[:, :, :], wo[:, :, :], wo_hi[:, :, :].bitcast(F32),
                                    ALU.subtract).then_inc(wo_lo_ready, 1)
            for f in range(ET):
                dve.wait_ge(vt_hi_ready, f + 1)
                nc.vector.scalar_tensor_tensor(vt_lo[:, f, :], proj[f][:, :], bv[:, f:f + 1], vt_hi[:, f, :].bitcast(F32),
                                               ALU.add, ALU.subtract).then_inc(v_ready, 1)
            for t in range(QT):
                dve.wait_ge(normed, t + 1)
                nc.vector.tensor_tensor(x_sb[:, t, :], x_sb[:, t, :], bo[:, :], ALU.add).then_inc(biased, 1)
            for t in range(QT):
                dve.wait_ge(projected, t + 1)
                dve.wait_ge(biased, t + 1)
                nc.vector.tensor_tensor(x_sb[:, t, :], x_sb[:, t, :], turn[t][:, :], ALU.add).then_inc(added, 1)


def route(nc, ctx, w_gate, b_out, ident, x_sb, r):
    retired = list(nc.released_uncleared_semaphores)
    sb = lambda n, s, d=F32: ctx.enter_context(nc.sbuf_tensor(n, s, d))
    sem = lambda n: ctx.enter_context(nc.semaphore(n))
    xn = sb("ro_xn", [P, QT, E])
    xt = sb("ro_xt", [P, ET, NQ])
    stats = sb("ro_stats", [P, QT, 6])
    mv = sb("ro_mv", [P, QT, 2])
    var = sb("ro_var", [P, QT])
    root = sb("ro_root", [P, QT])
    rstd = sb("ro_rstd", [P, 5, QT])
    wg = sb("ro_wg", [P, ET, NX])
    before = sb("ro_before", [P, P])
    every = sb("ro_every", [P, P])
    logits = sb("ro_logits", [P, QT, NX])
    sorted8 = sb("ro_sorted8", [P, QT, NX])
    places = sb("ro_places", [P, QT, NX], U32)
    places_f = sb("ro_places_f", [P, QT, NX])
    gap = sb("ro_gap", [P, QT])
    ratio = sb("ro_ratio", [P, QT])
    weight = sb("ro_weight", [P, 2, QT])
    first = sb("ro_first", [P, QT, NX])
    second = sb("ro_second", [P, QT, NX])
    longest = sb("ro_longest", [1, 1])
    turn = [ctx.enter_context(nc.psum_tensor(f"ro_turn{t}", [P, NQ], F32)) for t in range(ET)]
    gate = ctx.enter_context(nc.psum_tensor("ro_gate", [P, QT * NX], F32))
    ranks = ctx.enter_context(nc.psum_tensor("ro_ranks", [P, (QT + 1) * NX], F32))
    turned_weights = ctx.enter_context(nc.psum_tensor("ro_turned_weights", [NX, NQ], F32))
    var_ready, root_ready, small, chain, normed, turned, xt_ready = map(sem, (
        "ro_var_ready", "ro_root_ready", "ro_small", "ro_chain", "ro_normed", "ro_turned", "ro_xt_ready"))
    made, gated, link, gap_ready, ratio_ready, masked = map(sem, (
        "ro_made", "ro_gated", "ro_link", "ro_gap_ready", "ro_ratio_ready", "ro_masked"))
    weights_turned, combine_t_ready, ranked, hi_ready, done = map(sem, (
        "ro_weights_turned", "ro_combine_t_ready", "ro_ranked", "ro_hi_ready", "ro_done"))

    with nc.Block() as block:
        @block.sync
        def _(sp):
            sp.dma_start(wg[:, :, :], w_gate.rearrange("(t p) e -> p t e", p=P)).then_inc(small, 16)
            sp.dma_start(r.bo[:, :], b_out).then_inc(small, 16)

        @block.gpsimd
        def _(pool):
            for first in (n for n in retired if n - 1 not in retired):
                end = next(n for n in range(first, first + len(retired) + 1) if n not in retired)
                nc.gpsimd.sem_clear(range(first, end))
            rounds = r.numbers[:, :].rearrange("p (r n) -> p r n", n=COLS)
            nc.gpsimd.iota(rounds[:, :, 0:P], pattern=[[SLOTS, ROUNDS], [1, P]], base=0, channel_multiplier=0,
                           allow_small_or_imprecise_dtypes=True).then_inc(made, 1)
            for copy in range(2):
                pool.wait_ge(made, copy + 1)
                nc.gpsimd.iota(rounds[:, :, P + copy * PAIRED:P + (copy + 1) * PAIRED], pattern=[[SLOTS, ROUNDS], [1, PAIRED]],
                               base=P, channel_multiplier=0, allow_small_or_imprecise_dtypes=True).then_inc(made, 1)
            pool.wait_ge(made, 3)
            nc.gpsimd.memset(every[:, :], 1.0).then_inc(made, 1)
            pool.wait_ge(made, 4)
            nc.gpsimd.affine_select(out=before[:, :], in_=every[:, :], compare_op=ALU.is_gt, fill=0.0,
                                    base=0, pattern=[[1, P]], channel_multiplier=-1).then_inc(made, 1)

        @block.tensor
        def _(pe):
            norm_transpose(nc, pe, xn, ident, turn, normed, turned)
            pe.wait_ge(small, 32)
            pe.wait_ge(xt_ready, ET)
            for t in range(QT):
                for d in range(ET):
                    last = nc.tensor.matmul(gate[:, t * NX:(t + 1) * NX], xt[:, d, t * P:(t + 1) * P], wg[:, d, :],
                                            start=(d == 0), stop=(d == ET - 1))
            last.then_inc(gated, 1)
            pe.wait_ge(made, 5)
            pe.wait_ge(masked, 1)
            for t in range(QT + 1):
                for u in range(min(t + 1, QT)):
                    last = nc.tensor.matmul(ranks[:, t * NX:(t + 1) * NX], (before if u == t else every)[:, :],
                                            r.mask[:, u, :], start=(u == 0), stop=(u == min(t, QT - 1)))
            last.then_inc(ranked, 1)
            pe.wait_ge(link, 5 + 6 * QT)
            for t in range(QT):
                last = nc.tensor.transpose(turned_weights[:, t * P:(t + 1) * P], r.combine[:, t, :], ident[:, :])
            last.then_inc(weights_turned, 1)

        @block.scalar
        def _(act):
            norm_scalar(nc, act, var, root, var_ready, root_ready)
            act.wait_ge(turned, 1)
            for d in range(ET):
                nc.scalar.activation(xt[:, d, :], turn[d][:, :], ACT.Copy).then_inc(xt_ready, 1)
            nc.scalar.activation(r.x_hi[:, :, :], xn[:, :, :], ACT.Copy).then_inc(hi_ready, 1)
            act.wait_ge(gap_ready, 1)
            nc.scalar.activation(ratio[:, :], gap[:, :], ACT.Exp).then_inc(ratio_ready, 1)
            act.wait_ge(weights_turned, 1)
            nc.scalar.activation(r.combine_t[:, :], turned_weights[:, :], ACT.Copy).then_inc(combine_t_ready, 1)

        @block.vector
        def _(dve):
            norm_vector(nc, dve, x_sb, xn, stats, mv, var, root, rstd, chain, var_ready, root_ready, normed)
            dve.wait_ge(gated, 1)
            nc.vector.tensor_copy(logits[:, :, :], gate[:, :].rearrange("p (t e) -> p t e", e=NX)).then_inc(link, 1)
            dve.wait_ge(link, 1)
            for t in range(QT):
                nc.vector.max(sorted8[:, t, :], logits[:, t, :]).then_inc(link, 1)
            dve.wait_ge(link, 1 + QT)
            nc.vector.tensor_tensor(gap[:, :], sorted8[:, :, 1], sorted8[:, :, 0], ALU.subtract).then_inc(gap_ready, 1)
            for t in range(QT):
                nc.vector.max_index(places[:, t, :], sorted8[:, t, :], logits[:, t, :]).then_inc(link, 1)
            dve.wait_ge(link, 1 + 2 * QT)
            nc.vector.tensor_copy(places_f[:, :, :], places[:, :, :]).then_inc(link, 1)
            dve.wait_ge(made, 1)
            dve.wait_ge(link, 2 + 2 * QT)
            for t in range(QT):
                for place, chosen in enumerate((first, second)):
                    nc.vector.tensor_scalar(chosen[:, t, :], r.numbers[:, 0:NX], places_f[:, t, place:place + 1], None,
                                            ALU.is_equal).then_inc(link, 1)
            dve.wait_ge(link, 2 + 4 * QT)
            nc.vector.tensor_tensor(r.mask[:, :, :], first[:, :, :], second[:, :, :], ALU.add).then_inc(masked, 1)
            dve.wait_ge(ratio_ready, 1)
            nc.vector.tensor_scalar(weight[:, 1, :], ratio[:, :], 1.0, None, ALU.add).then_inc(link, 1)
            dve.wait_ge(link, 3 + 4 * QT)
            nc.vector.reciprocal(weight[:, 0, :], weight[:, 1, :]).then_inc(link, 1)
            dve.wait_ge(link, 4 + 4 * QT)
            nc.vector.tensor_tensor(weight[:, 1, :], weight[:, 0, :], ratio[:, :], ALU.mult).then_inc(link, 1)
            dve.wait_ge(link, 5 + 4 * QT)
            for t in range(QT):
                nc.vector.tensor_scalar(second[:, t, :], second[:, t, :], weight[:, 1, t:t + 1], None, ALU.mult).then_inc(link, 1)
            dve.wait_ge(masked, 1)
            dve.wait_ge(link, 5 + 5 * QT)
            for t in range(QT):
                nc.vector.scalar_tensor_tensor(r.combine[:, t, :], first[:, t, :], weight[:, 0, t:t + 1], second[:, t, :],
                                               ALU.mult, ALU.add).then_inc(link, 1)
            dve.wait_ge(hi_ready, 1)
            nc.vector.tensor_tensor(r.x_lo[:, :, :], xn[:, :, :], r.x_hi[:, :, :].bitcast(F32), ALU.subtract).then_inc(done, 1)
            dve.wait_ge(ranked, 1)
            nc.vector.tensor_copy(r.rank[:, :, :], ranks[:, 0:QT * NX].rearrange("p (t e) -> p t e", e=NX)).then_inc(done, 1)
            nc.vector.reduce_max(longest[:, :], ranks[0:1, QT * NX:(QT + 1) * NX], X).then_inc(link, 1)
            dve.wait_ge(link, 6 + 6 * QT)
            nc.vector.tensor_scalar(r.long[:, :], longest[:, :], float(SLOTS), None, ALU.is_gt).then_inc(done, 1)


class ExpertInputs:

    def __init__(self, nc, ctx):
        sb = lambda n, s: ctx.enter_context(nc.sbuf_tensor(n, s, F32))
        self.b_hidden = sb("ei_b_hidden", [P, NX, M // P])
        self.wi = [sb(f"ei_wi{b}", [P, ET, MC]) for b in range(2)]
        self.wo = [sb(f"ei_wo{b}", [P, MT, E]) for b in range(2)]

    def name_semaphores(self, nc, ctx, first_round):
        sem = lambda n: ctx.enter_context(nc.semaphore(f"ei{first_round}_{n}"))
        self.biases = sem("biases")
        self.wi_loaded = [sem(f"wi_loaded{b}") for b in range(2)]
        self.wo_loaded = [sem(f"wo_loaded{b}") for b in range(2)]

    def load_in(self, sp, w_in, e, mc):
        sp.dma_start(self.wi[mc % 2][:, :, :], w_in[bass.ds(e * E, E), mc * MC:(mc + 1) * MC]
                     .rearrange("(t p) m -> p t m", p=P)).then_inc(self.wi_loaded[mc % 2], 16)

    def load_out(self, sp, w_out, e, mc):
        sp.dma_start(self.wo[mc % 2][:, :, :], w_out[bass.ds(e * M + mc * MC, MC), :]
                     .rearrange("(t p) f -> p t f", p=P)).then_inc(self.wo_loaded[mc % 2], 16)

    def load_first(self, sp, w_in, b_in, w_out):
        sp.dma_start(self.b_hidden[:, :, :], b_in).then_inc(self.biases, 16)
        for mc in range(2):
            self.load_in(sp, w_in, 0, mc)
            self.load_out(sp, w_out, 0, mc)


def run_experts(nc, ctx, rounds, w_in, b_in, w_out, ident, x_sb, out_dram, r, inputs):
    u = f"ex{rounds[0]}_"
    sb = lambda n, s, d=F32: ctx.enter_context(nc.sbuf_tensor(u + n, s, d))
    sem = lambda n: ctx.enter_context(nc.semaphore(u + n))
    ST = COLS // P
    out_view = out_dram.rearrange("a (t p) e -> p (a t) e", p=P)
    STEPS = len(rounds) * NX
    expert_of = lambda step: step if STEPS == NX else step % NX
    b_cur = sb("b_cur", [P, M // P])
    b_hidden, wi, wo = inputs.b_hidden, inputs.wi, inputs.wo
    wi_hi = [sb(f"wi_hi{b}", [P, ET, MC], F32R) for b in range(2)]
    wi_lo = [sb(f"wi_lo{b}", [P, ET, MC], F32R) for b in range(2)]
    wo_hi = [sb(f"wo_hi{b}", [P, MT, E], F32R) for b in range(2)]
    wo_lo = [sb(f"wo_lo{b}", [P, MT, E], F32R) for b in range(2)]
    h = [sb(f"h{b}", [P, MT, COLS]) for b in range(2)]
    h_hi = [sb(f"h_hi{b}", [P, MT, P], F32R) for b in range(2)]
    h_lo = [sb(f"h_lo{b}", [P, MT, P], F32R) for b in range(2)]
    sel = sb("sel", [P, QT, COLS], F32R)
    sel_t = sb("sel_t", [P, ST, NQ], F32R)
    xg_hi = sb("xg_hi", [P, ET, COLS], F32R)
    xg_lo = sb("xg_lo", [P, ET, COLS], F32R)
    y_hi = sb("y_hi", [P, ST, E], F32R)
    y_lo = sb("y_lo", [P, ST, E], F32R)
    hp = [ctx.enter_context(nc.psum_tensor(f"{u}hp{b}", [P, MT, COLS], F32)) for b in range(2)]
    yp = ctx.enter_context(nc.psum_tensor(u + "yp", [P, ST, E], F32))
    move = ctx.enter_context(nc.psum_tensor(u + "move", [P, 2, NQ], F32))
    bias_banks = [yp[:, t, :] for t in range(2)] + [hp[1][:, 2 * t:2 * t + 2, :].rearrange("p a n -> p (a n)") for t in range(2)]
    move_g = move[:, :, :].rearrange("p a (b n) -> p (a b) n", n=COLS)
    b_ready, biased = map(sem, ("b_ready", "biased"))
    biases, wi_loaded, wo_loaded = inputs.biases, inputs.wi_loaded, inputs.wo_loaded
    wi_hi_ready, wi_lo_ready, wo_hi_ready, wo_lo_ready = map(sem, ("wi_hi_ready", "wi_lo_ready", "wo_hi_ready", "wo_lo_ready"))
    h_done, h_ready, h_hi_ready, h_lo_ready, y_done, y_hi_ready, y_lo_ready = map(sem, (
        "h_done", "h_ready", "h_hi_ready", "h_lo_ready", "y_done", "y_hi_ready", "y_lo_ready"))
    sel_ready, sel_turned, sel_t_ready, gathered, xg_ready, scattered, x_stands = map(sem, (
        "sel_ready", "sel_turned", "sel_t_ready", "gathered", "xg_ready", "scattered", "x_stands"))

    def guarded(eng, program):
        if rounds[0] == 0:
            program()
        else:
            flag = eng.value_load(r.long[:, :], min_val=0, max_val=1)
            with eng.If(flag > 0):
                program()

    with nc.Block() as block:
        @block.sync
        def _(sp):
            def expert(e, last):
                for mc in range(NMC):
                    n = NMC * e + mc
                    ahead = lambda steps: (expert_of(e + (mc + steps) // NMC), (mc + steps) % NMC)
                    if not (last and mc + 2 >= NMC):
                        sp.wait_ge(wi_lo_ready, n + 1)
                        inputs.load_in(sp, w_in, *ahead(2))
                    if not (last and mc + 1 >= NMC) and not (isinstance(n, int) and n == 0):
                        sp.wait_ge(y_done, n)
                        inputs.load_out(sp, w_out, *ahead(1))

            def program():
                if rounds[0] > 0:
                    inputs.load_first(sp, w_in, b_in, w_out)
                rolled(sp, STEPS, expert)
                for t in range(QT):
                    sp.wait_ge(x_stands, QT * STEPS + t + 1)
                    sp.dma_start(out_view[:, t, :], x_sb[:, t, :]).then_inc(r.stored, 16)
                if rounds[0] > 0:
                    sp.wait_ge(r.stored, 2 * 16 * QT)

            if rounds[0] > 0:
                sp.wait_ge(r.stored, 16 * QT)
            guarded(sp, program)

        @block.tensor
        def _(pe):
            def hidden(e, mc):
                n, b = NMC * e + mc, mc % 2
                pe.wait_ge(wi_lo_ready, n + 1)
                if mc == 0:
                    pe.wait_ge(xg_ready, 2 * (e + 1))
                if rounds[0] == 0 and isinstance(n, int) and n == 1:
                    pe.wait_ge(x_stands, QT)
                wait_reuse(pe, h_ready, MT * (n - 1))
                for t in range(MT):
                    for a, (lhs, rhs) in enumerate(((wi_hi, xg_hi), (wi_lo, xg_hi), (wi_hi, xg_lo))):
                        for d in range(ET):
                            last = nc.tensor.matmul(hp[b][:, t, :], lhs[b][:, d, t * P:(t + 1) * P], rhs[:, d, :],
                                                    start=(a == 0 and d == 0), stop=(a == 2 and d == ET - 1))
                    if t % 2 == 1:
                        last.then_inc(h_done, 1)

            def output(e, mc):
                n, b = NMC * e + mc, mc % 2
                pe.wait_ge(wo_lo_ready, n + 1)
                pe.wait_ge(h_lo_ready, MT * (n + 1))
                if mc == 0:
                    wait_reuse(pe, y_lo_ready, e)
                products = ((h_hi, wo_hi), (h_lo, wo_hi), (h_hi, wo_lo))
                for m in range(MT):
                    for a, (lhs, rhs) in enumerate(products):
                        nc.tensor.matmul(yp[:, 0, :], lhs[b][:, m, :], rhs[b][:, m, :],
                                         start=(mc == 0 and m == 0 and a == 0),
                                         stop=(mc == NMC - 1 and m == MT - 1 and a == 2))
                for m in range(0, MT, 2):
                    for i in range(2):
                        last = nc.tensor.matmul(yp[i * PAIRED:(i + 1) * PAIRED, 1, :],
                                                h[b][:, m + i, P + i * PAIRED:P + (i + 1) * PAIRED], wo[b][:, m + i, :],
                                                start=(mc == 0 and m == 0), stop=(mc == NMC - 1 and m == MT - 2))
                last.then_inc(y_done, 1)

            def gather(e, part):
                if part == 0:
                    pe.wait_ge(sel_ready, QT * (e + 1))
                    wait_reuse(pe, sel_t_ready, e)
                else:
                    pe.wait_ge(xg_ready, 2 * e + 1)
                for d in range(ET):
                    for t in range(QT):
                        last = nc.tensor.matmul(move_g[:, d, :], (r.x_hi, r.x_lo)[part][:, t, d * P:(d + 1) * P],
                                                sel[:, t, :], start=(t == 0), stop=(t == QT - 1))
                last.then_inc(gathered, 1)

            def turn_sel(e):
                pe.wait_ge(x_stands, QT * (e + 1))
                for s in range(ST):
                    for t in range(QT):
                        last = nc.tensor.transpose(move[:, s, t * P:(t + 1) * P], sel[:, t, s * P:(s + 1) * P].bitcast(F32),
                                                   ident[:, :])
                last.then_inc(sel_turned, 1)

            def scatter(e, tiles):
                if tiles[0] == 0:
                    pe.wait_ge(y_lo_ready, e + 1)
                    pe.wait_ge(sel_t_ready, e + 1)
                else:
                    pe.wait_ge(x_stands, QT * (e + 1) + tiles[0])
                for t in tiles:
                    for a, y in enumerate((y_hi, y_lo)):
                        for s in range(ST):
                            last = nc.tensor.matmul(move[:, t % 2, :], sel_t[:, s, t * P:(t + 1) * P], y[:, s, :],
                                                    start=(a == 0 and s == 0), stop=(a == 1 and s == ST - 1))
                last.then_inc(scattered, 1)

            def output_biases():
                for t in range(QT):
                    last = nc.tensor.matmul(bias_banks[t], r.combine_t[:, t * P:(t + 1) * P], r.bo[:, :],
                                            start=True, stop=True)
                last.then_inc(biased, 1)

            def expert(e, last):
                first = isinstance(e, int) and e == 0
                hidden(e, 0)
                if not first:
                    scatter(e - 1, (0, 1))
                hidden(e, 1)
                if not first:
                    scatter(e - 1, (2, 3))
                output(e, 0)
                turn_sel(e)
                hidden(e, 2)
                output(e, 1)
                hidden(e, 3)
                if not last:
                    gather(e + 1, 0)
                output(e, 2)
                if not last:
                    gather(e + 1, 1)
                output(e, 3)

            def program():
                gather(0, 0)
                if rounds[0] == 0:
                    output_biases()
                gather(0, 1)
                rolled(pe, STEPS, expert)
                scatter(STEPS - 1, (0, 1))
                scatter(STEPS - 1, (2, 3))

            guarded(pe, program)

        @block.scalar
        def _(act):
            def split_in(i, b):
                act.wait_ge(wi_loaded[b], 16 * (i + 1))
                nc.scalar.activation(wi_hi[b][:, :, :], wi[b][:, :, :], ACT.Copy).then_inc(wi_hi_ready, 1)

            def keep_gathered(e):
                for part, to in enumerate((xg_hi, xg_lo)):
                    act.wait_ge(gathered, 2 * e + part + 1)
                    nc.scalar.activation(to[:, :, :], move_g, ACT.Copy).then_inc(xg_ready, 1)

            def expert(e, last):
                for mc in range(NMC):
                    n, b = NMC * e + mc, mc % 2
                    if mc == 0:
                        act.wait_ge(b_ready, e + 1)
                    if not (last and mc == NMC - 1):
                        wait_reuse(act, h_done, 2 * n)
                        split_in(2 * e + (mc + 1) // 2, 1 - b)
                    wait_reuse(act, y_done, n - 1)
                    for t in range(MT):
                        act.wait_ge(h_done, 2 * n + t // 2 + 1)
                        nc.scalar.activation(h[b][:, t, :], hp[b][:, t, :], ACT.Gelu,
                                             bias=b_cur[:, mc * MT + t:mc * MT + t + 1]).then_inc(h_ready, 1)
                    act.wait_ge(wo_loaded[b], 16 * (2 * e + mc // 2 + 1))
                    nc.scalar.activation(wo_hi[b][:, :, :], wo[b][:, :, :], ACT.Copy).then_inc(wo_hi_ready, 1)
                    if mc == 1:
                        act.wait_ge(sel_turned, e + 1)
                        nc.scalar.activation(sel_t[:, :, :], move[:, :, :], ACT.Copy).then_inc(sel_t_ready, 1)
                if not last:
                    keep_gathered(e + 1)
                act.wait_ge(y_done, NMC * (e + 1))
                nc.scalar.activation(y_hi[:, :, :], yp[:, :, :], ACT.Copy).then_inc(y_hi_ready, 1)

            def program():
                split_in(0, 0)
                keep_gathered(0)
                rolled(act, STEPS, expert)

            guarded(act, program)

        @block.vector
        def _(dve):
            def split_in(n, b):
                dve.wait_ge(wi_hi_ready, n + 1)
                nc.vector.tensor_tensor(wi_lo[b][:, :, :], wi[b][:, :, :], wi_hi[b][:, :, :].bitcast(F32),
                                        ALU.subtract).then_inc(wi_lo_ready, 1)

            def select(e):
                x = bass.ds(expert_of(e), 1)
                if STEPS == NX:
                    numbers = r.numbers[:, 0:COLS]
                else:
                    numbers = r.numbers[:, bass.ds((rounds[0] + e // NX) * COLS, COLS)]
                for t in range(QT):
                    nc.vector.tensor_scalar(sel[:, t, :], numbers, r.rank[:, t, x], r.mask[:, t, x],
                                            ALU.is_equal, ALU.mult).then_inc(sel_ready, 1)

            def add(e, tiles):
                dve.wait_ge(x_stands, QT * (e + 1))
                dve.wait_ge(scattered, 2 * e + tiles[0] // 2 + 1)
                for t in tiles:
                    nc.vector.scalar_tensor_tensor(x_sb[:, t, :], move[:, t % 2, :], r.combine[:, t, bass.ds(expert_of(e), 1)],
                                                   x_sb[:, t, :], ALU.mult, ALU.add).then_inc(x_stands, 1)

            def expert(e, last):
                first = isinstance(e, int) and e == 0
                wait_reuse(dve, h_ready, NMC * MT * e)
                nc.vector.tensor_scalar(b_cur[:, :], b_hidden[:, bass.ds(expert_of(e), 1), :].rearrange("p a t -> p (a t)"), 1.0,
                                        None, ALU.mult).then_inc(b_ready, 1)
                for mc in range(NMC):
                    n, b = NMC * e + mc, mc % 2
                    if not (last and mc == NMC - 1):
                        split_in(n + 1, 1 - b)
                    wait_reuse(dve, y_done, n - 1)
                    for t in range(0, MT, 2):
                        two = slice(t, t + 2)
                        dve.wait_ge(h_ready, MT * n + t + 2)
                        nc.vector.tensor_copy(h_hi[b][:, two, :], h[b][:, two, 0:P]).then_inc(h_hi_ready, 1)
                        dve.wait_ge(h_hi_ready, 2 * n + t // 2 + 1)
                        nc.vector.tensor_tensor(h_lo[b][:, two, :], h[b][:, two, 0:P], h_hi[b][:, two, :].bitcast(F32),
                                                ALU.subtract).then_inc(h_lo_ready, 2)
                    dve.wait_ge(wo_hi_ready, n + 1)
                    nc.vector.tensor_tensor(wo_lo[b][:, :, :], wo[b][:, :, :], wo_hi[b][:, :, :].bitcast(F32),
                                            ALU.subtract).then_inc(wo_lo_ready, 1)
                    if mc < 2 and not first:
                        add(e - 1, (2 * mc, 2 * mc + 1))
                    if mc == 2 and not last:
                        dve.wait_ge(sel_turned, e + 1)
                        select(e + 1)
                dve.wait_ge(y_hi_ready, e + 1)
                nc.vector.tensor_tensor(y_lo[:, :, :], yp[:, :, :], y_hi[:, :, :].bitcast(F32),
                                        ALU.subtract).then_inc(y_lo_ready, 1)

            def program():
                select(0)
                dve.wait_ge(biases, 16)
                split_in(0, 0)
                if rounds[0] == 0:
                    dve.wait_ge(biased, 1)
                    for t in range(QT):
                        nc.vector.tensor_tensor(x_sb[:, t, :], x_sb[:, t, :], bias_banks[t], ALU.add).then_inc(x_stands, 1)
                else:
                    dve.wait_ge(r.stored, 16 * QT)
                    dve.sem_inc(x_stands, QT)
                rolled(dve, STEPS, expert)
                add(STEPS - 1, (0, 1))
                add(STEPS - 1, (2, 3))

            guarded(dve, program)


def feed_forward(nc, ctx, w_gate, w_in, b_in, w_out, b_out, ident, x_sb, out_dram, inputs):
    sb = lambda n, s, d=F32: ctx.enter_context(nc.sbuf_tensor(n, s, d))
    r = Routing()
    r.x_hi = sb("ff_x_hi", [P, QT, E], F32R)
    r.x_lo = sb("ff_x_lo", [P, QT, E], F32R)
    r.numbers = sb("ff_numbers", [P, ROUNDS * COLS])
    r.mask = sb("ff_mask", [P, QT, NX])
    r.rank = sb("ff_rank", [P, QT, NX])
    r.combine = sb("ff_combine", [P, QT, NX])
    r.combine_t = sb("ff_combine_t", [NX, NQ])
    r.bo = sb("ff_bo", [NX, E])
    r.long = sb("ff_long", [1, 1], I32)
    r.stored = ctx.enter_context(nc.semaphore("ff_stored"))
    with ExitStack() as s:
        route(nc, s, w_gate, b_out, ident, x_sb, r)
    for rounds in (range(1), range(1, ROUNDS)):
        with ExitStack() as s:
            if rounds[0] > 0:
                inputs.name_semaphores(nc, s, rounds[0])
            run_experts(nc, s, rounds, w_in, b_in, w_out, ident, x_sb, out_dram, r, inputs)


def perceiver_layer(nc, x, ctx_t, xw_in, xb_in, xb_cols, xw_out, xb_out, sw_in, sb_cols, sw_out, sb_out, w_gate,
                    w_in, b_in, w_out, b_out, out):
    k_hi_dram = nc.dram_tensor("k_hi_scratch", [E, NK], F32, kind="Internal").ap()
    k_lo_dram = nc.dram_tensor("k_lo_scratch", [E, NK], F32, kind="Internal").ap()
    v_dram = nc.dram_tensor("v_scratch", [NK, E], F32, kind="Internal").ap()
    width_first = lambda w: w.rearrange("(t p) f -> p t f", p=P)
    with ExitStack() as whole:
        keep = lambda n, s, d=F32, ctx=whole: ctx.enter_context(nc.sbuf_tensor(n, s, d))
        x_sb = keep("x_sb", [P, QT, E])
        ident = keep("ident", [P, P])
        a = Ahead()
        sem = lambda n: whole.enter_context(nc.semaphore(n))
        a.c_hi_ready, a.c_lo_ready = map(sem, ("sc_c_hi_ready", "sc_c_lo_ready"))
        a.c_loaded = [sem(f"sc_c_loaded{b}") for b in range(2)]
        a.biases, a.stacked, a.ones_set, a.late_loaded = map(sem, ("sc_biases", "pq_stacked", "at_ones_set", "late_loaded"))
        a.loaded = [sem("at_loaded0")]
        late_weights = whole.enter_context(ExitStack())
        with ExitStack() as cross:
            q_stack = keep("q_stack", [QROWS, H * NQ], F32R, cross)
            head_rows = keep("head_rows", [P, HG], F32, cross)
            bounded = keep("bounded", [1, 1], I32, cross)
            a.k = [keep("at_k0", [QROWS, HG, CH], F32R, cross)]
            a.v = [keep("at_v0", [P, KT, P], F32, cross)]
            with ExitStack() as stream:
                a.q_hi, a.q_lo = (keep(f"pq_q_{n}", [P, NG, NQ], F32R, stream) for n in ("hi", "lo"))
                a.w_hi, a.w_lo = (keep(f"sc_w_{n}", [P, ET, 2 * E], F32R, stream) for n in ("hi", "lo"))
                a.bk = keep("sc_bk", [P, NG], F32, stream)
                a.bv = keep("sc_bv", [P, E], F32, stream)
                a.c_hi, a.c_lo = ([keep(f"sc_c_{n}0", [P, ET, CH], F32R, stream)] for n in ("hi", "lo"))
                a.c = [keep(f"sc_c{b}", [P, ET, CH], F32, stream) for b in range(2)]
                with ExitStack() as s:
                    project_queries(nc, s, x, ctx_t, xw_in, xb_in, xb_cols, x_sb, ident, q_stack, head_rows, a)
                with ExitStack() as s:
                    stream_context(nc, s, ctx_t, k_hi_dram, k_lo_dram, v_dram, q_stack, head_rows, bounded, a)
            with ExitStack() as s:
                find_maxima(nc, s, k_hi_dram, k_lo_dram, ident, q_stack, bounded)
            at_right = lambda n, s: late_weights.enter_context(nc.sbuf_tensor(n, s, F32, side="right"))
            xwo, swv, swo = (at_right(n, [P, ET, E]) for n in ("xwo", "swv", "swo"))
            xbo, sbo = (at_right(n, [P, E]) for n in ("xbo", "sbo"))
            sbv = at_right("sbv", [P, ET])
            late = [t[:] for t in (xwo, xbo, swv, sbv, swo, sbo)]
            late_dram = [width_first(xw_out), xb_out.partition_broadcast(P), width_first(sw_in[:, 2, :]),
                         sb_cols[:, 2 * ET:3 * ET], width_first(sw_out), sb_out.partition_broadcast(P)]
            o_acc = keep("o_acc", [P, NG, NQ], F32, cross)
            total_acc = keep("total_acc", [P, NG, NQ], F32, cross)
            p_sum = keep("p_sum", [P, H * NQ], F32, cross)
            with ExitStack() as s:
                attend(nc, s, k_hi_dram, k_lo_dram, v_dram, q_stack, o_acc, p_sum, total_acc, a, late, late_dram)
            with ExitStack() as s:
                cross_output(nc, s, xwo, xbo, o_acc, p_sum, total_acc, x_sb)
        inputs = ExpertInputs(nc, whole)
        inputs.name_semaphores(nc, whole, 0)
        with ExitStack() as s:
            self_attention(nc, s, swv, sbv, swo, sbo, ident, x_sb,
                           lambda sp: inputs.load_first(sp, w_in, b_in, w_out))
        late_weights.close()
        with ExitStack() as s:
            feed_forward(nc, s, w_gate, w_in, b_in, w_out, b_out, ident, x_sb, out, inputs)


def kernel(**inputs):
    import numpy as np
    import concourse.bacc as bacc
    from concourse.bass_utils import run_bass_kernel_spmd

    a = {k: np.asarray(v) for k, v in inputs.items()}
    arrays = {
        "x": a["x"],
        "ctx_t": a["ctx_1024"][0].T,
        "xw_in": a["L0_xattn_in_proj_weight"].T,
        "xb_in": a["L0_xattn_in_proj_bias"],
        "xb_cols": a["L0_xattn_in_proj_bias"].reshape(3 * ET, P).T,
        "xw_out": a["L0_xattn_out_proj_weight"].T,
        "xb_out": a["L0_xattn_out_proj_bias"],
        "sw_in": a["L0_attn_in_proj_weight"].reshape(H, 3, D, E).transpose(3, 1, 0, 2).reshape(E, 3, E),
        "sb_cols": a["L0_attn_in_proj_bias"].reshape(H, 3, D).transpose(1, 0, 2).reshape(3 * ET, P).T,
        "sw_out": a["L0_attn_out_proj_weight"].T,
        "sb_out": a["L0_attn_out_proj_bias"],
        "w_gate": a["L0_ffn_W_gate"],
        "w_in": a["L0_ffn_W_in"].reshape(NX * E, M),
        "b_in": a["L0_ffn_b_in"].reshape(NX, M // P, P).transpose(2, 0, 1),
        "w_out": a["L0_ffn_W_out"].reshape(NX * M, E),
        "b_out": a["L0_ffn_b_out"],
    }
    arrays = {k: np.ascontiguousarray(v) for k, v in arrays.items()}
    nc = bacc.Bacc("TRN2", target_bir_lowering=False, num_devices=1)
    args = [nc.dram_tensor(k, v.shape, mybir.dt.from_np(v.dtype), kind="ExternalInput").ap() for k, v in arrays.items()]
    out = nc.dram_tensor("out", (1, NQ, E), F32, kind="ExternalOutput").ap()
    perceiver_layer(nc, *args, out)
    got = run_bass_kernel_spmd(nc, [arrays], core_ids=[0])
    return got.results[0]["out"]
```
